# Optimizing a Trainium2 kernel written in Bass

```python
import numpy as np
import jax
import jax.numpy as jnp

def _softmax(x, axis=-1):
    return jax.nn.softmax(x, axis=axis)

def _gelu(x):
    return jax.nn.gelu(x, approximate=True)

def _silu(x):
    return jax.nn.silu(x)

def _sigmoid(x):
    return jax.nn.sigmoid(x)

def _layernorm(x, axis=-1, eps=1e-05):
    m = jnp.mean(x, axis=axis, keepdims=True)
    v = jnp.var(x, axis=axis, keepdims=True)
    return (x - m) / jnp.sqrt(v + eps)

def _scatter_add(tgt, idx, src, axis=0):
    return tgt.at[idx].add(src)

def _segment_sum(src, seg, n):
    return jax.ops.segment_sum(src, seg, n)
kernel_name = 'mk_hybrid_d1_jaxref_r8_93753c'

def setup_inputs(seed: int=0):
    np.random.seed(seed)
    _w = jnp.asarray

    def _L0_attn_a_setup():
        import jax, jax.numpy as jnp
        import numpy as np
        CHUNK = 64
        NORM_EPS = 1e-05
        DENOM_EPS = 1.0
        B, S, HID, H = (4, 512, 128, 8)
        D = HID // H

        def rmsnorm(x, w, eps=NORM_EPS):
            var = jnp.mean(x * x, axis=-1, keepdims=True)
            return x * jax.lax.rsqrt(var + eps) * w

        def chunked_linear_attn(q, k, v):
            b, s, h, d = q.shape
            n = s // CHUNK

            def to_chunks(x):
                return x.reshape(b, n, CHUNK, h, d).transpose(1, 0, 3, 2, 4)
            qc, kc, vc = (to_chunks(q), to_chunks(k), to_chunks(v))
            mask = jnp.tril(jnp.ones((CHUNK, CHUNK), dtype=q.dtype))

            def step(state, inp):
                qq, kk, vv = inp
                inter = jnp.einsum('bhcd,bhde->bhce', qq, state)
                scores = jnp.einsum('bhcd,bhed->bhce', qq, kk) * mask
                intra = jnp.einsum('bhce,bhed->bhcd', scores, vv)
                state = state + jnp.einsum('bhcd,bhce->bhde', kk, vv)
                return (state, inter + intra)
            init = jnp.zeros((b, h, d, d), dtype=q.dtype)
            _, o = jax.lax.scan(step, init, (qc, kc, vc))
            return o.transpose(1, 0, 3, 2, 4).reshape(b, s, h, d)
        key = jax.random.key(seed)
        k0, k1, k2, k3, k4 = jax.random.split(key, 5)
        hidden_states = jax.random.normal(k0, (B, S, HID), dtype=jnp.float32)
        Wq = jax.random.normal(k1, (HID, HID), dtype=jnp.float32) * 0.02
        Wk = jax.random.normal(k2, (HID, HID), dtype=jnp.float32) * 0.02
        Wv = jax.random.normal(k3, (HID, HID), dtype=jnp.float32) * 0.02
        Wo = jax.random.normal(k4, (HID, HID), dtype=jnp.float32) * 0.02
        norm_w = jnp.ones((D,), dtype=jnp.float32)
        return {'hidden_states': hidden_states, 'Wq': Wq, 'Wk': Wk, 'Wv': Wv, 'Wo': Wo, 'norm_w': norm_w}
    _L0_attn_a_in = _L0_attn_a_setup()

    def _L0_attn_b_setup():
        import jax, jax.numpy as jnp
        import numpy as np
        SCALE_BASE = 512.0
        GAMMA = 0.96875

        def xpos(x, downscale=False):
            B, L, d = x.shape
            half = d // 2
            scale_vec = (jnp.arange(0, d, 2, dtype=jnp.float32) + 0.4 * d) / (1.4 * d)
            pos = jnp.arange(L, dtype=jnp.float32)
            scale = scale_vec[None, :] ** (pos[:, None] / SCALE_BASE)
            if downscale:
                scale = 1.0 / scale
            inv_freq = 1.0 / 10000.0 ** (jnp.arange(half, dtype=jnp.float32) / half)
            sinusoid = pos[:, None] * inv_freq[None, :]
            sin_s = jnp.repeat(jnp.sin(sinusoid) * scale, 2, axis=-1)
            cos_s = jnp.repeat(jnp.cos(sinusoid) * scale, 2, axis=-1)
            x1, x2 = (x[..., ::2], x[..., 1::2])
            rot = jnp.stack((-x2, x1), axis=-1).reshape(x.shape)
            return x * cos_s + rot * sin_s

        def decay_mask(L, gamma):
            n = jnp.arange(L)[:, None]
            m = jnp.arange(L)[None, :]
            diff = n - m
            expo = jnp.where(diff >= 0, diff, 0).astype(jnp.float32)
            return jnp.where(diff >= 0, gamma ** expo, 0.0)
        key = jax.random.key(seed)
        kx, kq, kk, kv = jax.random.split(key, 4)
        B, L, H = (4, 256, 128)
        hs = 128
        X = jax.random.normal(kx, (B, L, H), dtype=jnp.float32)
        W_Q = jax.random.normal(kq, (H, hs), dtype=jnp.float32) / H
        W_K = jax.random.normal(kk, (H, hs), dtype=jnp.float32) / H
        W_V = jax.random.normal(kv, (H, hs), dtype=jnp.float32) / H
        return {'X': X, 'W_Q': W_Q, 'W_K': W_K, 'W_V': W_V}
    _L0_attn_b_in = _L0_attn_b_setup()

    def _L0_ffn_setup():
        import jax, jax.numpy as jnp
        import numpy as np
        DIM = 128
        DEPTH = 6
        HEADS = 16
        DIM_HEAD = 64
        WINDOW = 32
        INNER = HEADS * DIM_HEAD
        DIM_INNER = int(DIM * 4 * 2 / 3)
        QK_SCALE = 8.0

        def shift_tokens(t):
            a, s = jnp.split(t, 2, -1)
            s = jnp.pad(s, ((0, 0), (1, 0), (0, 0)))[:, :-1]
            return jnp.concatenate([a, s], -1)

        def l2norm(t):
            return t / jnp.maximum(jnp.linalg.norm(t, axis=-1, keepdims=True), 1e-12)

        def rotate_half(x):
            x1, x2 = jnp.split(x, 2, -1)
            return jnp.concatenate([-x2, x1], -1)

        def rotary_tables(n):
            half = jnp.arange(0, DIM_HEAD, 2, dtype=jnp.float32)
            inv_freq = 1.0 / 10000.0 ** (half / DIM_HEAD)
            t = jnp.arange(n, dtype=jnp.float32)
            freqs = t[:, None] * inv_freq[None, :]
            freqs = jnp.concatenate([freqs, freqs], -1)
            base_scale = (half + 0.4 * DIM_HEAD) / (1.4 * DIM_HEAD)
            power = (t - n // 2) / (WINDOW // 2)
            scale = base_scale[None, :] ** power[:, None]
            scale = jnp.concatenate([scale, scale], -1)
            return (freqs, scale)

        def local_attention(q, k, v):
            b, h, n, d = q.shape
            w = WINDOW
            nw = n // w
            bq = q.reshape(b, h, nw, w, d)
            bk = k.reshape(b, h, nw, w, d)
            bv = v.reshape(b, h, nw, w, d)

            def look(t):
                p = jnp.pad(t, ((0, 0), (0, 0), (1, 0), (0, 0), (0, 0)))
                return jnp.concatenate([p[:, :, :nw], p[:, :, 1:]], axis=3)
            bk2, bv2 = (look(bk), look(bv))
            seq = jnp.arange(n).reshape(nw, w)
            seq_p = jnp.pad(seq, ((1, 0), (0, 0)), constant_values=-1)
            jt = jnp.concatenate([seq_p[:nw], seq_p[1:]], axis=1)
            it = seq[:, :, None]
            jb = jt[:, None, :]
            mask = (it < jb) | (it > jb + w) | (jb == -1)
            sim = jnp.einsum('bhwie,bhwje->bhwij', bq, bk2) * QK_SCALE
            sim = jnp.where(mask, -jnp.finfo(sim.dtype).max, sim)
            attn = jax.nn.softmax(sim, -1)
            out = jnp.einsum('bhwij,bhwje->bhwie', attn, bv2)
            return out.reshape(b, h, n, d)

        def attn_layer(x, Wqkv, qs, ksc, Wo):
            b, n, _ = x.shape
            qkv = x @ Wqkv
            q, k, v = jnp.split(qkv, 3, -1)
            sh = lambda t: t.reshape(b, n, HEADS, DIM_HEAD).transpose(0, 2, 1, 3)
            q, k, v = (sh(q), sh(k), sh(v))
            q = l2norm(q) * qs
            k = l2norm(k) * ksc
            freqs, scale = rotary_tables(n)
            cos, sin = (jnp.cos(freqs), jnp.sin(freqs))
            q = q * cos * scale + rotate_half(q) * sin * scale
            inv = 1.0 / scale
            k = k * cos * inv + rotate_half(k) * sin * inv
            out = local_attention(q, k, v)
            out = out.transpose(0, 2, 1, 3).reshape(b, n, INNER)
            return out @ Wo

        def ffn_layer(x, g, bln, W1, b1, W2, b2):
            mu = x.mean(-1, keepdims=True)
            var = ((x - mu) ** 2).mean(-1, keepdims=True)
            xn = (x - mu) / jnp.sqrt(var + 1e-05) * g + bln
            hg = xn @ W1 + b1
            a, gate = jnp.split(hg, 2, -1)
            return a * jax.nn.gelu(gate, approximate=False) @ W2 + b2
        key = jax.random.key(seed)
        ks = jax.random.split(key, 8)
        B, N = (2, 256)
        init = lambda k, shape: jax.random.normal(k, shape, jnp.float32) * 0.02
        return {'x': jax.random.normal(ks[0], (B, N, DIM), jnp.float32), 'Wqkv': init(ks[1], (DEPTH, DIM, 3 * INNER)), 'q_scale': jnp.ones((DEPTH, DIM_HEAD), jnp.float32), 'k_scale': jnp.ones((DEPTH, DIM_HEAD), jnp.float32), 'Wo': init(ks[2], (DEPTH, INNER, DIM)), 'ln_g': jnp.ones((DEPTH, DIM), jnp.float32), 'ln_b': jnp.zeros((DEPTH, DIM), jnp.float32), 'W1': init(ks[3], (DEPTH, DIM, 2 * DIM_INNER)), 'b1': jnp.zeros((DEPTH, 2 * DIM_INNER), jnp.float32), 'W2': init(ks[4], (DEPTH, DIM_INNER, DIM)), 'b2': jnp.zeros((DEPTH, DIM), jnp.float32)}
    _L0_ffn_in = _L0_ffn_setup()
    _d = {'L0_attn_a_hidden_states': _L0_attn_a_in['hidden_states'], 'L0_attn_a_Wq': _L0_attn_a_in['Wq'], 'L0_attn_a_Wk': _L0_attn_a_in['Wk'], 'L0_attn_a_Wv': _L0_attn_a_in['Wv'], 'L0_attn_a_Wo': _L0_attn_a_in['Wo'], 'L0_attn_a_norm_w': _L0_attn_a_in['norm_w'], 'L0_attn_b_W_Q': _L0_attn_b_in['W_Q'], 'L0_attn_b_W_K': _L0_attn_b_in['W_K'], 'L0_attn_b_W_V': _L0_attn_b_in['W_V'], 'L0_ffn_Wqkv': _L0_ffn_in['Wqkv'], 'L0_ffn_q_scale': _L0_ffn_in['q_scale'], 'L0_ffn_k_scale': _L0_ffn_in['k_scale'], 'L0_ffn_Wo': _L0_ffn_in['Wo'], 'L0_ffn_ln_g': _L0_ffn_in['ln_g'], 'L0_ffn_ln_b': _L0_ffn_in['ln_b'], 'L0_ffn_W1': _L0_ffn_in['W1'], 'L0_ffn_b1': _L0_ffn_in['b1'], 'L0_ffn_W2': _L0_ffn_in['W2'], 'L0_ffn_b2': _L0_ffn_in['b2']}
    _x0 = _d['L0_attn_a_hidden_states']
    _d['L0_attn_a_hidden_states'] = jax.random.normal(jax.random.fold_in(jax.random.key(seed), 1), (4, 512, 128), dtype=_x0.dtype)
    del _x0
    return _d

def reference(L0_attn_a_hidden_states, L0_attn_a_Wq, L0_attn_a_Wk, L0_attn_a_Wv, L0_attn_a_Wo, L0_attn_a_norm_w, L0_attn_b_W_Q, L0_attn_b_W_K, L0_attn_b_W_V, L0_ffn_Wqkv, L0_ffn_q_scale, L0_ffn_k_scale, L0_ffn_Wo, L0_ffn_ln_g, L0_ffn_ln_b, L0_ffn_W1, L0_ffn_b1, L0_ffn_W2, L0_ffn_b2):

    def _L0_attn_a_ref(hidden_states, Wq, Wk, Wv, Wo, norm_w):
        import jax, jax.numpy as jnp
        import numpy as np
        CHUNK = 64
        NORM_EPS = 1e-05
        DENOM_EPS = 1.0
        B, S, HID, H = (4, 512, 128, 8)
        D = HID // H

        def rmsnorm(x, w, eps=NORM_EPS):
            var = jnp.mean(x * x, axis=-1, keepdims=True)
            return x * jax.lax.rsqrt(var + eps) * w

        def chunked_linear_attn(q, k, v):
            b, s, h, d = q.shape
            n = s // CHUNK

            def to_chunks(x):
                return x.reshape(b, n, CHUNK, h, d).transpose(1, 0, 3, 2, 4)
            qc, kc, vc = (to_chunks(q), to_chunks(k), to_chunks(v))
            mask = jnp.tril(jnp.ones((CHUNK, CHUNK), dtype=q.dtype))

            def step(state, inp):
                qq, kk, vv = inp
                inter = jnp.einsum('bhcd,bhde->bhce', qq, state)
                scores = jnp.einsum('bhcd,bhed->bhce', qq, kk) * mask
                intra = jnp.einsum('bhce,bhed->bhcd', scores, vv)
                state = state + jnp.einsum('bhcd,bhce->bhde', kk, vv)
                return (state, inter + intra)
            init = jnp.zeros((b, h, d, d), dtype=q.dtype)
            _, o = jax.lax.scan(step, init, (qc, kc, vc))
            return o.transpose(1, 0, 3, 2, 4).reshape(b, s, h, d)
        b, s, _ = hidden_states.shape
        q = jnp.einsum('bsd,ed->bse', hidden_states, Wq).reshape(b, s, H, D)
        k = jnp.einsum('bsd,ed->bse', hidden_states, Wk).reshape(b, s, H, D)
        v = jnp.einsum('bsd,ed->bse', hidden_states, Wv).reshape(b, s, H, D)
        o = chunked_linear_attn(q, k, v)
        z = jnp.cumsum(k, axis=1)
        denom = jnp.maximum(jnp.abs(jnp.sum(q * z, axis=-1)), DENOM_EPS)[..., None]
        o = o / denom
        o = rmsnorm(o, norm_w)
        o = o.reshape(b, s, H * D)
        return jnp.einsum('bse,de->bsd', o, Wo)

    def _L0_attn_b_ref(X, W_Q, W_K, W_V):
        import jax, jax.numpy as jnp
        import numpy as np
        SCALE_BASE = 512.0
        GAMMA = 0.96875

        def xpos(x, downscale=False):
            B, L, d = x.shape
            half = d // 2
            scale_vec = (jnp.arange(0, d, 2, dtype=jnp.float32) + 0.4 * d) / (1.4 * d)
            pos = jnp.arange(L, dtype=jnp.float32)
            scale = scale_vec[None, :] ** (pos[:, None] / SCALE_BASE)
            if downscale:
                scale = 1.0 / scale
            inv_freq = 1.0 / 10000.0 ** (jnp.arange(half, dtype=jnp.float32) / half)
            sinusoid = pos[:, None] * inv_freq[None, :]
            sin_s = jnp.repeat(jnp.sin(sinusoid) * scale, 2, axis=-1)
            cos_s = jnp.repeat(jnp.cos(sinusoid) * scale, 2, axis=-1)
            x1, x2 = (x[..., ::2], x[..., 1::2])
            rot = jnp.stack((-x2, x1), axis=-1).reshape(x.shape)
            return x * cos_s + rot * sin_s

        def decay_mask(L, gamma):
            n = jnp.arange(L)[:, None]
            m = jnp.arange(L)[None, :]
            diff = n - m
            expo = jnp.where(diff >= 0, diff, 0).astype(jnp.float32)
            return jnp.where(diff >= 0, gamma ** expo, 0.0)
        L = X.shape[1]
        Q = xpos(X @ W_Q)
        K = xpos(X @ W_K, downscale=True)
        V = X @ W_V
        D = decay_mask(L, GAMMA)
        ret = jnp.einsum('bnd,bmd->bnm', Q, K) * D[None]
        return ret @ V

    def _L0_ffn_ref(x, Wqkv, q_scale, k_scale, Wo, ln_g, ln_b, W1, b1, W2, b2):
        import jax, jax.numpy as jnp
        import numpy as np
        DIM = 128
        DEPTH = 6
        HEADS = 16
        DIM_HEAD = 64
        WINDOW = 32
        INNER = HEADS * DIM_HEAD
        DIM_INNER = int(DIM * 4 * 2 / 3)
        QK_SCALE = 8.0

        def shift_tokens(t):
            a, s = jnp.split(t, 2, -1)
            s = jnp.pad(s, ((0, 0), (1, 0), (0, 0)))[:, :-1]
            return jnp.concatenate([a, s], -1)

        def l2norm(t):
            return t / jnp.maximum(jnp.linalg.norm(t, axis=-1, keepdims=True), 1e-12)

        def rotate_half(x):
            x1, x2 = jnp.split(x, 2, -1)
            return jnp.concatenate([-x2, x1], -1)

        def rotary_tables(n):
            half = jnp.arange(0, DIM_HEAD, 2, dtype=jnp.float32)
            inv_freq = 1.0 / 10000.0 ** (half / DIM_HEAD)
            t = jnp.arange(n, dtype=jnp.float32)
            freqs = t[:, None] * inv_freq[None, :]
            freqs = jnp.concatenate([freqs, freqs], -1)
            base_scale = (half + 0.4 * DIM_HEAD) / (1.4 * DIM_HEAD)
            power = (t - n // 2) / (WINDOW // 2)
            scale = base_scale[None, :] ** power[:, None]
            scale = jnp.concatenate([scale, scale], -1)
            return (freqs, scale)

        def local_attention(q, k, v):
            b, h, n, d = q.shape
            w = WINDOW
            nw = n // w
            bq = q.reshape(b, h, nw, w, d)
            bk = k.reshape(b, h, nw, w, d)
            bv = v.reshape(b, h, nw, w, d)

            def look(t):
                p = jnp.pad(t, ((0, 0), (0, 0), (1, 0), (0, 0), (0, 0)))
                return jnp.concatenate([p[:, :, :nw], p[:, :, 1:]], axis=3)
            bk2, bv2 = (look(bk), look(bv))
            seq = jnp.arange(n).reshape(nw, w)
            seq_p = jnp.pad(seq, ((1, 0), (0, 0)), constant_values=-1)
            jt = jnp.concatenate([seq_p[:nw], seq_p[1:]], axis=1)
            it = seq[:, :, None]
            jb = jt[:, None, :]
            mask = (it < jb) | (it > jb + w) | (jb == -1)
            sim = jnp.einsum('bhwie,bhwje->bhwij', bq, bk2) * QK_SCALE
            sim = jnp.where(mask, -jnp.finfo(sim.dtype).max, sim)
            attn = jax.nn.softmax(sim, -1)
            out = jnp.einsum('bhwij,bhwje->bhwie', attn, bv2)
            return out.reshape(b, h, n, d)

        def attn_layer(x, Wqkv, qs, ksc, Wo):
            b, n, _ = x.shape
            qkv = x @ Wqkv
            q, k, v = jnp.split(qkv, 3, -1)
            sh = lambda t: t.reshape(b, n, HEADS, DIM_HEAD).transpose(0, 2, 1, 3)
            q, k, v = (sh(q), sh(k), sh(v))
            q = l2norm(q) * qs
            k = l2norm(k) * ksc
            freqs, scale = rotary_tables(n)
            cos, sin = (jnp.cos(freqs), jnp.sin(freqs))
            q = q * cos * scale + rotate_half(q) * sin * scale
            inv = 1.0 / scale
            k = k * cos * inv + rotate_half(k) * sin * inv
            out = local_attention(q, k, v)
            out = out.transpose(0, 2, 1, 3).reshape(b, n, INNER)
            return out @ Wo

        def ffn_layer(x, g, bln, W1, b1, W2, b2):
            mu = x.mean(-1, keepdims=True)
            var = ((x - mu) ** 2).mean(-1, keepdims=True)
            xn = (x - mu) / jnp.sqrt(var + 1e-05) * g + bln
            hg = xn @ W1 + b1
            a, gate = jnp.split(hg, 2, -1)
            return a * jax.nn.gelu(gate, approximate=False) @ W2 + b2
        for i in range(DEPTH):
            x = attn_layer(shift_tokens(x), Wqkv[i], q_scale[i], k_scale[i], Wo[i]) + x
            x = ffn_layer(shift_tokens(x), ln_g[i], ln_b[i], W1[i], b1[i], W2[i], b2[i]) + x
        return x
    x = L0_attn_a_hidden_states
    x = x + _L0_attn_a_ref(_layernorm(x, axis=-1), L0_attn_a_Wq, L0_attn_a_Wk, L0_attn_a_Wv, L0_attn_a_Wo, L0_attn_a_norm_w)
    x = x + _L0_ffn_ref(_layernorm(x, axis=-1), L0_ffn_Wqkv, L0_ffn_q_scale, L0_ffn_k_scale, L0_ffn_Wo, L0_ffn_ln_g, L0_ffn_ln_b, L0_ffn_W1, L0_ffn_b1, L0_ffn_W2, L0_ffn_b2)
    x = x + _L0_attn_b_ref(_layernorm(x, axis=-1), L0_attn_b_W_Q, L0_attn_b_W_K, L0_attn_b_W_V)
    x = x + _L0_ffn_ref(_layernorm(x, axis=-1), L0_ffn_Wqkv, L0_ffn_q_scale, L0_ffn_k_scale, L0_ffn_Wo, L0_ffn_ln_g, L0_ffn_ln_b, L0_ffn_W1, L0_ffn_b1, L0_ffn_W2, L0_ffn_b2)
    return x

_drawn_inputs = setup_inputs


def setup_inputs(seed=0):
    import zlib

    import numpy as np

    out = dict(_drawn_inputs(seed))
    spreads = {'L0_attn_a_norm_w': (1.0, 0.2),
     'L0_ffn_q_scale': (1.0, 0.6),
     'L0_ffn_k_scale': (1.0, 0.6),
     'L0_ffn_ln_g': (1.0, 0.6),
     'L0_ffn_ln_b': (0.0, 0.8),
     'L0_ffn_b1': (0.0, 0.585),
     'L0_ffn_b2': (0.0, 0.1)}
    factors = {'L0_attn_b_W_Q': 3.349, 'L0_attn_b_W_K': 3.316, 'L0_attn_b_W_V': 3.299}
    for name, (base, spread) in spreads.items():
        noise = np.random.default_rng([zlib.crc32(name.encode()), seed]).standard_normal(out[name].shape)
        drawn = base * np.exp(spread * noise) if base else spread * noise
        out[name] = jnp.asarray(drawn.astype(out[name].dtype))
    for name, factor in factors.items():
        out[name] = (out[name] * factor).astype(out[name].dtype)
    return out
```

```python
import numpy as np


def build_hybrid(nc, x_in, tabs, wa, wb, wf, out):
    import math
    from contextlib import ExitStack

    import concourse.bass as bass
    from concourse import mybir

    F32, BF16 = mybir.dt.float32, mybir.dt.bfloat16
    ALU, ACT, AX = mybir.AluOpType, mybir.ActivationFunctionType, mybir.AxisListType

    C = 128
    B, N = 4, 512
    TOK = B * N
    DEPTH, HEADS, DH, WIN = 6, 16, 64, 32
    HQ = 4
    QUADS = HEADS // HQ
    TILES = N // 128
    FF = 341
    FFC = [128, 128, FF - 256]
    EPS = 1e-5
    AH, AD = 8, 16
    LN2 = math.log(2.0)

    ctx = ExitStack()
    with ctx:
        def sb(name, shape, dt=F32, scope=ctx):
            return scope.enter_context(nc.sbuf_tensor(name, shape, dt))

        def sem(name, scope=ctx):
            return scope.enter_context(nc.semaphore(name))

        class Signal:

            def __init__(self, name, per=1, count=1, ahead=0):
                self.sem, self.per, self.count, self.ahead = sem(name), per, count, ahead

        class Steps:

            def __init__(self, eng, step, used=((1, 0),)):
                self.eng, self.step = eng, step
                self.known = {(m, c): eng.snap(step * m + c) for m, c in used}

            def count(self, sig, at=0):
                return self.known[sig.count * sig.per, (at + 1 + sig.ahead - sig.count) * sig.per]

        ps = ctx.enter_context(nc.psum_tensor("ps", [128, 8, 512], F32))

        xT = sb("xT", [C, TOK])
        zT = sb("zT", [C, TOK])
        mean_w = sb("mean_w", [C, C])
        ident = sb("ident", [128, 128])

        loaded = sem("loaded")
        n_loaded = [0]

        def stage_a():
            scope = ExitStack()
            with scope:
                def t(name, shape):
                    return sb("a_" + name, shape, scope=scope)

                wq, wk, wv, wo = (t(n, [C, C]) for n in ("wq", "wk", "wv", "wo"))
                headmask, blockmask = t("headmask", [C, AH]), t("blockmask", [C, C])
                causal, nw = t("causal", [128, 128]), t("nw", [128, AD])
                xc, sq, rstd, xn = (t(n, [C, 128]) for n in ("xc", "sq", "rstd", "xn"))
                prj, zc, carry, qz = t("prj", [128, 512]), t("zc", [C, 128]), t("carry", [C, 1]), t("qz", [C, 128])
                kz, st, state, upd = t("kz", [C, AH, 128]), t("st", [128, AH, 128]), t("state", [C, C]), t("upd", [C, C])
                den, o, osq, ss, oT = t("den", [128, AH]), t("o", [128, C]), t("osq", [128, C]), t("ss", [128, AH]), t("oT", [C, 128])

                S = {n: Signal("a_" + n) for n in (
                    "mean", "xc", "sq", "var", "lnv", "rstd", "xn", "prj", "prj_sb", "zc", "carry", "qz", "kz", "s",
                    "st", "o", "den", "den1", "denmax", "rden", "upd", "state", "on", "osq", "ss", "lnr", "rr", "on2", "on3",
                    "oT", "oT_sb", "y", "x", "mean2", "xc2", "sq2", "var2", "lnv2", "rstd2")}
                S["z"] = Signal("a_z", ahead=1)
                block = scope.enter_context(nc.Block())

                @block.sync
                def _(sp):
                    parts = [(xT[:, :], x_in), (mean_w[:, :], tabs["mean_w"]), (ident[:, :], tabs["ident"]),
                             (wq[:, :], wa["wq"]), (wk[:, :], wa["wk"]), (wv[:, :], wa["wv"]), (wo[:, :], wa["wo"]),
                             (headmask[:, :], tabs["headmask"]), (blockmask[:, :], tabs["blockmask"]),
                             (causal[:, :], tabs["causal"]), (nw[:, :], wa["nw"])]
                    sp.sem_inc(S["z"].sem, 1)
                    for dst, src in parts:
                        sp.dma_start(dst, src).then_inc(loaded, 16)
                    n_loaded[0] += 16 * len(parts)

                @block.tensor
                def _(pe):
                    pe.wait_ge(loaded, 16 * 11)
                    with pe.Fori(0, B) as b:
                        with pe.Fori(0, TILES) as i:
                            n = b * TILES + i
                            now = Steps(pe, n + 1)
                            cols = bass.ts(n, 128)
                            nc.tensor.matmul(ps[:, 0, 0:128], mean_w[:, :], xT[:, cols], start=True, stop=True).then_inc(S["mean"].sem, 1)
                            pe.wait_ge(S["sq"].sem, now.count(S["sq"]))
                            nc.tensor.matmul(ps[:, 1, 0:128], mean_w[:, :], sq[:, :], start=True, stop=True).then_inc(S["var"].sem, 1)
                            pe.wait_ge(S["xn"].sem, now.count(S["xn"]))
                            nc.tensor.matmul(ps[:, 2, 0:128], wq[:, :], xn[:, :], start=True, stop=True)
                            nc.tensor.matmul(ps[:, 2, 128:256], wk[:, :], xn[:, :], start=True, stop=True)
                            nc.tensor.matmul(ps[:, 2, 256:384], xn[:, :], wv[:, :], start=True, stop=True)
                            nc.tensor.matmul(ps[:, 2, 384:512], xn[:, :], wk[:, :], start=True, stop=True).then_inc(S["prj"].sem, 1)
                            pe.wait_ge(S["prj_sb"].sem, now.count(S["prj_sb"]))
                            pe.wait_ge(S["kz"].sem, now.count(S["kz"]))
                            for h in range(AH):
                                last = nc.tensor.matmul(ps[:, 3 + h // 4, 128 * (h % 4):128 * (h % 4) + 128], kz[:, h, :], prj[:, 0:128],
                                                        start=True, stop=True)
                            last.then_inc(S["s"].sem, 1)
                            pe.wait_ge(S["qz"].sem, now.count(S["qz"]))
                            nc.tensor.matmul(ps[:, 6, 0:128], prj[:, 384:512], prj[:, 256:384], start=True, stop=True)
                            nc.tensor.matmul(ps[:, 6, 128:128 + AH], qz[:, :], headmask[:, :], start=True, stop=True).then_inc(S["den"].sem, 1)
                            pe.wait_ge(S["st"].sem, now.count(S["st"]))
                            nc.tensor.matmul(ps[:, 5, 0:128], prj[:, 0:128], state[:, :], start=True, stop=False, skip_group_check=True)
                            for h in range(AH):
                                last = nc.tensor.matmul(ps[:, 5, AD * h:AD * h + AD], st[:, h, :], prj[:, 256 + AD * h:256 + AD * h + AD],
                                                        start=False, stop=True, skip_group_check=True)
                            last.then_inc(S["o"].sem, 1)
                            pe.wait_ge(S["on3"].sem, now.count(S["on3"]))
                            nc.tensor.transpose(ps[:, 7, 0:128], o[:, :], ident[:, :]).then_inc(S["oT"].sem, 1)
                            pe.wait_ge(S["oT_sb"].sem, now.count(S["oT_sb"]))
                            nc.tensor.matmul(ps[:, 7, 128:256], wo[:, :], oT[:, :], start=True, stop=True).then_inc(S["y"].sem, 1)
                            pe.wait_ge(S["x"].sem, now.count(S["x"]))
                            nc.tensor.matmul(ps[:, 0, 0:128], mean_w[:, :], xT[:, cols], start=True, stop=True).then_inc(S["mean2"].sem, 1)
                            pe.wait_ge(S["sq2"].sem, now.count(S["sq2"]))
                            nc.tensor.matmul(ps[:, 1, 0:128], mean_w[:, :], sq[:, :], start=True, stop=True).then_inc(S["var2"].sem, 1)

                @block.scalar
                def _(act):
                    act.preload_act_table_set("natural_log_exp_and_others")
                    with act.Fori(0, B * TILES) as n:
                        now = Steps(act, n + 1)
                        act.wait_ge(S["xc"].sem, now.count(S["xc"]))
                        nc.scalar.activation(sq[:, :], xc[:, :], ACT.Square).then_inc(S["sq"].sem, 1)
                        act.wait_ge(S["var"].sem, now.count(S["var"]))
                        nc.scalar.activation(rstd[:, :], ps[:, 1, 0:128], ACT.Ln, bias=EPS).then_inc(S["lnv"].sem, 1)
                        act.wait_ge(S["lnv"].sem, now.count(S["lnv"]))
                        nc.scalar.activation(rstd[:, :], rstd[:, :], ACT.Exp, scale=-0.5).then_inc(S["rstd"].sem, 1)
                        act.wait_ge(S["prj"].sem, now.count(S["prj"]))
                        nc.scalar.activation(prj[:, :], ps[:, 2, :], ACT.Copy).then_inc(S["prj_sb"].sem, 1)
                        act.wait_ge(S["den"].sem, now.count(S["den"]))
                        nc.scalar.activation(den[:, :], ps[:, 6, 128:128 + AH], ACT.Abs).then_inc(S["den1"].sem, 1)
                        act.wait_ge(S["on"].sem, now.count(S["on"]))
                        nc.scalar.activation(osq[:, :], o[:, :], ACT.Square).then_inc(S["osq"].sem, 1)
                        act.wait_ge(S["ss"].sem, now.count(S["ss"]))
                        nc.scalar.activation(ss[:, :], ss[:, :], ACT.Ln, bias=EPS, scale=1.0 / AD).then_inc(S["lnr"].sem, 1)
                        act.wait_ge(S["lnr"].sem, now.count(S["lnr"]))
                        nc.scalar.activation(ss[:, :], ss[:, :], ACT.Exp, scale=-0.5).then_inc(S["rr"].sem, 1)
                        act.wait_ge(S["oT"].sem, now.count(S["oT"]))
                        nc.scalar.activation(oT[:, :], ps[:, 7, 0:128], ACT.Copy).then_inc(S["oT_sb"].sem, 1)
                        act.wait_ge(S["xc2"].sem, now.count(S["xc2"]))
                        nc.scalar.activation(sq[:, :], xc[:, :], ACT.Square).then_inc(S["sq2"].sem, 1)
                        act.wait_ge(S["var2"].sem, now.count(S["var2"]))
                        nc.scalar.activation(rstd[:, :], ps[:, 1, 0:128], ACT.Ln, bias=EPS).then_inc(S["lnv2"].sem, 1)
                        act.wait_ge(S["lnv2"].sem, now.count(S["lnv2"]))
                        nc.scalar.activation(rstd[:, :], rstd[:, :], ACT.Exp, scale=-0.5).then_inc(S["rstd2"].sem, 1)

                @block.vector
                def _(dve):
                    dve.wait_ge(loaded, 16 * 11)
                    reset = sem("a_reset", scope)
                    with dve.Fori(0, B) as b:
                        nc.vector.memset(carry[:, :], 0.0).then_inc(reset, 1)
                        nc.vector.memset(state[:, :], 0.0).then_inc(reset, 1)
                        resets = dve.snap((b + 1) * 2)
                        with dve.Fori(0, TILES) as i:
                            n = b * TILES + i
                            now = Steps(dve, n + 1, ((1, 0), (1, 1)))
                            dve.wait_ge(reset, resets)
                            cols = bass.ts(n, 128)
                            dve.wait_ge(S["z"].sem, now.count(S["z"], -1))
                            dve.wait_ge(S["mean"].sem, now.count(S["mean"]))
                            nc.vector.tensor_tensor(xc[:, :], xT[:, cols], ps[:, 0, 0:128], ALU.subtract).then_inc(S["xc"].sem, 1)
                            dve.wait_ge(S["rstd"].sem, now.count(S["rstd"]))
                            nc.vector.tensor_tensor(xn[:, :], xc[:, :], rstd[:, :], ALU.mult).then_inc(S["xn"].sem, 1)
                            dve.wait_ge(S["prj_sb"].sem, now.count(S["prj_sb"]))
                            nc.vector.tensor_tensor_scan(zc[:, :], prj[:, 128:256], prj[:, 128:256], carry[:, :], ALU.add, ALU.bypass).then_inc(S["zc"].sem, 1)
                            nc.vector.tensor_tensor(kz[:, :, :], prj[:, 128:256].unsqueeze(1).broadcast_to([C, AH, 128]),
                                                    headmask[:, :].unsqueeze(2).broadcast_to([C, AH, 128]), ALU.mult).then_inc(S["kz"].sem, 1)
                            dve.wait_ge(S["zc"].sem, now.count(S["zc"]))
                            nc.vector.tensor_copy(carry[:, :], zc[:, 127:128]).then_inc(S["carry"].sem, 1)
                            nc.vector.tensor_tensor(qz[:, :], prj[:, 0:128], zc[:, :], ALU.mult).then_inc(S["qz"].sem, 1)
                            dve.wait_ge(S["s"].sem, now.count(S["s"]))
                            nc.vector.tensor_tensor(st[:, :, :], ps[:, 3:5, :].rearrange("p a (h q) -> p (a h) q", q=128),
                                                    causal[:, :].unsqueeze(1).broadcast_to([128, AH, 128]), ALU.mult).then_inc(S["st"].sem, 1)
                            dve.wait_ge(S["den1"].sem, now.count(S["den1"]))
                            nc.vector.tensor_scalar_max(den[:, :], den[:, :], 1.0).then_inc(S["denmax"].sem, 1)
                            nc.vector.tensor_tensor(upd[:, :], ps[:, 6, 0:128], blockmask[:, :], ALU.mult).then_inc(S["upd"].sem, 1)
                            dve.wait_ge(S["upd"].sem, now.count(S["upd"]))
                            dve.wait_ge(S["o"].sem, now.count(S["o"]))
                            nc.vector.tensor_tensor(state[:, :], state[:, :], upd[:, :], ALU.add).then_inc(S["state"].sem, 1)
                            dve.wait_ge(S["denmax"].sem, now.count(S["denmax"]))
                            nc.vector.reciprocal(den[:, :], den[:, :]).then_inc(S["rden"].sem, 1)
                            dve.wait_ge(S["rden"].sem, now.count(S["rden"]))
                            nc.vector.tensor_tensor(o[:, :].rearrange("p (h d) -> p h d", d=AD), ps[:, 5, 0:128].rearrange("p (h d) -> p h d", d=AD),
                                                    den[:, :].unsqueeze(2).broadcast_to([128, AH, AD]), ALU.mult).then_inc(S["on"].sem, 1)
                            dve.wait_ge(S["osq"].sem, now.count(S["osq"]))
                            nc.vector.tensor_reduce(ss[:, :], osq[:, :].rearrange("p (h d) -> p h d", d=AD), AX.X, ALU.add).then_inc(S["ss"].sem, 1)
                            dve.wait_ge(S["rr"].sem, now.count(S["rr"]))
                            nc.vector.tensor_tensor(o[:, :].rearrange("p (h d) -> p h d", d=AD), o[:, :].rearrange("p (h d) -> p h d", d=AD),
                                                    ss[:, :].unsqueeze(2).broadcast_to([128, AH, AD]), ALU.mult).then_inc(S["on2"].sem, 1)
                            dve.wait_ge(S["on2"].sem, now.count(S["on2"]))
                            nc.vector.tensor_tensor(o[:, :].rearrange("p (h d) -> p h d", d=AD), o[:, :].rearrange("p (h d) -> p h d", d=AD),
                                                    nw[:, :].unsqueeze(1).broadcast_to([128, AH, AD]), ALU.mult).then_inc(S["on3"].sem, 1)
                            dve.wait_ge(S["y"].sem, now.count(S["y"]))
                            nc.vector.tensor_tensor(xT[:, cols], xT[:, cols], ps[:, 7, 128:256], ALU.add).then_inc(S["x"].sem, 1)
                            dve.wait_ge(S["mean2"].sem, now.count(S["mean2"]))
                            nc.vector.tensor_tensor(xc[:, :], xT[:, cols], ps[:, 0, 0:128], ALU.subtract).then_inc(S["xc2"].sem, 1)
                            dve.wait_ge(S["rstd2"].sem, now.count(S["rstd2"]))
                            dve.wait_ge(S["state"].sem, now.count(S["state"]))
                            dve.wait_ge(S["carry"].sem, now.count(S["carry"]))
                            nc.vector.tensor_tensor(zT[:, cols], xc[:, :], rstd[:, :], ALU.mult).then_inc(S["z"].sem, 1)


        NW = N // WIN
        PAD = WIN
        NORM_FLOOR_INV = 1e12
        PRE = 24
        NJ = 3

        def per_quad(name, per=1, ahead=0):
            return Signal(name, per, QUADS, ahead)

        ORDER = []
        for g in range(QUADS):
            ORDER += [("qk", g, i) for i in range(4)]
            if g % 2 == 0:
                ORDER += [("v", g // 2, i) for i in range(TILES)]
        qk_ready = [per_quad(f"qk_ready{i}", ahead=1 if i == 3 else 0) for i in range(4)]
        qk_read = [per_quad(f"qk_read{i}", ahead=1) for i in range(4)]
        v_ready = [Signal(f"v_ready{i}", 1, 2) for i in range(TILES)]
        v_read = [Signal(f"v_read{i}", 1, 2) for i in range(TILES)]
        xs_done = Signal("xs_done", 32, ahead=1)
        sq_done = Signal("sq_done", 1, 4 * QUADS)
        sq_sum, n_ready = per_quad("sq_sum"), per_quad("n_ready", ahead=1)
        n_log, n_inv, u_done, r_done = per_quad("n_log"), per_quad("n_inv"), per_quad("u_done", 2), per_quad("r_done")
        gain, rope_q, rope_k = per_quad("gain"), per_quad("rope_q", ahead=1), per_quad("rope_k", ahead=1)
        k_dma, s_ready = per_quad("k_dma", 16 * HQ), per_quad("s_ready", ahead=2)
        s_max, s_sub, p_exp = per_quad("s_max"), per_quad("s_sub", ahead=1), per_quad("p_exp")
        p_sum, p_inv, p_norm = per_quad("p_sum"), per_quad("p_inv"), per_quad("p_norm")
        p_tr, t_dma = per_quad("p_tr", ahead=2), per_quad("t_dma", 16 * HQ, ahead=2)
        o_ready = [per_quad(f"o_ready{i}", ahead=3) for i in range(2)]
        o_read = [per_quad(f"o_read{i}", ahead=1) for i in range(2)]
        vs_dma = Signal("vs_dma", 32, 2)
        wo_ready = Signal("wo_ready", 1, 1, 1)
        F = {n: Signal("f_" + n) for n in ("x1", "mean", "xc", "sq", "var", "lnv", "rstd", "xn", "xa", "w2")}
        fs_done = Signal("fs_done", 2)
        x2 = Signal("x2", 1, 1, 4)
        gate_ready, gate_done, val_ready, val_done = (Signal(n, 1, 3) for n in ("gate_ready", "gate_done", "val_ready", "val_done"))
        w_attn, w_out, w_ff = Signal("w_attn", 32), Signal("w_out", 16), Signal("w_ff", 64)
        GRANTED = [xs_done, qk_ready[3], *qk_read, n_ready, rope_q, rope_k, s_ready, s_sub, p_tr, t_dma, *o_ready, *o_read, wo_ready, x2]

        SP_USES = [(1, 1), (2, -1), (2, 0), (4, -2), (4, -1), (4, 0), (4, 1), (4, 2)]
        PE_USES = [(32, 0), (1, 0), (1, 3), (2, -1), (2, 0), (3, -2), (3, -1), (3, 0), *((4, c) for c in range(-3, 2)), (64, -32), (64, 0),
                   *((256, 64 * c) for c in range(-3, 3))]
        ACT_USES = [(1, 0), (2, -1), (2, 0), (3, -2), (3, -1), (3, 0), *((4, c) for c in range(-3, 4))]
        POOL_USES = [*((4, c) for c in range(-3, 1)), *((16, c) for c in range(-12, 1, 4))]
        DVE_USES = [(1, 0), (1, 1), (3, -2), (3, -1), (3, 0), *((4, c) for c in range(-3, 3)), *((8, c) for c in range(-6, 1, 2)),
                    *((256, 64 * c) for c in range(-3, 1))]

        def stage_ffn(phase):
            scope = ExitStack()
            with scope:
                def t(name, shape, dt=F32):
                    return sb(f"f{phase}_" + name, shape, dt, scope=scope)

                wqkv, wout = t("wqkv", [C, QUADS, 6, 128]), t("wout", [128, 8, C])
                w1, w2 = t("w1", [C, 2 * FF]), t("w2", [128, 3, C])
                pa, pf = t("pa", [128, 4]), t("pf", [128, 9])
                tan2, cos2 = t("tan2", [128, 2, N]), t("cos2", [128, 2, N])
                mask, ones = t("mask", [128, 2, 512], BF16), t("ones", [128, 128])
                identb = t("identb", [128, 128], BF16)
                xs, x1 = t("xs", [C, N]), t("x1", [C, N])
                sq, ab, rn, u = t("sq", [128, 4, N]), t("ab", [128, 2, 4, N]), t("rn", [128, 2, N]), t("u", [128, 4, N])
                kb = t("kb", [128, 2, HQ, PAD + N])
                p, pt = t("p", [128, 2, 1024]), t("pt", [128, 2, 1024])
                tb = t("tb", [128, HQ, 1024])
                v, vs = t("v", [128, TILES, 1024]), t("vs", [128, TILES, 1024])
                ot = t("ot", [128, 8, N])
                mx, rs = t("mx", [128, 16]), t("rs", [128, 16])
                fs, fc, fq, fn, hid = t("fs", [C, N]), t("fc", [C, N]), t("fq", [C, N]), t("fn", [C, N]), t("hid", [128, 3, N])
                consts = sem(f"f{phase}_consts", scope)
                zeroed = sem(f"f{phase}_zeroed", scope)
                masked = sem(f"f{phase}_masked", scope)
                xs_first = sem(f"f{phase}_xs_first", scope)
                N_CONST, N_ZERO = 7 * 16, 6
                block = scope.enter_context(nc.Block())

                FIRST = phase * DEPTH

                def window(tile, i):
                    return 128 * tile + WIN * i

                def bank(*which):
                    return ps[:, ORDER.index(which) % NJ, :]

                NO, SS, FB = (3, 4), (5, 6), 7

                @block.sync
                def _(sp):
                    if phase == 0:
                        for s in GRANTED:
                            if s.ahead:
                                sp.sem_inc(s.sem, s.ahead * s.per)
                    for dst, src in ((tan2[:, :, :], tabs["tan2"]), (cos2[:, :, :], tabs["cos2"]), (ones[:, :], tabs["headsum"]),
                                     (fq[:, :], tabs["mask0"]), (fn[:, :], tabs["mask1"]), (fs[:, 0:128], tabs["ident"]),
                                     (mean_w[:, :], tabs["mean_w"])):
                        sp.dma_start(dst, src).then_inc(consts, 16)
                    sp.wait_ge(zeroed, N_ZERO)
                    sp.dma_start(xs[0:64, :], zT[0:64, 0:N]).then_inc(xs_first, 16)
                    sp.dma_start(xs[64:128, 1:N], zT[64:128, 0:N - 1]).then_inc(xs_first, 16)
                    with sp.Fori(FIRST, FIRST + DEPTH) as layer:
                        last = Steps(sp, layer * B, ((4, 1), (1, 1), (1, 4)))
                        at = layer - FIRST
                        sp.wait_ge(qk_ready[3].sem, last.count(qk_ready[3], 3))
                        sp.dma_start(wqkv[:, :, :, :], wf["wqkv"][bass.ds(at, 1)].rearrange("l c q k n -> (l c) q k n")).then_inc(w_attn.sem, 16)
                        sp.dma_start(pa[:, :], wf["pa"][bass.ds(at, 1)].rearrange("l c n -> (l c) n")).then_inc(w_attn.sem, 16)
                        sp.wait_ge(wo_ready.sem, last.count(wo_ready))
                        sp.dma_start(wout[:, :, :], wf["wout"][bass.ds(at, 1)].rearrange("l (k p) n -> p (l k) n", p=128)).then_inc(w_out.sem, 16)
                        sp.wait_ge(x2.sem, last.count(x2))
                        sp.dma_start(w1[:, :], wf["w1"][bass.ds(at, 1)].rearrange("l c n -> (l c) n")).then_inc(w_ff.sem, 16)
                        sp.dma_start(w2[:, 0:2, :], wf["w2"][bass.ds(at, 1), 0:256].rearrange("l (k p) n -> p (l k) n", p=128)).then_inc(w_ff.sem, 16)
                        sp.dma_start(w2[0:FFC[2], 2, :], wf["w2"][bass.ds(at, 1), 256:FF].rearrange("l p n -> (l p) n")).then_inc(w_ff.sem, 16)
                        sp.dma_start(pf[:, :], wf["pf"][bass.ds(at, 1)].rearrange("l c n -> (l c) n")).then_inc(w_ff.sem, 16)
                        with sp.Fori(0, B) as b:
                            now = Steps(sp, layer * B + b + 1, SP_USES)
                            next_col = sp.snap((b + 1) % B * N)
                            for k in range(QUADS + 2):
                                if k in (0, 2):
                                    i = k // 2
                                    for tile in range(TILES):
                                        sp.wait_ge(v_read[tile].sem, now.count(v_read[tile], i))
                                    half = slice(512 * i, 512 * i + 512)
                                    sp.dma_start(vs[WIN:128, :, half], v[0:128 - WIN, :, half]).then_inc(vs_dma.sem, 16)
                                    sp.dma_start(vs[0:WIN, 1:TILES, half], v[128 - WIN:128, 0:TILES - 1, half]).then_inc(vs_dma.sem, 16)
                                if k == QUADS:
                                    sp.wait_ge(x2.sem, now.count(x2, -3))
                                    sp.wait_ge(qk_ready[3].sem, now.count(qk_ready[3], 3))
                                    sp.dma_start(xs[0:64, :], zT[0:64, bass.ds(next_col, N)]).then_inc(xs_done.sem, 16)
                                    sp.dma_start(xs[64:128, 1:N], zT[64:128, bass.ds(next_col, N - 1)]).then_inc(xs_done.sem, 16)
                                if k < QUADS:
                                    sp.wait_ge(rope_k.sem, now.count(rope_k, k))
                                    sp.wait_ge(s_ready.sem, now.count(s_ready, k - 1))
                                    for h in range(HQ):
                                        rows = slice(32 * h, 32 * h + 32)
                                        sp.dma_start(kb[rows, :, h, PAD:], ab[rows, k % 2, 2:4, :]).then_inc(k_dma.sem, 16)
                                if 1 <= k <= QUADS:
                                    g = k - 1
                                    sp.wait_ge(p_tr.sem, now.count(p_tr, g))
                                    sp.wait_ge(o_ready[1].sem, now.count(o_ready[1], g - 1))
                                    for w in range(4):
                                        rows = slice(32 * w, 32 * w + 32)
                                        sp.dma_start(tb[rows, w, :], pt[rows, g % 2, :]).then_inc(t_dma.sem, 16)

                @block.tensor
                def _(pe):
                    pe.wait_ge(masked, 3)
                    pe.wait_ge(consts, N_CONST)
                    pe.wait_ge(xs_first, 32)
                    with pe.Fori(FIRST, FIRST + DEPTH) as layer:
                        own = Steps(pe, layer + 1, ((32, 0), (16, 0), (64, 0)))
                        with pe.Fori(0, B) as b:
                            now = Steps(pe, layer * B + b + 1, PE_USES)

                            def bank_free(*which):
                                n = ORDER.index(which) - NJ
                                kind, g, i = ORDER[n]
                                if kind == "qk":
                                    pe.wait_ge(qk_read[i].sem, now.count(qk_read[i], g if n >= 0 else g - QUADS))
                                else:
                                    pe.wait_ge(v_read[i].sem, now.count(v_read[i], g))

                            def project(g):
                                for i in range(4):
                                    bank_free("qk", g, i)
                                    nc.tensor.matmul(bank("qk", g, i), wqkv[:, g, i, :], xs[:, :], start=True, stop=True).then_inc(qk_ready[i].sem, 1)
                                if g % 2 == 0:
                                    for tile in range(TILES):
                                        bank_free("v", g // 2, tile)
                                        nc.tensor.matmul(bank("v", g // 2, tile), xs[:, 128 * tile:128 * tile + 128], wqkv[:, g:g + 2, 4:6, :],
                                                         start=True, stop=True).then_inc(v_ready[tile].sem, 1)

                            def norms(g):
                                pe.wait_ge(sq_sum.sem, now.count(sq_sum, g))
                                if g == 0 or g == 3:
                                    for i in range(2):
                                        pe.wait_ge(o_read[i].sem, now.count(o_read[i], -1 if g == 0 else 0))
                                else:
                                    pe.wait_ge(n_log.sem, now.count(n_log, g - 1))
                                for i in range(2):
                                    last = nc.tensor.matmul(ps[:, NO[i], :], ones[:, :], sq[:, 2 * i, :], start=True, stop=True)
                                last.then_inc(n_ready.sem, 1)

                            def scores(g):
                                pe.wait_ge(k_dma.sem, now.count(k_dma, g))
                                pe.wait_ge(rope_q.sem, now.count(rope_q, g))
                                pe.wait_ge(s_sub.sem, now.count(s_sub, g - 1))
                                for j in range(2):
                                    nc.tensor.matmul(ps[:, SS[j], :], identb[:, :], mask[:, j, :], start=True, stop=False, skip_group_check=True)
                                    for tile in (2 * j, 2 * j + 1):
                                        for i in range(4):
                                            w0 = window(tile, i)
                                            rows = slice(32 * i, 32 * i + 32)
                                            for a in range(2):
                                                last = nc.tensor.matmul(ps[rows, SS[j], 256 * (tile % 2):256 * (tile % 2) + 256],
                                                                        ab[:, g % 2, a, w0:w0 + WIN], kb[:, a, :, w0:w0 + 2 * WIN],
                                                                        start=False, stop=a == 1, skip_group_check=True, tile_position=(0, 32 * i))
                                if j == 1:
                                        last.then_inc(s_ready.sem, 1)

                            def values(g):
                                pe.wait_ge(t_dma.sem, now.count(t_dma, g))
                                pe.wait_ge(vs_dma.sem, now.count(vs_dma, g // 2))
                                if g == 2 or g == 3:
                                    for i in range(2):
                                        pe.wait_ge(o_read[i].sem, now.count(o_read[i], g - 1))
                                pe.wait_ge(n_log.sem, now.count(n_log, min(g + 2, 3)))
                                for pair in range(2):
                                    for tile in range(TILES):
                                        for h in (2 * pair, 2 * pair + 1):
                                            rows = slice(64 * (h % 2), 64 * (h % 2) + 64)
                                            for blk, val in ((0, vs), (1, v)):
                                                c0 = ((tile * HQ + h) * 2 + blk) * WIN
                                                last = nc.tensor.matmul(ps[rows, NO[pair], 128 * tile:128 * tile + 128],
                                                                        val[:, tile, 256 * g + 64 * h:256 * g + 64 * h + 64], tb[:, :, c0:c0 + WIN],
                                                                        start=blk == 0, stop=blk == 1, tile_position=(0, 64 * (h % 2)))
                                    last.then_inc(o_ready[pair].sem, 1)

                            pe.wait_ge(w_attn.sem, own.count(w_attn))
                            pe.wait_ge(xs_done.sem, now.count(xs_done, -1))
                            for k in range(QUADS + 2):
                                if k < QUADS:
                                    project(k)
                                if 1 <= k <= QUADS:
                                    scores(k - 1)
                                if k < QUADS:
                                    norms(k)
                                if k >= 2:
                                    values(k - 2)

                            f = ps[:, FB, :]
                            pe.wait_ge(w_out.sem, own.count(w_out))
                            pe.wait_ge(w_ff.sem, own.count(w_ff))
                            for i in range(2):
                                pe.wait_ge(o_read[i].sem, now.count(o_read[i], 3))
                            pe.wait_ge(x2.sem, now.count(x2, -1))
                            for i in range(8):
                                last = nc.tensor.matmul(f, wout[:, i, :], ot[:, i, :], start=i == 0, stop=i == 7)
                            last.then_inc(wo_ready.sem, 1)
                            pe.wait_ge(fs_done.sem, now.count(fs_done))
                            nc.tensor.matmul(f, mean_w[:, :], fs[:, :], start=True, stop=True).then_inc(F["mean"].sem, 1)
                            pe.wait_ge(F["sq"].sem, now.count(F["sq"]))
                            nc.tensor.matmul(f, mean_w[:, :], fq[:, :], start=True, stop=True).then_inc(F["var"].sem, 1)
                            pe.wait_ge(F["xa"].sem, now.count(F["xa"]))
                            for first, ready, done in ((FF, gate_ready, gate_done), (0, val_ready, val_done)):
                                for j in range(3):
                                    if j:
                                        pe.wait_ge(done.sem, now.count(done, j - 1))
                                    elif first == 0:
                                        pe.wait_ge(gate_done.sem, now.count(gate_done, 2))
                                    c0, m = first + 128 * j, FFC[j]
                                    nc.tensor.matmul(ps[0:m, FB, :], w1[:, c0:c0 + m], fn[:, :], start=True, stop=True).then_inc(ready.sem, 1)
                            pe.wait_ge(val_done.sem, now.count(val_done, 2))
                            for j in range(3):
                                m = FFC[j]
                                last = nc.tensor.matmul(f, w2[0:m, j, :], hid[0:m, j, :], start=j == 0, stop=j == 2)
                            last.then_inc(F["w2"].sem, 1)

                @block.scalar
                def _(act):
                    act.preload_act_table_set("natural_log_exp_and_others")
                    act.wait_ge(masked, 3)
                    act.wait_ge(zeroed, N_ZERO)
                    with act.Fori(FIRST, FIRST + DEPTH) as layer:
                        own = Steps(act, layer + 1, ((32, 0), (64, 0)))
                        with act.Fori(0, B) as b:
                            now = Steps(act, layer * B + b + 1, ACT_USES)
                            act.wait_ge(w_attn.sem, own.count(w_attn))
                            for k in range(QUADS + 2):
                                if k < QUADS:
                                    g = k
                                    act.wait_ge(n_ready.sem, now.count(n_ready, g - 1))
                                    act.wait_ge(s_ready.sem, now.count(s_ready, g - 2))
                                    for i in range(4):
                                        act.wait_ge(qk_ready[i].sem, now.count(qk_ready[i], g))
                                        nc.scalar.activation(sq[:, i, :], bank("qk", g, i), ACT.Square).then_inc(sq_done.sem, 1)
                                        nc.scalar.activation(ab[:, g % 2, i, :], bank("qk", g, i), ACT.Identity, scale=pa[:, i:i + 1]).then_inc(qk_read[i].sem, 1)
                                    if g % 2 == 0:
                                        act.wait_ge(o_ready[1].sem, now.count(o_ready[1], g + 1 - QUADS))
                                        for tile in range(TILES):
                                            act.wait_ge(v_ready[tile].sem, now.count(v_ready[tile], g // 2))
                                            nc.scalar.activation(v[:, tile, 512 * (g // 2):512 * (g // 2) + 512], bank("v", g // 2, tile), ACT.Copy).then_inc(v_read[tile].sem, 1)
                                    act.wait_ge(rope_q.sem, now.count(rope_q, g - 1))
                                    act.wait_ge(rope_k.sem, now.count(rope_k, g - 1))
                                    act.wait_ge(n_ready.sem, now.count(n_ready, g))
                                    nc.scalar.activation(rn[:, :, :], ps[:, 3:5, :], ACT.Ln, scale=2.0 ** PRE).then_inc(n_log.sem, 1)
                                    act.wait_ge(n_log.sem, now.count(n_log, g))
                                    nc.scalar.activation(rn[:, :, :], rn[:, :, :], ACT.Exp, scale=-0.5).then_inc(n_inv.sem, 1)
                                if 1 <= k <= QUADS:
                                    g = k - 1
                                    act.wait_ge(s_sub.sem, now.count(s_sub, g))
                                    nc.scalar.activation(p[:, g % 2, :], p[:, g % 2, :], ACT.Exp).then_inc(p_exp.sem, 1)
                                if k >= 2:
                                    g = k - 2
                                    if g == 0:
                                        act.wait_ge(wo_ready.sem, now.count(wo_ready, -1))
                                    for pair in range(2):
                                        act.wait_ge(o_ready[pair].sem, now.count(o_ready[pair], g))
                                        nc.scalar.activation(ot[:, 2 * g + pair, :], ps[:, NO[pair], :], ACT.Copy).then_inc(o_read[pair].sem, 1)
                            act.wait_ge(w_ff.sem, own.count(w_ff))
                            act.wait_ge(F["x1"].sem, now.count(F["x1"]))
                            nc.scalar.activation(fs[0:64, :], x1[0:64, :], ACT.Copy).then_inc(fs_done.sem, 1)
                            nc.scalar.activation(fs[64:128, 1:N], x1[64:128, 0:N - 1], ACT.Copy).then_inc(fs_done.sem, 1)
                            act.wait_ge(F["xc"].sem, now.count(F["xc"]))
                            nc.scalar.activation(fq[:, :], fc[:, :], ACT.Square).then_inc(F["sq"].sem, 1)
                            act.wait_ge(F["var"].sem, now.count(F["var"]))
                            nc.scalar.activation(fq[:, :], ps[:, FB, :], ACT.Ln, bias=EPS).then_inc(F["lnv"].sem, 1)
                            act.wait_ge(F["lnv"].sem, now.count(F["lnv"]))
                            nc.scalar.activation(fq[:, :], fq[:, :], ACT.Exp, scale=-0.5).then_inc(F["rstd"].sem, 1)
                            act.wait_ge(F["xn"].sem, now.count(F["xn"]))
                            nc.scalar.activation(fn[:, :], fc[:, :], ACT.Identity, bias=pf[:, 1:2], scale=pf[:, 0:1]).then_inc(F["xa"].sem, 1)
                            for j in range(3):
                                m = FFC[j]
                                act.wait_ge(gate_ready.sem, now.count(gate_ready, j))
                                nc.scalar.activation(hid[0:m, j, :], ps[0:m, FB, :], ACT.Gelu, bias=pf[0:m, 3 + j:4 + j]).then_inc(gate_done.sem, 1)
                            act.preload_act_table_set("natural_log_exp_and_others")

                @block.gpsimd
                def _(pool):
                    nc.gpsimd.memset(kb[:, :, :, :], 0.0).then_inc(zeroed, 1)
                    nc.gpsimd.memset(vs[0:WIN, 0, :], 0.0).then_inc(zeroed, 1)
                    with pool.Fori(FIRST, FIRST + DEPTH) as layer:
                        with pool.Fori(0, B) as b:
                            now = Steps(pool, layer * B + b + 1, POOL_USES)
                            for k in range(QUADS + 1):
                                if k < QUADS:
                                    pool.wait_ge(sq_done.sem, now.count(sq_done, 4 * k + 3))
                                    nc.gpsimd.tensor_tensor(sq[:, 0:3:2, :], sq[:, 0:3:2, :], sq[:, 1:4:2, :], ALU.add).then_inc(sq_sum.sem, 1)
                                    pool.wait_ge(r_done.sem, now.count(r_done, k))
                                    pool.wait_ge(gain.sem, now.count(gain, k))
                                    nc.gpsimd.tensor_tensor(ab[:, k % 2, 0:2, :], u[:, 0:2, :], rn[:, 0:1, :].broadcast_to([128, 2, N]), ALU.mult).then_inc(rope_q.sem, 1)
                                if k >= 1:
                                    g = k - 1
                                    pool.wait_ge(p_inv.sem, now.count(p_inv, g))
                                    nc.gpsimd.tensor_tensor(p[:, g % 2, :].rearrange("p (n k) -> p n k", k=64), p[:, g % 2, :].rearrange("p (n k) -> p n k", k=64),
                                                            rs[:, :].unsqueeze(2).broadcast_to([128, 16, 64]), ALU.mult).then_inc(p_norm.sem, 1)

                @block.vector
                def _(dve):
                    nc.vector.memset(tb[:, :, :], 0.0).then_inc(zeroed, 1)
                    nc.vector.memset(xs[64:128, 0:1], 0.0).then_inc(zeroed, 1)
                    dve.wait_ge(consts, N_CONST)
                    nc.vector.tensor_copy(mask[:, 0, :], fq[:, :]).then_inc(masked, 1)
                    nc.vector.tensor_copy(mask[:, 1, :], fn[:, :]).then_inc(masked, 1)
                    nc.vector.tensor_copy(identb[:, :], fs[:, 0:128]).then_inc(masked, 1)
                    dve.wait_ge(masked, 3)
                    nc.vector.memset(fs[64:128, 0:1], 0.0).then_inc(zeroed, 2)
                    dve.wait_ge(zeroed, N_ZERO)
                    with dve.Fori(FIRST, FIRST + DEPTH) as layer:
                        own = Steps(dve, layer + 1, ((64, 0),))
                        with dve.Fori(0, B) as b:
                            now = Steps(dve, layer * B + b + 1, DVE_USES)
                            cols = bass.ts(b, N)
                            for k in range(QUADS + 1):
                                if k < QUADS:
                                    for i in range(4):
                                        dve.wait_ge(qk_read[i].sem, now.count(qk_read[i], k))
                                    dve.wait_ge(rope_q.sem, now.count(rope_q, k - 1))
                                    dve.wait_ge(rope_k.sem, now.count(rope_k, k - 1))
                                    for a in range(2):
                                        nc.vector.tensor_tensor(u[:, a:4:2, :], ab[:, k % 2, 1 - a:4:2, :], tan2[:, a:a + 1, :].broadcast_to([128, 2, N]),
                                                                ALU.mult).then_inc(u_done.sem, 1)
                                    dve.wait_ge(u_done.sem, now.count(u_done, k))
                                    nc.vector.tensor_tensor(u[:, :, :], u[:, :, :], ab[:, k % 2, :, :], ALU.add).then_inc(r_done.sem, 1)
                                if k >= 1:
                                    g = k - 1
                                    srow = ps[:, 5:7, :].rearrange("p a (n k) -> p (a n) k", k=64)
                                    prow = p[:, g % 2, :].rearrange("p (n k) -> p n k", k=64)
                                    dve.wait_ge(s_ready.sem, now.count(s_ready, g))
                                    nc.vector.tensor_reduce(mx[:, :], srow, AX.X, ALU.max).then_inc(s_max.sem, 1)
                                    dve.wait_ge(s_max.sem, now.count(s_max, g))
                                    dve.wait_ge(p_tr.sem, now.count(p_tr, g - 2))
                                    nc.vector.tensor_tensor(prow, srow, mx[:, :].unsqueeze(2).broadcast_to([128, 16, 64]), ALU.subtract).then_inc(s_sub.sem, 1)
                                if k < QUADS:
                                    dve.wait_ge(n_inv.sem, now.count(n_inv, k))
                                    nc.vector.scalar_tensor_tensor(out=rn[:, :, :], in0=rn[:, :, :], scalar=NORM_FLOOR_INV / 2 ** (PRE // 2), in1=cos2[:, :, :],
                                                                   op0=ALU.min, op1=ALU.mult).then_inc(gain.sem, 1)
                                    dve.wait_ge(gain.sem, now.count(gain, k))
                                    dve.wait_ge(r_done.sem, now.count(r_done, k))
                                    nc.vector.tensor_tensor(ab[:, k % 2, 2:4, :], u[:, 2:4, :], rn[:, 1:2, :].broadcast_to([128, 2, N]), ALU.mult).then_inc(rope_k.sem, 1)
                                if k >= 1:
                                    g = k - 1
                                    dve.wait_ge(p_exp.sem, now.count(p_exp, g))
                                    nc.vector.tensor_reduce(rs[:, :], p[:, g % 2, :].rearrange("p (n k) -> p n k", k=64), AX.X, ALU.add).then_inc(p_sum.sem, 1)
                                    dve.wait_ge(p_sum.sem, now.count(p_sum, g))
                                    nc.vector.reciprocal(rs[:, :], rs[:, :]).then_inc(p_inv.sem, 1)
                                    dve.wait_ge(p_norm.sem, now.count(p_norm, g))
                                    dve.wait_ge(t_dma.sem, now.count(t_dma, g - 2))
                                    nc.vector.transpose(pt[:, g % 2, :], p[:, g % 2, :]).then_inc(p_tr.sem, 1)
                            f = ps[:, FB, :]
                            dve.wait_ge(w_ff.sem, own.count(w_ff))
                            dve.wait_ge(wo_ready.sem, now.count(wo_ready))
                            nc.vector.tensor_tensor(x1[:, :], zT[:, cols], f, ALU.add).then_inc(F["x1"].sem, 1)
                            dve.wait_ge(F["mean"].sem, now.count(F["mean"]))
                            nc.vector.tensor_tensor(fc[:, :], fs[:, :], f, ALU.subtract).then_inc(F["xc"].sem, 1)
                            dve.wait_ge(F["rstd"].sem, now.count(F["rstd"]))
                            nc.vector.tensor_tensor(fc[:, :], fc[:, :], fq[:, :], ALU.mult).then_inc(F["xn"].sem, 1)
                            for j in range(3):
                                m = FFC[j]
                                dve.wait_ge(gate_done.sem, now.count(gate_done, j))
                                dve.wait_ge(val_ready.sem, now.count(val_ready, j))
                                nc.vector.scalar_tensor_tensor(out=hid[0:m, j, :], in0=ps[0:m, FB, :], scalar=pf[0:m, 6 + j:7 + j], in1=hid[0:m, j, :],
                                                               op0=ALU.add, op1=ALU.mult).then_inc(val_done.sem, 1)
                            dve.wait_ge(F["w2"].sem, now.count(F["w2"]))
                            nc.vector.scalar_tensor_tensor(out=zT[:, cols], in0=f, scalar=pf[:, 2:3], in1=x1[:, :], op0=ALU.add, op1=ALU.add).then_inc(x2.sem, 1)

        def stage_b():
            scope = ExitStack()
            with scope:
                def t(name, shape):
                    return sb("b_" + name, shape, scope=scope)

                wq, wk, wv = (t(n, [C, C]) for n in ("wq", "wk", "wv"))
                wqr, wkr = t("wqr", [C, C]), t("wkr", [C, C])
                qcos, qsin, kcos, ksin, decay = (t(n, [128, N]) for n in ("qcos", "qsin", "kcos", "ksin", "decay"))
                xb, xc, sq, xn = (t(n, [C, N]) for n in ("xb", "xc", "sq", "xn"))
                rope, qk = t("rope", [C, 4, N]), t("qk", [C, 2, N])
                v, st = t("v", [128, N]), t("st", [128, TILES, N])
                names = ("x", "mean", "xc", "sq", "var", "lnv", "rstd", "xn", "proj", "v_sb", "rope4", "qk", "scores", "st", "ret",
                         "x2", "xout", "mean2", "xc2", "sq2", "var2", "lnv2", "rstd2")
                S = {n: Signal("b_" + n) for n in names}
                S["rope4"].per, S["st"].per, S["qk"].per = 4, TILES, 2
                S["z"] = Signal("b_z", ahead=1)
                consts, turned = sem("b_consts", scope), sem("b_turned", scope)
                USES = [(1, 0), (1, 1), (2, 0), (4, 0)]
                block = scope.enter_context(nc.Block())

                @block.sync
                def _(sp):
                    sp.sem_inc(S["z"].sem, 1)
                    for dst, src in ((wq, wb["wq"]), (wk, wb["wk"]), (wv, wb["wv"]), (qcos, tabs["ret_qcos"]), (qsin, tabs["ret_qsin"]),
                                     (kcos, tabs["ret_kcos"]), (ksin, tabs["ret_ksin"]), (decay, tabs["ret_decay"])):
                        sp.dma_start(dst[:, :], src).then_inc(consts, 16)

                @block.tensor
                def _(pe):
                    pe.wait_ge(turned, 4)
                    with pe.Fori(0, B) as b:
                        now = Steps(pe, b + 1, USES)
                        pe.wait_ge(S["x"].sem, now.count(S["x"]))
                        nc.tensor.matmul(ps[:, 0, :], mean_w[:, :], xb[:, :], start=True, stop=True).then_inc(S["mean"].sem, 1)
                        pe.wait_ge(S["sq"].sem, now.count(S["sq"]))
                        nc.tensor.matmul(ps[:, 1, :], mean_w[:, :], sq[:, :], start=True, stop=True).then_inc(S["var"].sem, 1)
                        pe.wait_ge(S["xn"].sem, now.count(S["xn"]))
                        for i, w in enumerate((wq, wqr, wk, wkr)):
                            nc.tensor.matmul(ps[:, 2 + i, :], w[:, :], xn[:, :], start=True, stop=True)
                        for i in range(TILES):
                            last = nc.tensor.matmul(ps[:, 6, 128 * i:128 * i + 128], xn[:, 128 * i:128 * i + 128], wv[:, :], start=True, stop=True)
                        last.then_inc(S["proj"].sem, 1)
                        pe.wait_ge(S["qk"].sem, now.count(S["qk"]))
                        for i in range(TILES):
                            last = nc.tensor.matmul(ps[:, 2 + i, 128 * i:N], qk[:, 1, 128 * i:128 * i + 128], qk[:, 0, 128 * i:N], start=True, stop=True)
                        last.then_inc(S["scores"].sem, 1)
                        pe.wait_ge(S["st"].sem, now.count(S["st"]))
                        pe.wait_ge(S["v_sb"].sem, now.count(S["v_sb"]))
                        for i in range(TILES):
                            last = nc.tensor.matmul(ps[:, 7, 128 * i:N], v[:, 128 * i:128 * i + 128], st[:, i, 128 * i:N],
                                                    start=i == 0, stop=i == TILES - 1, skip_group_check=True)
                        last.then_inc(S["ret"].sem, 1)
                        pe.wait_ge(S["x2"].sem, now.count(S["x2"]))
                        nc.tensor.matmul(ps[:, 0, :], mean_w[:, :], xb[:, :], start=True, stop=True).then_inc(S["mean2"].sem, 1)
                        pe.wait_ge(S["sq2"].sem, now.count(S["sq2"]))
                        nc.tensor.matmul(ps[:, 1, :], mean_w[:, :], sq[:, :], start=True, stop=True).then_inc(S["var2"].sem, 1)

                @block.scalar
                def _(act):
                    with act.Fori(0, B) as b:
                        now = Steps(act, b + 1, USES)
                        act.wait_ge(S["xc"].sem, now.count(S["xc"]))
                        nc.scalar.activation(sq[:, :], xc[:, :], ACT.Square).then_inc(S["sq"].sem, 1)
                        act.wait_ge(S["var"].sem, now.count(S["var"]))
                        nc.scalar.activation(sq[:, :], ps[:, 1, :], ACT.Ln, bias=EPS).then_inc(S["lnv"].sem, 1)
                        act.wait_ge(S["lnv"].sem, now.count(S["lnv"]))
                        nc.scalar.activation(sq[:, :], sq[:, :], ACT.Exp, scale=-0.5).then_inc(S["rstd"].sem, 1)
                        act.wait_ge(S["proj"].sem, now.count(S["proj"]))
                        nc.scalar.activation(v[:, :], ps[:, 6, :], ACT.Copy).then_inc(S["v_sb"].sem, 1)
                        act.wait_ge(S["xc2"].sem, now.count(S["xc2"]))
                        nc.scalar.activation(sq[:, :], xc[:, :], ACT.Square).then_inc(S["sq2"].sem, 1)
                        act.wait_ge(S["var2"].sem, now.count(S["var2"]))
                        nc.scalar.activation(sq[:, :], ps[:, 1, :], ACT.Ln, bias=EPS).then_inc(S["lnv2"].sem, 1)
                        act.wait_ge(S["lnv2"].sem, now.count(S["lnv2"]))
                        nc.scalar.activation(sq[:, :], sq[:, :], ACT.Exp, scale=-0.5).then_inc(S["rstd2"].sem, 1)

                @block.vector
                def _(dve):
                    dve.wait_ge(consts, 16 * 8)
                    for dst, src in ((wqr, wq), (wkr, wk)):
                        nc.vector.tensor_scalar_mul(dst[:, 0:C:2], src[:, 1:C:2], -1.0).then_inc(turned, 1)
                        nc.vector.tensor_copy(dst[:, 1:C:2], src[:, 0:C:2]).then_inc(turned, 1)
                    with dve.Fori(0, B) as b:
                        now = Steps(dve, b + 1, USES)
                        cols = bass.ts(b, N)
                        dve.wait_ge(S["z"].sem, now.count(S["z"], -1))
                        nc.vector.tensor_tensor(xb[:, :], xT[:, cols], zT[:, cols], ALU.add).then_inc(S["x"].sem, 1)
                        dve.wait_ge(S["mean"].sem, now.count(S["mean"]))
                        nc.vector.tensor_tensor(xc[:, :], xb[:, :], ps[:, 0, :], ALU.subtract).then_inc(S["xc"].sem, 1)
                        dve.wait_ge(S["rstd"].sem, now.count(S["rstd"]))
                        nc.vector.tensor_tensor(xn[:, :], xc[:, :], sq[:, :], ALU.mult).then_inc(S["xn"].sem, 1)
                        dve.wait_ge(S["proj"].sem, now.count(S["proj"]))
                        for i, tab in enumerate((qcos, qsin, kcos, ksin)):
                            nc.vector.tensor_tensor(rope[:, i, :], ps[:, 2 + i, :], tab[:, :], ALU.mult).then_inc(S["rope4"].sem, 1)
                        dve.wait_ge(S["rope4"].sem, now.count(S["rope4"]))
                        for i in range(2):
                            nc.vector.tensor_tensor(qk[:, i, :], rope[:, 2 * i, :], rope[:, 2 * i + 1, :], ALU.add).then_inc(S["qk"].sem, 1)
                        dve.wait_ge(S["scores"].sem, now.count(S["scores"]))
                        for i in range(TILES):
                            nc.vector.tensor_tensor(st[:, i, 128 * i:N], ps[:, 2 + i, 128 * i:N], decay[:, 0:N - 128 * i], ALU.mult).then_inc(S["st"].sem, 1)
                        dve.wait_ge(S["ret"].sem, now.count(S["ret"]))
                        nc.vector.tensor_tensor(xb[:, :], xb[:, :], ps[:, 7, :], ALU.add).then_inc(S["x2"].sem, 1)
                        dve.wait_ge(S["mean2"].sem, now.count(S["mean2"]))
                        nc.vector.tensor_tensor(xc[:, :], xb[:, :], ps[:, 0, :], ALU.subtract).then_inc(S["xc2"].sem, 1)
                        nc.vector.tensor_copy(xT[:, cols], xb[:, :]).then_inc(S["xout"].sem, 1)
                        dve.wait_ge(S["rstd2"].sem, now.count(S["rstd2"]))
                        dve.wait_ge(S["xout"].sem, now.count(S["xout"]))
                        nc.vector.tensor_tensor(zT[:, cols], xc[:, :], sq[:, :], ALU.mult).then_inc(S["z"].sem, 1)

        def finish():
            summed, stored = sem("summed"), sem("stored")
            with nc.Block() as block:
                @block.vector
                def _(dve):
                    for b in range(B):
                        cols = slice(N * b, N * b + N)
                        nc.vector.tensor_tensor(xT[:, cols], xT[:, cols], zT[:, cols], ALU.add).then_inc(summed, 1)

                @block.sync
                def _(sp):
                    for b in range(B):
                        cols = slice(N * b, N * b + N)
                        sp.wait_ge(summed, b + 1)
                        sp.dma_start(out[:, cols], xT[:, cols]).then_inc(stored, 16)
                    sp.wait_ge(stored, 16 * B)

        stage_a()
        stage_ffn(0)
        stage_b()
        stage_ffn(1)
        finish()


def constants():
    f = np.float32
    C = 128
    p = np.arange(128)
    t = {}
    t["mean_w"] = np.full((C, C), 1.0 / C, f)
    t["ident"] = np.eye(128, dtype=f)
    t["headmask"] = (p[:, None] // 16 == np.arange(8)[None, :]).astype(f)
    t["blockmask"] = (p[:, None] // 16 == p[None, :] // 16).astype(f)
    t["headsum"] = (p[:, None] // 32 == p[None, :] // 32).astype(f)
    n, dh, win = 512, 64, 32
    half = np.arange(0, dh, 2, dtype=f)
    inv_freq = f(1.0) / (10000.0 ** (half.astype(np.float64) / dh)).astype(f)
    freqs = (np.arange(n, dtype=f)[:, None] * inv_freq[None, :]).astype(f).astype(np.float64)
    base = ((half + f(0.4 * dh)) / f(1.4 * dh)).astype(f)
    power = ((np.arange(n, dtype=f) - f(n // 2)) / f(win // 2)).astype(f)
    scale = base.astype(np.float64)[None, :] ** power.astype(np.float64)[:, None]
    tan, cos = np.tan(freqs), np.cos(freqs)
    four = lambda a: np.tile(a.T, (4, 1))
    t["tan2"] = np.stack([four(-tan), four(tan)], 1).astype(f)
    t["cos2"] = (np.stack([four(8.0 * cos * scale), four(cos / scale)], 1) * 2.0 ** 12).astype(f)
    q, key = p % 32, np.arange(64)
    off = (key[None, :] < q[:, None]) | (key[None, :] > q[:, None] + 32)
    later = np.where(off, f(-1e30), f(0.0)).astype(f)
    first = np.where(off | ((p[:, None] < 32) & (key[None, :] < 32)), f(-1e30), f(0.0)).astype(f)
    t["mask0"] = np.concatenate([np.tile(first, (1, 4)), np.tile(later, (1, 4))], 1)
    t["mask1"] = np.tile(later, (1, 8))
    vec = (np.arange(0, C, 2, dtype=f) + f(0.4 * C)) / f(1.4 * C)
    freq = f(1.0) / (10000.0 ** (np.arange(C // 2, dtype=np.float64) / (C // 2))).astype(f)
    pos = np.arange(n, dtype=f)
    scale = np.repeat(vec.astype(np.float64)[:, None] ** (pos / f(512.0)).astype(np.float64)[None, :], 2, axis=0)
    angle = np.repeat((pos[None, :] * freq[:, None]).astype(f).astype(np.float64), 2, axis=0)
    t["ret_qcos"], t["ret_qsin"] = (np.cos(angle) * scale).astype(f), (np.sin(angle) * scale).astype(f)
    t["ret_kcos"], t["ret_ksin"] = (np.cos(angle) / scale).astype(f), (np.sin(angle) / scale).astype(f)
    gap = np.arange(n)[None, :] - p[:, None]
    t["ret_decay"] = np.where(gap >= 0, 0.96875 ** np.maximum(gap, 0), 0.0).astype(f)
    t["causal"] = (p[:, None] <= p[None, :]).astype(f)
    return t


def kernel(**inputs):
    import concourse.bacc as _bacc
    from concourse import mybir as _mybir
    from concourse.bass_utils import run_bass_kernel_spmd as _run

    nc = _bacc.Bacc("TRN2", target_bir_lowering=False, num_devices=1)
    arrays = {}

    def give(name, a):
        a = np.ascontiguousarray(a)
        arrays[name] = a
        return nc.dram_tensor(name, a.shape, _mybir.dt.from_np(a.dtype), kind="ExternalInput").ap()

    i = {k: np.asarray(v) for k, v in inputs.items()}
    x = give("x", i["L0_attn_a_hidden_states"].reshape(-1, 128).T)
    tabs = {k: give("t_" + k, v) for k, v in constants().items()}
    wa = {"wq": give("wq", i["L0_attn_a_Wq"].T), "wk": give("wk", i["L0_attn_a_Wk"].T), "wv": give("wv", i["L0_attn_a_Wv"].T),
          "wo": give("wo", i["L0_attn_a_Wo"].T), "nw": give("nw", np.tile(i["L0_attn_a_norm_w"][None, :], (128, 1)))}
    wb = {n: give("ret_" + n, i["L0_attn_b_W_" + n[1].upper()]) for n in ("wq", "wk", "wv")}
    wf = {}
    w = i["L0_ffn_Wqkv"].reshape(6, 128, 3, 4, 4, 2, 32)
    qk = w[:, :, 0:2].transpose(0, 1, 3, 2, 5, 4, 6).reshape(6, 128, 4, 4, 128)
    wf["wqkv"] = give("wqkv", np.concatenate([qk, w[:, :, 2].reshape(6, 128, 4, 2, 128)], 3))
    qs, ks = (np.tile(i["L0_ffn_" + n].reshape(6, 1, 2, 32), (1, 4, 1, 1)).transpose(0, 1, 3, 2).reshape(6, 128, 2) for n in ("q_scale", "k_scale"))
    wf["pa"] = give("pa", np.concatenate([qs, ks], 2))
    wf["wout"] = give("wout", i["L0_ffn_Wo"])
    wf["w1"], wf["w2"] = give("w1", i["L0_ffn_W1"]), give("w2", i["L0_ffn_W2"])
    b1 = np.zeros((6, 2, 384), np.float32)
    b1[:, :, :341] = i["L0_ffn_b1"].reshape(6, 2, 341)
    b1 = b1.reshape(6, 2, 3, 128).transpose(0, 3, 1, 2)
    wf["pf"] = give("pf", np.concatenate([np.stack([i["L0_ffn_" + n] for n in ("ln_g", "ln_b", "b2")], 2), b1[:, :, 1], b1[:, :, 0]], 2))
    out = nc.dram_tensor("y", (128, 2048), _mybir.dt.float32, kind="ExternalOutput").ap()
    build_hybrid(nc, x, tabs, wa, wb, wf, out)
    r = _run(nc, [arrays], core_ids=[0])
    return r.results[0]["y"].T.reshape(4, 512, 128)
```

```python
import numpy as np


def build_hybrid(nc, x_in, tabs, wa, wb, wf, out):
    import math
    from contextlib import ExitStack

    import concourse.bass as bass
    from concourse import mybir

    F32, F32R, BF16 = mybir.dt.float32, mybir.dt.float32r, mybir.dt.bfloat16
    ALU, ACT, AX = mybir.AluOpType, mybir.ActivationFunctionType, mybir.AxisListType

    C = 128
    B, N = 4, 512
    TOK = B * N
    DEPTH, HEADS, DH, WIN = 6, 16, 64, 32
    HQ = 4
    QUADS = HEADS // HQ
    TILES = N // 128
    FF = 341
    FFC = [128, 128, FF - 256]
    EPS = 1e-5
    AH, AD = 8, 16
    LN2 = math.log(2.0)

    ctx = ExitStack()
    with ctx:
        def sb(name, shape, dt=F32, scope=ctx):
            return scope.enter_context(nc.sbuf_tensor(name, shape, dt))

        def sem(name, scope=ctx):
            return scope.enter_context(nc.semaphore(name))

        class Signal:

            def __init__(self, name, per=1, count=1, ahead=0):
                self.sem, self.per, self.count, self.ahead = sem(name), per, count, ahead

        class Steps:

            def __init__(self, eng, step, used=((1, 0),)):
                self.eng, self.step = eng, step
                self.known = {} if isinstance(step, int) else {(m, c): eng.snap(step * m + c) for m, c in used}

            def count(self, sig, at=0):
                key = (sig.count * sig.per, (at + 1 + sig.ahead - sig.count) * sig.per)
                if isinstance(self.step, int):
                    assert self.step * key[0] + key[1] > 0
                    return self.step * key[0] + key[1]
                return self.known[key]

        ps = ctx.enter_context(nc.psum_tensor("ps", [128, 8, 512], F32))

        xT = sb("xT", [C, TOK])
        zT = sb("zT", [C, TOK])
        mean_w = sb("mean_w", [C, C])
        split_w = nc.dram_tensor("split_w", (DEPTH * QUADS, 2, C, 6 * 128), F32, kind="Internal").ap()

        loaded = sem("loaded")
        n_loaded = [0]

        def stage_a():
            scope = ExitStack()
            with scope:
                def t(name, shape):
                    return sb("a_" + name, shape, scope=scope)

                wq, wk, wv, wo = (t(n, [C, C]) for n in ("wq", "wk", "wv", "wo"))
                headmask, blockmask = t("headmask", [C, AH]), t("blockmask", [C, C])
                causal, nw, ident = t("causal", [128, 128]), t("nw", [128, AD]), t("ident", [128, 128])
                w_raw, zero = t("w_raw", [C, 2, 6 * 128]), t("zero", [C, 1])
                w_hi, w_lo = (sb("a_" + n, [C, 2, 6 * 128], F32R, scope) for n in ("w_hi", "w_lo"))
                xc, sq, rstd, xn = (t(n, [C, 128]) for n in ("xc", "sq", "rstd", "xn"))
                prj, zc, carry, qz = t("prj", [128, 512]), t("zc", [C, 128]), t("carry", [C, 1]), t("qz", [C, 128])
                kz, st, state, upd = t("kz", [C, AH, 128]), t("st", [128, AH, 128]), t("state", [C, C]), t("upd", [C, C])
                den, o, osq, ss, oT = t("den", [128, AH]), t("o", [128, C]), t("osq", [128, C]), t("ss", [128, AH]), t("oT", [C, 128])

                S = {n: Signal("a_" + n) for n in (
                    "mean", "xc", "sq", "var", "lnv", "rstd", "xn", "prj", "prj_sb", "zc", "carry", "qz", "kz", "s",
                    "st", "o", "den", "den1", "denmax", "rden", "upd", "state", "on", "osq", "ss", "lnr", "rr", "on2", "on3",
                    "oT", "oT_sb", "y", "x", "mean2", "xc2", "sq2", "var2", "lnv2", "rstd2")}
                S["z"] = Signal("a_z", ahead=1)
                raw_in, hi_done, lo_done = ([Signal(f"{n}{j}", per) for j in range(2)] for n, per in (("raw_in", 16), ("hi_done", 1), ("lo_done", 1)))
                split_out = [Signal(f"split_out{j}", 32, ahead=1) for j in range(2)]
                block = scope.enter_context(nc.Block())

                @block.sync
                def _(sp):
                    parts = [(xT[:, :], x_in), (mean_w[:, :], tabs["mean_w"]), (ident[:, :], tabs["ident"]),
                             (wq[:, :], wa["wq"]), (wk[:, :], wa["wk"]), (wv[:, :], wa["wv"]), (wo[:, :], wa["wo"]),
                             (headmask[:, :], tabs["headmask"]), (blockmask[:, :], tabs["blockmask"]),
                             (causal[:, :], tabs["causal"]), (nw[:, :], wa["nw"])]
                    sp.sem_inc(S["z"].sem, 1)
                    for dst, src in parts:
                        sp.dma_start(dst, src).then_inc(loaded, 16)
                    for j in range(2):
                        sp.sem_inc(split_out[j].sem, 32)
                    with sp.Fori(0, DEPTH * QUADS // 2) as n:
                        now = Steps(sp, n + 1, ((1, 0), (16, 0), (32, 0)))
                        for j in range(2):
                            sp.dma_start(w_raw[:, j], wf["wqkv"][bass.ds(n * 2 + j, 1)].rearrange("l c n -> (l c) n")).then_inc(raw_in[j].sem, 16)
                        for j in range(2):
                            sp.wait_ge(lo_done[j].sem, now.count(lo_done[j]))
                            for part, w in enumerate((w_hi, w_lo)):
                                sp.dma_start(split_w[bass.ds(n * 2 + j, 1), part].rearrange("l c n -> (l c) n"), w[:, j].bitcast(F32)).then_inc(split_out[j].sem, 16)
                    for j in range(2):
                        sp.wait_ge(split_out[j].sem, 32 * (DEPTH * QUADS // 2 + 1))

                @block.gpsimd
                def _(pool):
                    cleared = sem("a_cleared", scope)
                    nc.gpsimd.memset(zero[:, :], 0.0).then_inc(cleared, 1)
                    pool.wait_ge(cleared, 1)
                    with pool.Fori(0, DEPTH * QUADS // 2) as n:
                        now = Steps(pool, n + 1, ((1, 0), (16, 0), (32, 0)))
                        for j in range(2):
                            pool.wait_ge(raw_in[j].sem, now.count(raw_in[j]))
                            pool.wait_ge(split_out[j].sem, now.count(split_out[j], -1))
                            nc.gpsimd.tensor_tensor(w_hi[:, j], w_raw[:, j], zero[:, :].broadcast_to([C, 6 * 128]), ALU.add).then_inc(hi_done[j].sem, 1)
                            pool.wait_ge(hi_done[j].sem, now.count(hi_done[j]))
                            nc.gpsimd.tensor_tensor(w_lo[:, j], w_raw[:, j], w_hi[:, j].bitcast(F32), ALU.subtract).then_inc(lo_done[j].sem, 1)

                @block.tensor
                def _(pe):
                    pe.wait_ge(loaded, 16 * 11)
                    with pe.Fori(0, B) as b:
                        with pe.Fori(0, TILES) as i:
                            n = b * TILES + i
                            now = Steps(pe, n + 1)
                            cols = bass.ts(n, 128)
                            nc.tensor.matmul(ps[:, 0, 0:128], mean_w[:, :], xT[:, cols], start=True, stop=True).then_inc(S["mean"].sem, 1)
                            pe.wait_ge(S["sq"].sem, now.count(S["sq"]))
                            nc.tensor.matmul(ps[:, 1, 0:128], mean_w[:, :], sq[:, :], start=True, stop=True).then_inc(S["var"].sem, 1)
                            pe.wait_ge(S["xn"].sem, now.count(S["xn"]))
                            nc.tensor.matmul(ps[:, 2, 0:128], wq[:, :], xn[:, :], start=True, stop=True)
                            nc.tensor.matmul(ps[:, 2, 128:256], wk[:, :], xn[:, :], start=True, stop=True)
                            nc.tensor.matmul(ps[:, 2, 256:384], xn[:, :], wv[:, :], start=True, stop=True)
                            nc.tensor.matmul(ps[:, 2, 384:512], xn[:, :], wk[:, :], start=True, stop=True).then_inc(S["prj"].sem, 1)
                            pe.wait_ge(S["prj_sb"].sem, now.count(S["prj_sb"]))
                            pe.wait_ge(S["kz"].sem, now.count(S["kz"]))
                            for h in range(AH):
                                last = nc.tensor.matmul(ps[:, 3 + h // 4, 128 * (h % 4):128 * (h % 4) + 128], kz[:, h, :], prj[:, 0:128],
                                                        start=True, stop=True)
                            last.then_inc(S["s"].sem, 1)
                            pe.wait_ge(S["qz"].sem, now.count(S["qz"]))
                            nc.tensor.matmul(ps[:, 6, 0:128], prj[:, 384:512], prj[:, 256:384], start=True, stop=True)
                            nc.tensor.matmul(ps[:, 6, 128:128 + AH], qz[:, :], headmask[:, :], start=True, stop=True).then_inc(S["den"].sem, 1)
                            pe.wait_ge(S["st"].sem, now.count(S["st"]))
                            nc.tensor.matmul(ps[:, 5, 0:128], prj[:, 0:128], state[:, :], start=True, stop=False, skip_group_check=True)
                            for h in range(AH):
                                last = nc.tensor.matmul(ps[:, 5, AD * h:AD * h + AD], st[:, h, :], prj[:, 256 + AD * h:256 + AD * h + AD],
                                                        start=False, stop=True, skip_group_check=True)
                            last.then_inc(S["o"].sem, 1)
                            pe.wait_ge(S["on3"].sem, now.count(S["on3"]))
                            nc.tensor.transpose(ps[:, 7, 0:128], o[:, :], ident[:, :]).then_inc(S["oT"].sem, 1)
                            pe.wait_ge(S["oT_sb"].sem, now.count(S["oT_sb"]))
                            nc.tensor.matmul(ps[:, 7, 128:256], wo[:, :], oT[:, :], start=True, stop=True).then_inc(S["y"].sem, 1)
                            pe.wait_ge(S["x"].sem, now.count(S["x"]))
                            nc.tensor.matmul(ps[:, 0, 0:128], mean_w[:, :], xT[:, cols], start=True, stop=True).then_inc(S["mean2"].sem, 1)
                            pe.wait_ge(S["sq2"].sem, now.count(S["sq2"]))
                            nc.tensor.matmul(ps[:, 1, 0:128], mean_w[:, :], sq[:, :], start=True, stop=True).then_inc(S["var2"].sem, 1)

                @block.scalar
                def _(act):
                    act.preload_act_table_set("natural_log_exp_and_others")
                    with act.Fori(0, B * TILES) as n:
                        now = Steps(act, n + 1)
                        act.wait_ge(S["xc"].sem, now.count(S["xc"]))
                        nc.scalar.activation(sq[:, :], xc[:, :], ACT.Square).then_inc(S["sq"].sem, 1)
                        act.wait_ge(S["var"].sem, now.count(S["var"]))
                        nc.scalar.activation(rstd[:, :], ps[:, 1, 0:128], ACT.Ln, bias=EPS).then_inc(S["lnv"].sem, 1)
                        act.wait_ge(S["lnv"].sem, now.count(S["lnv"]))
                        nc.scalar.activation(rstd[:, :], rstd[:, :], ACT.Exp, scale=-0.5).then_inc(S["rstd"].sem, 1)
                        act.wait_ge(S["prj"].sem, now.count(S["prj"]))
                        nc.scalar.activation(prj[:, :], ps[:, 2, :], ACT.Copy).then_inc(S["prj_sb"].sem, 1)
                        act.wait_ge(S["den"].sem, now.count(S["den"]))
                        nc.scalar.activation(den[:, :], ps[:, 6, 128:128 + AH], ACT.Abs).then_inc(S["den1"].sem, 1)
                        act.wait_ge(S["on"].sem, now.count(S["on"]))
                        nc.scalar.activation(osq[:, :], o[:, :], ACT.Square).then_inc(S["osq"].sem, 1)
                        act.wait_ge(S["ss"].sem, now.count(S["ss"]))
                        nc.scalar.activation(ss[:, :], ss[:, :], ACT.Ln, bias=EPS, scale=1.0 / AD).then_inc(S["lnr"].sem, 1)
                        act.wait_ge(S["lnr"].sem, now.count(S["lnr"]))
                        nc.scalar.activation(ss[:, :], ss[:, :], ACT.Exp, scale=-0.5).then_inc(S["rr"].sem, 1)
                        act.wait_ge(S["oT"].sem, now.count(S["oT"]))
                        nc.scalar.activation(oT[:, :], ps[:, 7, 0:128], ACT.Copy).then_inc(S["oT_sb"].sem, 1)
                        act.wait_ge(S["xc2"].sem, now.count(S["xc2"]))
                        nc.scalar.activation(sq[:, :], xc[:, :], ACT.Square).then_inc(S["sq2"].sem, 1)
                        act.wait_ge(S["var2"].sem, now.count(S["var2"]))
                        nc.scalar.activation(rstd[:, :], ps[:, 1, 0:128], ACT.Ln, bias=EPS).then_inc(S["lnv2"].sem, 1)
                        act.wait_ge(S["lnv2"].sem, now.count(S["lnv2"]))
                        nc.scalar.activation(rstd[:, :], rstd[:, :], ACT.Exp, scale=-0.5).then_inc(S["rstd2"].sem, 1)

                @block.vector
                def _(dve):
                    dve.wait_ge(loaded, 16 * 11)
                    reset = sem("a_reset", scope)
                    with dve.Fori(0, B) as b:
                        nc.vector.memset(carry[:, :], 0.0).then_inc(reset, 1)
                        nc.vector.memset(state[:, :], 0.0).then_inc(reset, 1)
                        resets = dve.snap((b + 1) * 2)
                        with dve.Fori(0, TILES) as i:
                            n = b * TILES + i
                            now = Steps(dve, n + 1, ((1, 0), (1, 1)))
                            dve.wait_ge(reset, resets)
                            cols = bass.ts(n, 128)
                            dve.wait_ge(S["z"].sem, now.count(S["z"], -1))
                            dve.wait_ge(S["mean"].sem, now.count(S["mean"]))
                            nc.vector.tensor_tensor(xc[:, :], xT[:, cols], ps[:, 0, 0:128], ALU.subtract).then_inc(S["xc"].sem, 1)
                            dve.wait_ge(S["rstd"].sem, now.count(S["rstd"]))
                            nc.vector.tensor_tensor(xn[:, :], xc[:, :], rstd[:, :], ALU.mult).then_inc(S["xn"].sem, 1)
                            dve.wait_ge(S["prj_sb"].sem, now.count(S["prj_sb"]))
                            nc.vector.tensor_tensor_scan(zc[:, :], prj[:, 128:256], prj[:, 128:256], carry[:, :], ALU.add, ALU.bypass).then_inc(S["zc"].sem, 1)
                            nc.vector.tensor_tensor(kz[:, :, :], prj[:, 128:256].unsqueeze(1).broadcast_to([C, AH, 128]),
                                                    headmask[:, :].unsqueeze(2).broadcast_to([C, AH, 128]), ALU.mult).then_inc(S["kz"].sem, 1)
                            dve.wait_ge(S["zc"].sem, now.count(S["zc"]))
                            nc.vector.tensor_copy(carry[:, :], zc[:, 127:128]).then_inc(S["carry"].sem, 1)
                            nc.vector.tensor_tensor(qz[:, :], prj[:, 0:128], zc[:, :], ALU.mult).then_inc(S["qz"].sem, 1)
                            dve.wait_ge(S["s"].sem, now.count(S["s"]))
                            nc.vector.tensor_tensor(st[:, :, :], ps[:, 3:5, :].rearrange("p a (h q) -> p (a h) q", q=128),
                                                    causal[:, :].unsqueeze(1).broadcast_to([128, AH, 128]), ALU.mult).then_inc(S["st"].sem, 1)
                            dve.wait_ge(S["den1"].sem, now.count(S["den1"]))
                            nc.vector.tensor_scalar_max(den[:, :], den[:, :], 1.0).then_inc(S["denmax"].sem, 1)
                            nc.vector.tensor_tensor(upd[:, :], ps[:, 6, 0:128], blockmask[:, :], ALU.mult).then_inc(S["upd"].sem, 1)
                            dve.wait_ge(S["upd"].sem, now.count(S["upd"]))
                            dve.wait_ge(S["o"].sem, now.count(S["o"]))
                            nc.vector.tensor_tensor(state[:, :], state[:, :], upd[:, :], ALU.add).then_inc(S["state"].sem, 1)
                            dve.wait_ge(S["denmax"].sem, now.count(S["denmax"]))
                            nc.vector.reciprocal(den[:, :], den[:, :]).then_inc(S["rden"].sem, 1)
                            dve.wait_ge(S["rden"].sem, now.count(S["rden"]))
                            nc.vector.tensor_tensor(o[:, :].rearrange("p (h d) -> p h d", d=AD), ps[:, 5, 0:128].rearrange("p (h d) -> p h d", d=AD),
                                                    den[:, :].unsqueeze(2).broadcast_to([128, AH, AD]), ALU.mult).then_inc(S["on"].sem, 1)
                            dve.wait_ge(S["osq"].sem, now.count(S["osq"]))
                            nc.vector.tensor_reduce(ss[:, :], osq[:, :].rearrange("p (h d) -> p h d", d=AD), AX.X, ALU.add).then_inc(S["ss"].sem, 1)
                            dve.wait_ge(S["rr"].sem, now.count(S["rr"]))
                            nc.vector.tensor_tensor(o[:, :].rearrange("p (h d) -> p h d", d=AD), o[:, :].rearrange("p (h d) -> p h d", d=AD),
                                                    ss[:, :].unsqueeze(2).broadcast_to([128, AH, AD]), ALU.mult).then_inc(S["on2"].sem, 1)
                            dve.wait_ge(S["on2"].sem, now.count(S["on2"]))
                            nc.vector.tensor_tensor(o[:, :].rearrange("p (h d) -> p h d", d=AD), o[:, :].rearrange("p (h d) -> p h d", d=AD),
                                                    nw[:, :].unsqueeze(1).broadcast_to([128, AH, AD]), ALU.mult).then_inc(S["on3"].sem, 1)
                            dve.wait_ge(S["y"].sem, now.count(S["y"]))
                            nc.vector.tensor_tensor(xT[:, cols], xT[:, cols], ps[:, 7, 128:256], ALU.add).then_inc(S["x"].sem, 1)
                            dve.wait_ge(S["mean2"].sem, now.count(S["mean2"]))
                            nc.vector.tensor_tensor(xc[:, :], xT[:, cols], ps[:, 0, 0:128], ALU.subtract).then_inc(S["xc2"].sem, 1)
                            dve.wait_ge(S["rstd2"].sem, now.count(S["rstd2"]))
                            dve.wait_ge(S["state"].sem, now.count(S["state"]))
                            dve.wait_ge(S["carry"].sem, now.count(S["carry"]))
                            nc.vector.tensor_tensor(zT[:, cols], xc[:, :], rstd[:, :], ALU.mult).then_inc(S["z"].sem, 1)


        PAD = WIN
        NORM_FLOOR_INV = 1e12
        PRE = 24
        STEPS = DEPTH * B
        NJ = 3
        NO, SS, FB = (3, 4), (5, 6), 7

        def per_quad(name, per=1, ahead=0):
            return Signal(name, per, QUADS, ahead)

        ORDER = ([("qk", 0, i) for i in range(4)] + [("qk", 1, i) for i in range(4)] + [("v", 0, i) for i in range(TILES)]
                 + [("qk", 2, i) for i in range(4)] + [("v", 1, i) for i in range(TILES)] + [("qk", 3, i) for i in range(4)]
                 + [("gate", -1, i) for i in range(3)] + [("val", -1, i) for i in range(3)])
        assert len(ORDER) % NJ == 0
        qk_ready = [per_quad(f"qk_ready{i}") for i in range(4)]
        qk_read = [per_quad(f"qk_read{i}", ahead=1) for i in range(4)]
        v_ready = [Signal(f"v_ready{i}", 1, 2) for i in range(TILES)]
        v_read = [Signal(f"v_read{i}", 1, 2) for i in range(TILES)]
        xs_done = Signal("xs_done", 32, ahead=1)
        x_hi, x_lo = Signal("x_hi", ahead=1), Signal("x_lo", ahead=1)
        sq_done = Signal("sq_done", 1, 4 * QUADS)
        sq_sum, n_ready = per_quad("sq_sum"), per_quad("n_ready", ahead=1)
        n_log, n_inv, u_done, r_done = per_quad("n_log"), per_quad("n_inv"), per_quad("u_done", 2), per_quad("r_done")
        gain, rope_q, rope_k = per_quad("gain"), per_quad("rope_q", ahead=1), per_quad("rope_k", ahead=1)
        k_dma, s_ready = per_quad("k_dma", 16 * HQ), per_quad("s_ready", ahead=2)
        s_max, s_sub, p_exp = per_quad("s_max"), per_quad("s_sub", ahead=1), per_quad("p_exp")
        p_sum, p_inv, p_norm = per_quad("p_sum"), per_quad("p_inv"), per_quad("p_norm")
        p_tr, t_dma = per_quad("p_tr", ahead=2), per_quad("t_dma", 16 * HQ, ahead=2)
        o_ready = [per_quad(f"o_ready{i}", ahead=3) for i in range(2)]
        o_read = [per_quad(f"o_read{i}", ahead=3) for i in range(2)]
        vs_dma = Signal("vs_dma", 32, 2)
        wo_ready, fs_done = Signal("wo_ready"), Signal("fs_done", 2)
        F = {n: Signal("f_" + n) for n in ("x1", "mean", "xc", "sq", "var", "lnv", "rstd", "xn", "xa", "w2")}
        x2 = Signal("x2", 1, 1, 4)
        gate_ready, val_ready = Signal("gate_ready", 1, 3), Signal("val_ready", 1, 3)
        gate_done, val_done = Signal("gate_done", 1, 3), Signal("val_done", 1, 3, ahead=3)
        w_qkv = [Signal(f"w_qkv{g}", 48) for g in range(QUADS)]
        w_out, w_ff = Signal("w_out", 16), Signal("w_ff", 64)
        GRANTED = [xs_done, x_hi, x_lo, *qk_read, n_ready, rope_q, rope_k, s_ready, s_sub, p_tr, t_dma, *o_ready, *o_read, x2, val_done]

        SP_USES = [(1, -1), (1, 1), (1, 3), (2, -1), (2, 0), *((4, c) for c in range(-3, 2))]
        PE_USES = [(1, -1), (1, 0), (1, 2), *((2, c) for c in range(-2, 1)), (3, -5), (3, -4), (3, -3), (3, 0), *((4, c) for c in range(-4, 2)),
                   (64, -64), (64, -32), *((256, 64 * c) for c in range(-4, 1))]
        ACT_USES = [(1, -1), (32, 32), (2, -1), (2, 0), (3, -5), (3, -4), (3, -3), *((4, c) for c in range(-3, 2))]
        POOL_USES = [*((4, c) for c in range(-4, 1)), *((16, c) for c in range(-12, 1, 4))]
        DVE_USES = [(1, -1), (1, 1), (3, -5), (3, -4), (3, -3), *((4, c) for c in range(-4, 2)), *((8, c) for c in range(-6, 1, 2)),
                    *((256, 64 * c) for c in range(-4, 1))]

        def stage_ffn(phase):
            scope = ExitStack()
            with scope:
                def t(name, shape, dt=F32):
                    return sb(f"f{phase}_" + name, shape, dt, scope=scope)

                wh, wl = t("wh", [C, QUADS, 6, 128], F32R), t("wl", [C, QUADS, 6, 128], F32R)
                wout = t("wout", [128, 8, C])
                w1, w2 = t("w1", [C, 2 * FF]), t("w2", [128, 3, C])
                pa, pf = t("pa", [128, QUADS, 4]), t("pf", [128, 9])
                tan2, cos2 = t("tan2", [128, 2, N]), t("cos2", [128, 2, N])
                mask, ones = t("mask", [128, 768], BF16), t("ones", [128, 128])
                identb = t("identb", [128, 128], BF16)
                xs, xh, x1 = t("xs", [C, N]), t("xh", [C, N], F32R), t("x1", [C, N])
                xl = xs[:, :].bitcast(F32R)
                sq, ab, rn, u = t("sq", [128, 4, N]), t("ab", [128, 2, 4, N]), t("rn", [128, 2, N]), t("u", [128, 4, N])
                kb = t("kb", [128, 2, HQ, PAD + N])
                p, pt = t("p", [128, 1024]), t("pt", [128, 1024])
                tb = t("tb", [128, HQ, 1024])
                v, vs = t("v", [128, TILES, 1024]), t("vs", [128, TILES, 1024])
                ot = t("ot", [128, 8, N])
                mx, rs = t("mx", [128, 16]), t("rs", [128, 16])
                fs, fc, fq, hid = t("fs", [C, N]), t("fc", [C, N]), t("fq", [C, N]), t("hid", [128, 3, N])
                consts, zeroed = sem(f"f{phase}_consts", scope), sem(f"f{phase}_zeroed", scope)
                masked, xs_first = sem(f"f{phase}_masked", scope), sem(f"f{phase}_xs_first", scope)
                split_first = sem(f"f{phase}_split_first", scope)
                N_CONST, N_ZERO, N_MASKED = 6 * 16, 5, 2
                block = scope.enter_context(nc.Block())

                L0, FIRST = phase * DEPTH, phase * STEPS

                def bank(*which):
                    return ps[:, ORDER.index(which) % NJ, :]

                def window(tile, i):
                    return 128 * tile + WIN * i

                def steps_of(eng, step):
                    step(FIRST, False, True)
                    with eng.Fori(FIRST + 1, FIRST + STEPS) as s:
                        step(s, True, True)
                    step(FIRST + STEPS, True, False)

                @block.sync
                def _(sp):
                    if phase == 0:
                        for s in GRANTED:
                            sp.sem_inc(s.sem, s.ahead * s.per)

                    def load_qkv(at):
                        for g in range(QUADS):
                            for part, w in enumerate((wh, wl)):
                                sp.dma_start(w[:, g].bitcast(F32), split_w[bass.ds(at * QUADS + g, 1), part].rearrange("l c (q n) -> (l c) q n", q=6)).then_inc(w_qkv[g].sem, 16)
                            sp.dma_start(pa[:, g], wf["pa"][bass.ds(at, 1)].rearrange("l c n -> (l c) n")).then_inc(w_qkv[g].sem, 16)

                    def load_out(at):
                        sp.dma_start(wout[:, :, :], wf["wout"][bass.ds(at, 1)].rearrange("l (k p) n -> p (l k) n", p=128)).then_inc(w_out.sem, 16)

                    def load_ff(at):
                        sp.dma_start(w1[:, :], wf["w1"][bass.ds(at, 1)].rearrange("l c n -> (l c) n")).then_inc(w_ff.sem, 16)
                        sp.dma_start(w2[:, 0:2, :], wf["w2"][bass.ds(at, 1), 0:256].rearrange("l (k p) n -> p (l k) n", p=128)).then_inc(w_ff.sem, 16)
                        sp.dma_start(w2[0:FFC[2], 2, :], wf["w2"][bass.ds(at, 1), 256:FF].rearrange("l p n -> (l p) n")).then_inc(w_ff.sem, 16)
                        sp.dma_start(pf[:, :], wf["pf"][bass.ds(at, 1)].rearrange("l c n -> (l c) n")).then_inc(w_ff.sem, 16)

                    sp.wait_ge(zeroed, N_ZERO)
                    sp.dma_start(xs[0:64, :], zT[0:64, 0:N]).then_inc(xs_first, 16)
                    sp.dma_start(xs[64:128, 1:N], zT[64:128, 0:N - 1]).then_inc(xs_first, 16)
                    load_qkv(0)
                    for dst, src in ((ones[:, :], tabs["headsum"]), (tan2[:, :, :], tabs["tan2"]), (cos2[:, :, :], tabs["cos2"]),
                                     (hid[:, 0:2, 0:384], tabs["mask"].rearrange("p (a n) -> p a n", a=2)), (fc[:, 0:128], tabs["ident"]),
                                     (mean_w[:, :], tabs["mean_w"])):
                        sp.dma_start(dst, src).then_inc(consts, 16)
                    load_out(0)
                    load_ff(0)

                    def step(s, prev, cur, new_layer=None):
                        now = Steps(sp, s + 1, SP_USES)
                        if new_layer is not None:
                            sp.wait_ge(qk_read[3].sem, now.count(qk_read[3], -1))
                            load_qkv(new_layer)
                        next_col = N if not prev else sp.snap((s + 1) % B * N)
                        for k in range(QUADS):
                            if k in (1, 2) and cur:
                                i = k - 1
                                for tile in range(TILES):
                                    sp.wait_ge(v_read[tile].sem, now.count(v_read[tile], i))
                                half = slice(512 * i, 512 * i + 512)
                                sp.dma_start(vs[WIN:128, :, half], v[0:128 - WIN, :, half]).then_inc(vs_dma.sem, 16)
                                sp.dma_start(vs[0:WIN, 1:TILES, half], v[128 - WIN:128, 0:TILES - 1, half]).then_inc(vs_dma.sem, 16)
                            if k == 3 and cur:
                                sp.wait_ge(x2.sem, now.count(x2, -3))
                                sp.wait_ge(qk_ready[3].sem, now.count(qk_ready[3], 3))
                                sp.dma_start(xs[0:64, :], zT[0:64, bass.ds(next_col, N)]).then_inc(xs_done.sem, 16)
                                sp.dma_start(xs[64:128, 1:N], zT[64:128, bass.ds(next_col, N - 1)]).then_inc(xs_done.sem, 16)
                            if k == 3 and new_layer is not None:
                                sp.wait_ge(wo_ready.sem, now.count(wo_ready, -1))
                                load_out(new_layer)
                            if cur:
                                sp.wait_ge(s_ready.sem, now.count(s_ready, k - 1))
                                sp.wait_ge(rope_k.sem, now.count(rope_k, k))
                                for h in range(HQ):
                                    rows = slice(32 * h, 32 * h + 32)
                                    sp.dma_start(kb[rows, :, h, PAD:], ab[rows, k % 2, 2:4, :]).then_inc(k_dma.sem, 16)
                            if cur if k else prev:
                                g = k - 1
                                sp.wait_ge(o_ready[1].sem, now.count(o_ready[1], g - 1))
                                sp.wait_ge(p_tr.sem, now.count(p_tr, g))
                                for w in range(4):
                                    rows = slice(32 * w, 32 * w + 32)
                                    sp.dma_start(tb[rows, w, :], pt[rows, :]).then_inc(t_dma.sem, 16)
                        if new_layer is not None:
                            sp.wait_ge(x2.sem, now.count(x2, -1))
                            load_ff(new_layer)

                    def later_sequences(first):
                        with sp.Fori(1, B) as b:
                            step(first + b, True, True)

                    step(FIRST, False, True)
                    with sp.Fori(1, DEPTH) as at:
                        later_sequences(FIRST - B + at * B)
                        step(FIRST + at * B, True, True, new_layer=at)
                    later_sequences(FIRST + STEPS - B)
                    step(FIRST + STEPS, True, False)

                @block.tensor
                def _(pe):
                    def step(s, prev, cur):
                        now = Steps(pe, s + 1, PE_USES)
                        layer = Steps(pe, (s >> 2) + 1, ((48, 0),))
                        before = Steps(pe, ((s - 1) >> 2) + 1, ((16, 0), (64, 0)))

                        def bank_free(*which):
                            n = ORDER.index(which) - NJ
                            while not (prev if ORDER[n][1] < 0 else cur) and n >= 0:
                                n -= NJ
                            if n < 0 and not prev:
                                return
                            kind, g, i = ORDER[n]
                            at = 0 if n >= 0 else -1
                            if kind == "qk":
                                pe.wait_ge(qk_read[i].sem, now.count(qk_read[i], g + QUADS * at))
                            elif kind == "v":
                                pe.wait_ge(v_read[i].sem, now.count(v_read[i], g + 2 * at))
                            elif kind == "gate":
                                pe.wait_ge(gate_done.sem, now.count(gate_done, i + 3 * (at - 1)))
                            else:
                                pe.wait_ge(val_done.sem, now.count(val_done, i + 3 * (at - 1)))

                        def project(g):
                            pe.wait_ge(w_qkv[g].sem, layer.count(w_qkv[g]))
                            for i in range(4):
                                bank_free("qk", g, i)
                                nc.tensor.matmul(bank("qk", g, i), wh[:, g, i, :], xh[:, :], start=True, stop=False)
                                nc.tensor.matmul(bank("qk", g, i), wh[:, g, i, :], xl, start=False, stop=False)
                                nc.tensor.matmul(bank("qk", g, i), wl[:, g, i, :], xh[:, :], start=False, stop=True).then_inc(qk_ready[i].sem, 1)

                        def project_v(i):
                            pe.wait_ge(w_qkv[2 * i + 1].sem, layer.count(w_qkv[2 * i + 1]))
                            for tile in range(TILES):
                                bank_free("v", i, tile)
                                cols, pair = slice(128 * tile, 128 * tile + 128), slice(2 * i, 2 * i + 2)
                                nc.tensor.matmul(bank("v", i, tile), xh[:, cols], wh[:, pair, 4:6, :], start=True, stop=False)
                                nc.tensor.matmul(bank("v", i, tile), xh[:, cols], wl[:, pair, 4:6, :], start=False, stop=False)
                                nc.tensor.matmul(bank("v", i, tile), xl[:, cols], wh[:, pair, 4:6, :], start=False, stop=True).then_inc(v_ready[tile].sem, 1)

                        def norms(g):
                            pe.wait_ge(sq_sum.sem, now.count(sq_sum, g))
                            for i in range(2):
                                pe.wait_ge(o_read[i].sem, now.count(o_read[i], g - 3))
                            for i in range(2):
                                last = nc.tensor.matmul(ps[:, NO[i], :], ones[:, :], sq[:, 2 * i, :], start=True, stop=True)
                            last.then_inc(n_ready.sem, 1)

                        def scores(g):
                            pe.wait_ge(s_sub.sem, now.count(s_sub, g - 1))
                            for j in range(2):
                                last = nc.tensor.matmul(ps[:, SS[j], :], identb[:, :], mask[:, 256 * j:256 * j + 512], start=True, stop=False, skip_group_check=True)
                            pe.wait_ge(rope_q.sem, now.count(rope_q, g))
                            pe.wait_ge(k_dma.sem, now.count(k_dma, g))
                            for tile in range(TILES):
                                for i in range(4):
                                    w0 = window(tile, i)
                                    rows = slice(32 * i, 32 * i + 32)
                                    for a in range(2):
                                        last = nc.tensor.matmul(ps[rows, SS[tile // 2], 256 * (tile % 2):256 * (tile % 2) + 256],
                                                                ab[:, g % 2, a, w0:w0 + WIN], kb[:, a, :, w0:w0 + 2 * WIN],
                                                                start=False, stop=a == 1, skip_group_check=True, tile_position=(0, 32 * i))
                            last.then_inc(s_ready.sem, 1)

                        def values(g):
                            at = g + 2 if cur else -1
                            pe.wait_ge(n_log.sem, now.count(n_log, at))
                            if not cur and g == -1:
                                for i in range(2):
                                    pe.wait_ge(o_read[i].sem, now.count(o_read[i], g - 1))
                            pe.wait_ge(vs_dma.sem, now.count(vs_dma, g // 2))
                            pe.wait_ge(t_dma.sem, now.count(t_dma, g))
                            for pair in range(2):
                                for tile in range(TILES):
                                    for h in (2 * pair, 2 * pair + 1):
                                        rows = slice(64 * (h % 2), 64 * (h % 2) + 64)
                                        for blk, val in ((0, vs), (1, v)):
                                            c0 = ((tile * HQ + h) * 2 + blk) * WIN
                                            d0 = 256 * (g % QUADS) + 64 * h
                                            last = nc.tensor.matmul(ps[rows, NO[pair], 128 * tile:128 * tile + 128],
                                                                    val[:, tile, d0:d0 + 64], tb[:, :, c0:c0 + WIN],
                                                                    start=blk == 0, stop=blk == 1, tile_position=(0, 64 * (h % 2)))
                                last.then_inc(o_ready[pair].sem, 1)

                        f = ps[:, FB, :]

                        def project_out(g):
                            if g == 0:
                                pe.wait_ge(x2.sem, now.count(x2, -2))
                                pe.wait_ge(w_out.sem, before.count(w_out))
                            for i in range(2):
                                pe.wait_ge(o_read[i].sem, now.count(o_read[i], g - QUADS))
                                last = nc.tensor.matmul(f, wout[:, 2 * g + i, :], ot[:, 2 * g + i, :], start=g + i == 0, stop=g + i == QUADS)
                            if g == QUADS - 1:
                                last.then_inc(wo_ready.sem, 1)

                        def hidden(kind, first, ready):
                            for j in range(3):
                                m = FFC[j]
                                bank_free(kind, -1, j)
                                nc.tensor.matmul(bank(kind, -1, j)[0:m], w1[:, first + 128 * j:first + 128 * j + m], fq[:, :],
                                                 start=True, stop=True).then_inc(ready.sem, 1)

                        if cur:
                            if not prev:
                                pe.wait_ge(split_first, 2)
                            pe.wait_ge(x_hi.sem, now.count(x_hi, -1))
                            pe.wait_ge(x_lo.sem, now.count(x_lo, -1))
                            project(0)
                        if prev:
                            scores(-1)
                        if cur:
                            norms(0)
                        if prev:
                            project_out(0)
                            project_out(1)
                            values(-2)
                        if cur:
                            project(1)
                            scores(0)
                            project_v(0)
                            norms(1)
                        if prev:
                            project_out(2)
                            values(-1)
                        if cur:
                            project(2)
                        if prev:
                            project_out(3)
                        if cur:
                            scores(1)
                        if prev:
                            pe.wait_ge(fs_done.sem, now.count(fs_done, -1))
                            nc.tensor.matmul(f, mean_w[:, :], fs[:, :], start=True, stop=True).then_inc(F["mean"].sem, 1)
                        if cur:
                            project_v(1)
                            norms(2)
                        if prev:
                            pe.wait_ge(F["sq"].sem, now.count(F["sq"], -1))
                            nc.tensor.matmul(f, mean_w[:, :], fq[:, :], start=True, stop=True).then_inc(F["var"].sem, 1)
                        if cur:
                            values(0)
                        if cur:
                            project(3)
                        if prev:
                            pe.wait_ge(w_ff.sem, before.count(w_ff))
                            pe.wait_ge(F["xa"].sem, now.count(F["xa"], -1))
                            hidden("gate", FF, gate_ready)
                        if cur:
                            scores(2)
                            norms(3)
                        if prev:
                            hidden("val", 0, val_ready)
                        if cur:
                            values(1)
                        if prev:
                            pe.wait_ge(val_done.sem, now.count(val_done, 2 - 3))
                            for j in range(3):
                                m = FFC[j]
                                last = nc.tensor.matmul(f, w2[0:m, j, :], hid[0:m, j, :], start=j == 0, stop=j == 2)
                            last.then_inc(F["w2"].sem, 1)
                        else:
                            for i in range(1, 4):
                                pe.wait_ge(qk_read[i].sem, now.count(qk_read[i], 3))

                    pe.wait_ge(masked, N_MASKED)
                    pe.wait_ge(consts, N_CONST)
                    steps_of(pe, step)

                @block.scalar
                def _(act):
                    def step(s, prev, cur):
                        now = Steps(act, s + 1, ACT_USES)

                        def evacuate(g):
                            act.wait_ge(n_ready.sem, now.count(n_ready, g - 1))
                            act.wait_ge(s_ready.sem, now.count(s_ready, g - 2))
                            for i in range(4):
                                act.wait_ge(qk_ready[i].sem, now.count(qk_ready[i], g))
                                nc.scalar.activation(sq[:, i, :], bank("qk", g, i), ACT.Square).then_inc(sq_done.sem, 1)
                                nc.scalar.activation(ab[:, g % 2, i, :], bank("qk", g, i), ACT.Identity, scale=pa[:, g, i:i + 1]).then_inc(qk_read[i].sem, 1)

                        def evacuate_v(i):
                            act.wait_ge(o_ready[1].sem, now.count(o_ready[1], 2 * i + 1 - QUADS))
                            for tile in range(TILES):
                                act.wait_ge(v_ready[tile].sem, now.count(v_ready[tile], i))
                                nc.scalar.activation(v[:, tile, 512 * i:512 * i + 512], bank("v", i, tile), ACT.Copy).then_inc(v_read[tile].sem, 1)

                        def inverse_norms(g):
                            act.wait_ge(rope_q.sem, now.count(rope_q, g - 1))
                            act.wait_ge(rope_k.sem, now.count(rope_k, g - 1))
                            act.wait_ge(n_ready.sem, now.count(n_ready, g))
                            nc.scalar.activation(rn[:, :, :], ps[:, 3:5, :], ACT.Ln, scale=2.0 ** PRE).then_inc(n_log.sem, 1)
                            act.wait_ge(n_log.sem, now.count(n_log, g))
                            nc.scalar.activation(rn[:, :, :], rn[:, :, :], ACT.Exp, scale=-0.5).then_inc(n_inv.sem, 1)

                        def exponentials(g):
                            act.wait_ge(s_sub.sem, now.count(s_sub, g))
                            nc.scalar.activation(p[:, :], p[:, :], ACT.Exp).then_inc(p_exp.sem, 1)

                        def evacuate_out(g):
                            for pair in range(2):
                                act.wait_ge(o_ready[pair].sem, now.count(o_ready[pair], g))
                                nc.scalar.activation(ot[:, 2 * (g % QUADS) + pair, :], ps[:, NO[pair], :], ACT.Copy).then_inc(o_read[pair].sem, 1)

                        if cur:
                            evacuate(0)
                            inverse_norms(0)
                        if prev:
                            exponentials(-1)
                            evacuate_out(-2)
                        if cur:
                            evacuate(1)
                            evacuate_v(0)
                            inverse_norms(1)
                            exponentials(0)
                        if prev:
                            evacuate_out(-1)
                        if cur:
                            evacuate(2)
                        if prev:
                            act.wait_ge(F["x1"].sem, now.count(F["x1"], -1))
                            nc.scalar.activation(fs[0:64, :], x1[0:64, :], ACT.Copy).then_inc(fs_done.sem, 1)
                            nc.scalar.activation(fs[64:128, 1:N], x1[64:128, 0:N - 1], ACT.Copy).then_inc(fs_done.sem, 1)
                            act.wait_ge(F["xc"].sem, now.count(F["xc"], -1))
                            nc.scalar.activation(fq[:, :], fc[:, :], ACT.Square).then_inc(F["sq"].sem, 1)
                        if cur:
                            evacuate_v(1)
                            inverse_norms(2)
                        if prev:
                            act.wait_ge(F["var"].sem, now.count(F["var"], -1))
                            nc.scalar.activation(fq[:, :], ps[:, FB, :], ACT.Ln, bias=EPS).then_inc(F["lnv"].sem, 1)
                            act.wait_ge(F["lnv"].sem, now.count(F["lnv"], -1))
                            nc.scalar.activation(fq[:, :], fq[:, :], ACT.Exp, scale=-0.5).then_inc(F["rstd"].sem, 1)
                            act.wait_ge(F["xn"].sem, now.count(F["xn"], -1))
                            nc.scalar.activation(fq[:, :], fc[:, :], ACT.Identity, bias=pf[:, 1:2], scale=pf[:, 0:1]).then_inc(F["xa"].sem, 1)
                        if cur:
                            exponentials(1)
                            evacuate_out(0)
                        if cur:
                            evacuate(3)
                        if prev:
                            for j in range(3):
                                m = FFC[j]
                                act.wait_ge(gate_ready.sem, now.count(gate_ready, j - 3))
                                nc.scalar.activation(hid[0:m, j, :], bank("gate", -1, j)[0:m], ACT.Gelu, bias=pf[0:m, 3 + j:4 + j]).then_inc(gate_done.sem, 1)
                            act.preload_act_table_set("natural_log_exp_and_others")
                        if cur:
                            inverse_norms(3)
                            act.wait_ge(xs_done.sem, now.count(xs_done))
                            nc.scalar.activation(xh[:, :], xs[:, :], ACT.Copy).then_inc(x_hi.sem, 1)
                            exponentials(2)
                            evacuate_out(1)

                    act.preload_act_table_set("natural_log_exp_and_others")
                    act.wait_ge(masked, N_MASKED)
                    act.wait_ge(zeroed, N_ZERO)
                    act.wait_ge(xs_first, 32)
                    nc.scalar.activation(xh[:, :], xs[:, :], ACT.Copy).then_inc(split_first, 1)
                    steps_of(act, step)

                @block.gpsimd
                def _(pool):
                    def step(s, prev, cur):
                        now = Steps(pool, s + 1, POOL_USES)
                        for k in range(QUADS):
                            if cur:
                                pool.wait_ge(sq_done.sem, now.count(sq_done, 4 * k + 3))
                                nc.gpsimd.tensor_tensor(sq[:, 0:3:2, :], sq[:, 0:3:2, :], sq[:, 1:4:2, :], ALU.add).then_inc(sq_sum.sem, 1)
                                pool.wait_ge(r_done.sem, now.count(r_done, k))
                                pool.wait_ge(gain.sem, now.count(gain, k))
                                nc.gpsimd.tensor_tensor(ab[:, k % 2, 0:2, :], u[:, 0:2, :], rn[:, 0:1, :].broadcast_to([128, 2, N]), ALU.mult).then_inc(rope_q.sem, 1)
                            if cur if k else prev:
                                g = k - 1
                                pool.wait_ge(p_inv.sem, now.count(p_inv, g))
                                prow = p[:, :].rearrange("p (n k) -> p n k", k=64)
                                nc.gpsimd.tensor_tensor(prow, prow, rs[:, :].unsqueeze(2).broadcast_to([128, 16, 64]), ALU.mult).then_inc(p_norm.sem, 1)

                    nc.gpsimd.memset(kb[:, :, :, :], 0.0).then_inc(zeroed, 1)
                    nc.gpsimd.memset(vs[0:WIN, 0, :], 0.0).then_inc(zeroed, 1)
                    steps_of(pool, step)

                @block.vector
                def _(dve):
                    def step(s, prev, cur):
                        now = Steps(dve, s + 1, DVE_USES)
                        cols = slice(N * ((s - 1) % B), N * ((s - 1) % B) + N) if not (prev and cur) else bass.ds(((s - 1) & (B - 1)) * N, N)
                        f = ps[:, FB, :]
                        for k in range(QUADS):
                            if k == 2 and prev:
                                dve.wait_ge(wo_ready.sem, now.count(wo_ready, -1))
                                nc.vector.tensor_tensor(x1[:, :], zT[:, cols], f, ALU.add).then_inc(F["x1"].sem, 1)
                            if cur:
                                for i in range(4):
                                    dve.wait_ge(qk_read[i].sem, now.count(qk_read[i], k))
                                dve.wait_ge(rope_q.sem, now.count(rope_q, k - 1))
                                dve.wait_ge(rope_k.sem, now.count(rope_k, k - 1))
                                for a in range(2):
                                    nc.vector.tensor_tensor(u[:, a:4:2, :], ab[:, k % 2, 1 - a:4:2, :], tan2[:, a:a + 1, :].broadcast_to([128, 2, N]),
                                                            ALU.mult).then_inc(u_done.sem, 1)
                                dve.wait_ge(u_done.sem, now.count(u_done, k))
                                nc.vector.tensor_tensor(u[:, :, :], u[:, :, :], ab[:, k % 2, :, :], ALU.add).then_inc(r_done.sem, 1)
                            if k == 2 and prev:
                                dve.wait_ge(F["mean"].sem, now.count(F["mean"], -1))
                                nc.vector.tensor_tensor(fc[:, :], fs[:, :], f, ALU.subtract).then_inc(F["xc"].sem, 1)
                            softmax = cur if k else prev
                            g = k - 1
                            prow = p[:, :].rearrange("p (n k) -> p n k", k=64)
                            if softmax:
                                srow = ps[:, 5:7, :].rearrange("p a (n k) -> p (a n) k", k=64)
                                dve.wait_ge(s_ready.sem, now.count(s_ready, g))
                                nc.vector.tensor_reduce(mx[:, :], srow, AX.X, ALU.max).then_inc(s_max.sem, 1)
                                dve.wait_ge(s_max.sem, now.count(s_max, g))
                                dve.wait_ge(p_tr.sem, now.count(p_tr, g - 1))
                                nc.vector.tensor_tensor(prow, srow, mx[:, :].unsqueeze(2).broadcast_to([128, 16, 64]), ALU.subtract).then_inc(s_sub.sem, 1)
                            if k == 3 and prev:
                                for j in range(3):
                                    m = FFC[j]
                                    dve.wait_ge(gate_done.sem, now.count(gate_done, j - 3))
                                    dve.wait_ge(val_ready.sem, now.count(val_ready, j - 3))
                                    nc.vector.scalar_tensor_tensor(out=hid[0:m, j, :], in0=bank("val", -1, j)[0:m], scalar=pf[0:m, 6 + j:7 + j],
                                                                   in1=hid[0:m, j, :], op0=ALU.add, op1=ALU.mult).then_inc(val_done.sem, 1)
                            if cur:
                                dve.wait_ge(n_inv.sem, now.count(n_inv, k))
                                nc.vector.scalar_tensor_tensor(out=rn[:, :, :], in0=rn[:, :, :], scalar=NORM_FLOOR_INV / 2 ** (PRE // 2), in1=cos2[:, :, :],
                                                               op0=ALU.min, op1=ALU.mult).then_inc(gain.sem, 1)
                                dve.wait_ge(gain.sem, now.count(gain, k))
                                dve.wait_ge(r_done.sem, now.count(r_done, k))
                                nc.vector.tensor_tensor(ab[:, k % 2, 2:4, :], u[:, 2:4, :], rn[:, 1:2, :].broadcast_to([128, 2, N]), ALU.mult).then_inc(rope_k.sem, 1)
                            if k == 2 and prev:
                                dve.wait_ge(F["rstd"].sem, now.count(F["rstd"], -1))
                                nc.vector.tensor_tensor(fc[:, :], fc[:, :], fq[:, :], ALU.mult).then_inc(F["xn"].sem, 1)
                            if k == 3 and cur:
                                dve.wait_ge(x_hi.sem, now.count(x_hi))
                                nc.vector.tensor_tensor(xl, xs[:, :], xh[:, :].bitcast(F32), ALU.subtract).then_inc(x_lo.sem, 1)
                            if softmax:
                                dve.wait_ge(p_exp.sem, now.count(p_exp, g))
                                nc.vector.tensor_reduce(rs[:, :], prow, AX.X, ALU.add).then_inc(p_sum.sem, 1)
                                dve.wait_ge(p_sum.sem, now.count(p_sum, g))
                                nc.vector.reciprocal(rs[:, :], rs[:, :]).then_inc(p_inv.sem, 1)
                            if softmax:
                                dve.wait_ge(p_norm.sem, now.count(p_norm, g))
                                dve.wait_ge(t_dma.sem, now.count(t_dma, g - 1))
                                nc.vector.transpose(pt[:, :], p[:, :]).then_inc(p_tr.sem, 1)
                        if prev:
                            dve.wait_ge(F["w2"].sem, now.count(F["w2"], -1))
                            nc.vector.scalar_tensor_tensor(out=zT[:, cols], in0=f, scalar=pf[:, 2:3], in1=x1[:, :], op0=ALU.add, op1=ALU.add).then_inc(x2.sem, 1)

                    nc.vector.memset(xs[64:128, 0:1], 0.0).then_inc(zeroed, 1)
                    nc.vector.memset(fs[64:128, 0:1], 0.0).then_inc(zeroed, 1)
                    nc.vector.memset(tb[:, :, :], 0.0).then_inc(zeroed, 1)
                    dve.wait_ge(consts, N_CONST)
                    nc.vector.tensor_copy(mask[:, :].rearrange("p (a n) -> p a n", a=2), hid[:, 0:2, 0:384]).then_inc(masked, 1)
                    nc.vector.tensor_copy(identb[:, :], fc[:, 0:128]).then_inc(masked, 1)
                    dve.wait_ge(masked, N_MASKED)
                    dve.wait_ge(zeroed, N_ZERO)
                    dve.wait_ge(split_first, 1)
                    nc.vector.tensor_tensor(xl, xs[:, :], xh[:, :].bitcast(F32), ALU.subtract).then_inc(split_first, 1)
                    steps_of(dve, step)

        def stage_b():
            scope = ExitStack()
            with scope:
                def t(name, shape):
                    return sb("b_" + name, shape, scope=scope)

                wq, wk, wv = (t(n, [C, C]) for n in ("wq", "wk", "wv"))
                wqr, wkr = t("wqr", [C, C]), t("wkr", [C, C])
                qcos, qsin, kcos, ksin, decay = (t(n, [128, N]) for n in ("qcos", "qsin", "kcos", "ksin", "decay"))
                xb, xc, sq, xn = (t(n, [C, N]) for n in ("xb", "xc", "sq", "xn"))
                rope, qk = t("rope", [C, 4, N]), t("qk", [C, 2, N])
                v, st = t("v", [128, N]), t("st", [128, TILES, N])
                names = ("x", "mean", "xc", "sq", "var", "lnv", "rstd", "xn", "proj", "v_sb", "rope4", "qk", "scores", "st", "ret",
                         "x2", "xout", "mean2", "xc2", "sq2", "var2", "lnv2", "rstd2")
                S = {n: Signal("b_" + n) for n in names}
                S["rope4"].per, S["st"].per, S["qk"].per = 4, TILES, 2
                S["z"] = Signal("b_z", ahead=1)
                consts, turned = sem("b_consts", scope), sem("b_turned", scope)
                USES = [(1, 0), (1, 1), (2, 0), (4, 0)]
                block = scope.enter_context(nc.Block())

                @block.sync
                def _(sp):
                    sp.sem_inc(S["z"].sem, 1)
                    for dst, src in ((wq, wb["wq"]), (wk, wb["wk"]), (wv, wb["wv"]), (qcos, tabs["ret_qcos"]), (qsin, tabs["ret_qsin"]),
                                     (kcos, tabs["ret_kcos"]), (ksin, tabs["ret_ksin"]), (decay, tabs["ret_decay"])):
                        sp.dma_start(dst[:, :], src).then_inc(consts, 16)

                @block.tensor
                def _(pe):
                    pe.wait_ge(turned, 4)
                    with pe.Fori(0, B) as b:
                        now = Steps(pe, b + 1, USES)
                        pe.wait_ge(S["x"].sem, now.count(S["x"]))
                        nc.tensor.matmul(ps[:, 0, :], mean_w[:, :], xb[:, :], start=True, stop=True).then_inc(S["mean"].sem, 1)
                        pe.wait_ge(S["sq"].sem, now.count(S["sq"]))
                        nc.tensor.matmul(ps[:, 1, :], mean_w[:, :], sq[:, :], start=True, stop=True).then_inc(S["var"].sem, 1)
                        pe.wait_ge(S["xn"].sem, now.count(S["xn"]))
                        for i, w in enumerate((wq, wqr, wk, wkr)):
                            nc.tensor.matmul(ps[:, 2 + i, :], w[:, :], xn[:, :], start=True, stop=True)
                        for i in range(TILES):
                            last = nc.tensor.matmul(ps[:, 6, 128 * i:128 * i + 128], xn[:, 128 * i:128 * i + 128], wv[:, :], start=True, stop=True)
                        last.then_inc(S["proj"].sem, 1)
                        pe.wait_ge(S["qk"].sem, now.count(S["qk"]))
                        for i in range(TILES):
                            last = nc.tensor.matmul(ps[:, 2 + i, 128 * i:N], qk[:, 1, 128 * i:128 * i + 128], qk[:, 0, 128 * i:N], start=True, stop=True)
                        last.then_inc(S["scores"].sem, 1)
                        pe.wait_ge(S["st"].sem, now.count(S["st"]))
                        pe.wait_ge(S["v_sb"].sem, now.count(S["v_sb"]))
                        for i in range(TILES):
                            last = nc.tensor.matmul(ps[:, 7, 128 * i:N], v[:, 128 * i:128 * i + 128], st[:, i, 128 * i:N],
                                                    start=i == 0, stop=i == TILES - 1, skip_group_check=True)
                        last.then_inc(S["ret"].sem, 1)
                        pe.wait_ge(S["x2"].sem, now.count(S["x2"]))
                        nc.tensor.matmul(ps[:, 0, :], mean_w[:, :], xb[:, :], start=True, stop=True).then_inc(S["mean2"].sem, 1)
                        pe.wait_ge(S["sq2"].sem, now.count(S["sq2"]))
                        nc.tensor.matmul(ps[:, 1, :], mean_w[:, :], sq[:, :], start=True, stop=True).then_inc(S["var2"].sem, 1)

                @block.scalar
                def _(act):
                    with act.Fori(0, B) as b:
                        now = Steps(act, b + 1, USES)
                        act.wait_ge(S["xc"].sem, now.count(S["xc"]))
                        nc.scalar.activation(sq[:, :], xc[:, :], ACT.Square).then_inc(S["sq"].sem, 1)
                        act.wait_ge(S["var"].sem, now.count(S["var"]))
                        nc.scalar.activation(sq[:, :], ps[:, 1, :], ACT.Ln, bias=EPS).then_inc(S["lnv"].sem, 1)
                        act.wait_ge(S["lnv"].sem, now.count(S["lnv"]))
                        nc.scalar.activation(sq[:, :], sq[:, :], ACT.Exp, scale=-0.5).then_inc(S["rstd"].sem, 1)
                        act.wait_ge(S["proj"].sem, now.count(S["proj"]))
                        nc.scalar.activation(v[:, :], ps[:, 6, :], ACT.Copy).then_inc(S["v_sb"].sem, 1)
                        act.wait_ge(S["xc2"].sem, now.count(S["xc2"]))
                        nc.scalar.activation(sq[:, :], xc[:, :], ACT.Square).then_inc(S["sq2"].sem, 1)
                        act.wait_ge(S["var2"].sem, now.count(S["var2"]))
                        nc.scalar.activation(sq[:, :], ps[:, 1, :], ACT.Ln, bias=EPS).then_inc(S["lnv2"].sem, 1)
                        act.wait_ge(S["lnv2"].sem, now.count(S["lnv2"]))
                        nc.scalar.activation(sq[:, :], sq[:, :], ACT.Exp, scale=-0.5).then_inc(S["rstd2"].sem, 1)

                @block.vector
                def _(dve):
                    dve.wait_ge(consts, 16 * 8)
                    for dst, src in ((wqr, wq), (wkr, wk)):
                        nc.vector.tensor_scalar_mul(dst[:, 0:C:2], src[:, 1:C:2], -1.0).then_inc(turned, 1)
                        nc.vector.tensor_copy(dst[:, 1:C:2], src[:, 0:C:2]).then_inc(turned, 1)
                    with dve.Fori(0, B) as b:
                        now = Steps(dve, b + 1, USES)
                        cols = bass.ts(b, N)
                        dve.wait_ge(S["z"].sem, now.count(S["z"], -1))
                        nc.vector.tensor_tensor(xb[:, :], xT[:, cols], zT[:, cols], ALU.add).then_inc(S["x"].sem, 1)
                        dve.wait_ge(S["mean"].sem, now.count(S["mean"]))
                        nc.vector.tensor_tensor(xc[:, :], xb[:, :], ps[:, 0, :], ALU.subtract).then_inc(S["xc"].sem, 1)
                        dve.wait_ge(S["rstd"].sem, now.count(S["rstd"]))
                        nc.vector.tensor_tensor(xn[:, :], xc[:, :], sq[:, :], ALU.mult).then_inc(S["xn"].sem, 1)
                        dve.wait_ge(S["proj"].sem, now.count(S["proj"]))
                        for i, tab in enumerate((qcos, qsin, kcos, ksin)):
                            nc.vector.tensor_tensor(rope[:, i, :], ps[:, 2 + i, :], tab[:, :], ALU.mult).then_inc(S["rope4"].sem, 1)
                        dve.wait_ge(S["rope4"].sem, now.count(S["rope4"]))
                        for i in range(2):
                            nc.vector.tensor_tensor(qk[:, i, :], rope[:, 2 * i, :], rope[:, 2 * i + 1, :], ALU.add).then_inc(S["qk"].sem, 1)
                        dve.wait_ge(S["scores"].sem, now.count(S["scores"]))
                        for i in range(TILES):
                            nc.vector.tensor_tensor(st[:, i, 128 * i:N], ps[:, 2 + i, 128 * i:N], decay[:, 0:N - 128 * i], ALU.mult).then_inc(S["st"].sem, 1)
                        dve.wait_ge(S["ret"].sem, now.count(S["ret"]))
                        nc.vector.tensor_tensor(xb[:, :], xb[:, :], ps[:, 7, :], ALU.add).then_inc(S["x2"].sem, 1)
                        dve.wait_ge(S["mean2"].sem, now.count(S["mean2"]))
                        nc.vector.tensor_tensor(xc[:, :], xb[:, :], ps[:, 0, :], ALU.subtract).then_inc(S["xc2"].sem, 1)
                        nc.vector.tensor_copy(xT[:, cols], xb[:, :]).then_inc(S["xout"].sem, 1)
                        dve.wait_ge(S["rstd2"].sem, now.count(S["rstd2"]))
                        dve.wait_ge(S["xout"].sem, now.count(S["xout"]))
                        nc.vector.tensor_tensor(zT[:, cols], xc[:, :], sq[:, :], ALU.mult).then_inc(S["z"].sem, 1)

        def finish():
            summed, stored = sem("summed"), sem("stored")
            with nc.Block() as block:
                @block.vector
                def _(dve):
                    for b in range(B):
                        cols = slice(N * b, N * b + N)
                        nc.vector.tensor_tensor(xT[:, cols], xT[:, cols], zT[:, cols], ALU.add).then_inc(summed, 1)

                @block.sync
                def _(sp):
                    for b in range(B):
                        cols = slice(N * b, N * b + N)
                        sp.wait_ge(summed, b + 1)
                        sp.dma_start(out[:, cols], xT[:, cols]).then_inc(stored, 16)
                    sp.wait_ge(stored, 16 * B)

        stage_a()
        stage_ffn(0)
        stage_b()
        stage_ffn(1)
        finish()


def constants():
    f = np.float32
    C = 128
    p = np.arange(128)
    t = {}
    t["mean_w"] = np.full((C, C), 1.0 / C, f)
    t["ident"] = np.eye(128, dtype=f)
    t["headmask"] = (p[:, None] // 16 == np.arange(8)[None, :]).astype(f)
    t["blockmask"] = (p[:, None] // 16 == p[None, :] // 16).astype(f)
    t["headsum"] = (p[:, None] // 32 == p[None, :] // 32).astype(f)
    n, dh, win = 512, 64, 32
    half = np.arange(0, dh, 2, dtype=f)
    inv_freq = f(1.0) / (10000.0 ** (half.astype(np.float64) / dh)).astype(f)
    freqs = (np.arange(n, dtype=f)[:, None] * inv_freq[None, :]).astype(f).astype(np.float64)
    base = ((half + f(0.4 * dh)) / f(1.4 * dh)).astype(f)
    power = ((np.arange(n, dtype=f) - f(n // 2)) / f(win // 2)).astype(f)
    scale = base.astype(np.float64)[None, :] ** power.astype(np.float64)[:, None]
    tan, cos = np.tan(freqs), np.cos(freqs)
    four = lambda a: np.tile(a.T, (4, 1))
    t["tan2"] = np.stack([four(-tan), four(tan)], 1).astype(f)
    t["cos2"] = (np.stack([four(8.0 * cos * scale), four(cos / scale)], 1) * 2.0 ** 12).astype(f)
    q, key = p % 32, np.arange(64)
    off = (key[None, :] < q[:, None]) | (key[None, :] > q[:, None] + 32)
    later = np.where(off, f(-1e30), f(0.0)).astype(f)
    first = np.where(off | ((p[:, None] < 32) & (key[None, :] < 32)), f(-1e30), f(0.0)).astype(f)
    t["mask"] = np.concatenate([np.tile(first, (1, 4)), np.tile(later, (1, 8))], 1)
    vec = (np.arange(0, C, 2, dtype=f) + f(0.4 * C)) / f(1.4 * C)
    freq = f(1.0) / (10000.0 ** (np.arange(C // 2, dtype=np.float64) / (C // 2))).astype(f)
    pos = np.arange(n, dtype=f)
    scale = np.repeat(vec.astype(np.float64)[:, None] ** (pos / f(512.0)).astype(np.float64)[None, :], 2, axis=0)
    angle = np.repeat((pos[None, :] * freq[:, None]).astype(f).astype(np.float64), 2, axis=0)
    t["ret_qcos"], t["ret_qsin"] = (np.cos(angle) * scale).astype(f), (np.sin(angle) * scale).astype(f)
    t["ret_kcos"], t["ret_ksin"] = (np.cos(angle) / scale).astype(f), (np.sin(angle) / scale).astype(f)
    gap = np.arange(n)[None, :] - p[:, None]
    t["ret_decay"] = np.where(gap >= 0, 0.96875 ** np.maximum(gap, 0), 0.0).astype(f)
    t["causal"] = (p[:, None] <= p[None, :]).astype(f)
    return t


def kernel(**inputs):
    import concourse.bacc as _bacc
    from concourse import mybir as _mybir
    from concourse.bass_utils import run_bass_kernel_spmd as _run

    nc = _bacc.Bacc("TRN2", target_bir_lowering=False, num_devices=1)
    arrays = {}

    def give(name, a):
        a = np.ascontiguousarray(a)
        arrays[name] = a
        return nc.dram_tensor(name, a.shape, _mybir.dt.from_np(a.dtype), kind="ExternalInput").ap()

    i = {k: np.asarray(v) for k, v in inputs.items()}
    x = give("x", i["L0_attn_a_hidden_states"].reshape(-1, 128).T)
    tabs = {k: give("t_" + k, v) for k, v in constants().items()}
    wa = {"wq": give("wq", i["L0_attn_a_Wq"].T), "wk": give("wk", i["L0_attn_a_Wk"].T), "wv": give("wv", i["L0_attn_a_Wv"].T),
          "wo": give("wo", i["L0_attn_a_Wo"].T), "nw": give("nw", np.tile(i["L0_attn_a_norm_w"][None, :], (128, 1)))}
    wb = {n: give("ret_" + n, i["L0_attn_b_W_" + n[1].upper()]) for n in ("wq", "wk", "wv")}
    wf = {}
    w = i["L0_ffn_Wqkv"].reshape(6, 128, 3, 4, 4, 2, 32)
    qk = w[:, :, 0:2].transpose(0, 1, 3, 2, 5, 4, 6).reshape(6, 128, 4, 4, 128)
    wf["wqkv"] = give("wqkv", np.concatenate([qk, w[:, :, 2].reshape(6, 128, 4, 2, 128)], 3).transpose(0, 2, 1, 3, 4).reshape(24, 128, 768))
    qs, ks = (np.tile(i["L0_ffn_" + n].reshape(6, 1, 2, 32), (1, 4, 1, 1)).transpose(0, 1, 3, 2).reshape(6, 128, 2) for n in ("q_scale", "k_scale"))
    wf["pa"] = give("pa", np.concatenate([qs, ks], 2))
    wf["wout"] = give("wout", i["L0_ffn_Wo"])
    wf["w1"], wf["w2"] = give("w1", i["L0_ffn_W1"]), give("w2", i["L0_ffn_W2"])
    b1 = np.zeros((6, 2, 384), np.float32)
    b1[:, :, :341] = i["L0_ffn_b1"].reshape(6, 2, 341)
    b1 = b1.reshape(6, 2, 3, 128).transpose(0, 3, 1, 2)
    wf["pf"] = give("pf", np.concatenate([np.stack([i["L0_ffn_" + n] for n in ("ln_g", "ln_b", "b2")], 2), b1[:, :, 1], b1[:, :, 0]], 2))
    out = nc.dram_tensor("y", (128, 2048), _mybir.dt.float32, kind="ExternalOutput").ap()
    build_hybrid(nc, x, tabs, wa, wb, wf, out)
    r = _run(nc, [arrays], core_ids=[0])
    return r.results[0]["y"].T.reshape(4, 512, 128)
```

```python
import numpy as np


def build_hybrid(nc, x_in, tabs, wa, wb, wf, out):
    import math
    from contextlib import ExitStack

    import concourse.bass as bass
    from concourse import mybir

    F32, F32R, BF16 = mybir.dt.float32, mybir.dt.float32r, mybir.dt.bfloat16
    ALU, ACT, AX = mybir.AluOpType, mybir.ActivationFunctionType, mybir.AxisListType

    C = 128
    B, N = 4, 512
    TOK = B * N
    DEPTH, HEADS, DH, WIN = 6, 16, 64, 32
    HQ = 4
    QUADS = HEADS // HQ
    TILES = N // 128
    FF = 341
    FFC = [128, 128, FF - 256]
    EPS = 1e-5
    AH, AD = 8, 16
    LN2 = math.log(2.0)

    ctx = ExitStack()
    with ctx:
        def sb(name, shape, dt=F32, scope=ctx):
            return scope.enter_context(nc.sbuf_tensor(name, shape, dt))

        def sem(name, scope=ctx):
            return scope.enter_context(nc.semaphore(name))

        class Signal:

            def __init__(self, name, per=1, count=1, ahead=0):
                self.sem, self.per, self.count, self.ahead = sem(name), per, count, ahead

        class Steps:

            def __init__(self, eng, step, used=((1, 0),)):
                self.eng, self.step = eng, step
                self.known = {} if isinstance(step, int) else {(m, c): eng.snap(step * m + c) for m, c in used}

            def count(self, sig, at=0):
                key = (sig.count * sig.per, (at + 1 + sig.ahead - sig.count) * sig.per)
                if isinstance(self.step, int):
                    assert self.step * key[0] + key[1] > 0
                    return self.step * key[0] + key[1]
                return self.known[key]

        ps = ctx.enter_context(nc.psum_tensor("ps", [128, 8, 512], F32))

        xT = sb("xT", [C, TOK])
        zT = sb("zT", [C, TOK])
        mean_w = sb("mean_w", [C, C])
        split_w = nc.dram_tensor("split_w", (DEPTH * QUADS, 2, C, 6 * 128), F32, kind="Internal").ap()

        loaded = sem("loaded")
        loaded_rest = sem("loaded_rest")

        def stage_a():
            scope = ExitStack()
            with scope:
                def t(name, shape, dt=F32):
                    return sb("a_" + name, shape, dt, scope)

                wq, wk, wv_wk, wo = t("wq", [C, C]), t("wk", [C, C]), t("wv_wk", [C, 2 * C]), t("wo", [C, C])
                headmask, blockmask = t("headmask", [C, AH]), t("blockmask", [C, C])
                causal, nw, ident = t("causal", [128, 128]), t("nw", [C, 1]), t("ident", [128, 128])
                w_raw, zero = t("w_raw", [C, 2, 6 * 128]), t("zero", [C, 1])
                w_hi, w_lo = t("w_hi", [C, 2, 6 * 128], F32R), t("w_lo", [C, 2, 6 * 128], F32R)
                xc, sq, xn = t("xc", [C, N]), t("sq", [C, N]), t("xn", [C, N])
                qk, vk = t("qk", [C, 2, N]), t("vk", [128, TILES, 2 * C])
                ksum, qz, qm = t("ksum", [C, N]), t("qz", [C, N]), t("qm", [C, TILES, AH, 128])
                state, den = t("state", [C, TILES, C]), t("den", [128, TILES * AH])
                st = t("st", [128, 2, AH, 128])
                o, osq, ss, oT = t("o", [128, N]), t("osq", [128, N]), t("ss", [128, TILES * AH]), t("oT", [C, N])
                xb, xc2, sq2 = t("xb", [C, N]), t("xc2", [C, N]), t("sq2", [C, N])

                S = {n: Signal("a_" + n) for n in ("mean", "xc", "sq", "var", "lnv", "rstd", "xn", "proj", "ksum", "qz", "states", "den", "denmax",
                                                   "rden", "on", "osq", "ss", "lnr", "rr", "on2", "oT", "oT_sb", "y", "x1", "mean2", "xc2", "sq2",
                                                   "var2", "rstd2", "z")}
                S.update({n: Signal("a_" + n, ahead=1) for n in ("state", "den1")}, lnv2=Signal("a_lnv2", ahead=2),
                         qk_sb=Signal("a_qk_sb", 2), vk_sb=Signal("a_vk_sb", 2), qm=Signal("a_qm", TILES))
                s_tile, st_tile, o_tile = (Signal("a_" + n, 1, TILES) for n in ("s_tile", "st_tile", "o_tile"))
                raw_in, hi_done, lo_done = ([Signal(f"{n}{j}", per) for j in range(2)] for n, per in (("raw_in", 16), ("hi_done", 1), ("lo_done", 1)))
                split_out = [Signal(f"split_out{j}", 32, ahead=1) for j in range(2)]
                PE_USES = [(1, c) for c in range(-1, 1)] + [(2, -2), (2, 0), (4, -4)] + [(4, c) for c in range(-7, -3)]
                ACT_USES = [(1, -1), (1, 0), (1, 1), (4, -4)]
                DVE_USES = [(1, -1), (1, 0), (1, 1), (2, 0)] + [(4, c) for c in range(-7, -3)]
                LOADS = 11
                block = scope.enter_context(nc.Block())

                def steps_of(eng, step):
                    step(0, False, True)
                    with eng.Fori(1, B) as s:
                        step(s, True, True)
                    step(B, True, False)

                @block.sync
                def _(sp):
                    for sig in (S["state"], S["den1"], S["lnv2"]):
                        sp.sem_inc(sig.sem, sig.ahead)
                    for dst, src in ((xT[:, 0:N], x_in[:, 0:N]), (mean_w[:, :], tabs["mean_w"]), (wq[:, :], wa["wq"]), (wk[:, :], wa["wk"]),
                                     (wv_wk[:, :], wa["wv_wk"]), (headmask[:, :], tabs["headmask"]), (blockmask[:, :], tabs["blockmask"]),
                                     (causal[:, :], tabs["causal"]), (wo[:, :], wa["wo"]), (nw[:, :], wa["nw"]), (ident[:, :], tabs["ident"])):
                        sp.dma_start(dst, src).then_inc(loaded, 16)
                    sp.dma_start(xT[:, N:], x_in[:, N:]).then_inc(loaded_rest, 16)
                    for j in range(2):
                        sp.sem_inc(split_out[j].sem, 32)
                    with sp.Fori(0, DEPTH * QUADS // 2) as n:
                        now = Steps(sp, n + 1, ((1, 0), (16, 0), (32, 0)))
                        for j in range(2):
                            sp.dma_start(w_raw[:, j], wf["wqkv"][bass.ds(n * 2 + j, 1)].rearrange("l c n -> (l c) n")).then_inc(raw_in[j].sem, 16)
                        for j in range(2):
                            sp.wait_ge(lo_done[j].sem, now.count(lo_done[j]))
                            for part, w in enumerate((w_hi, w_lo)):
                                sp.dma_start(split_w[bass.ds(n * 2 + j, 1), part].rearrange("l c n -> (l c) n"), w[:, j].bitcast(F32)).then_inc(split_out[j].sem, 16)
                    for j in range(2):
                        sp.wait_ge(split_out[j].sem, 32 * (DEPTH * QUADS // 2 + 1))

                @block.gpsimd
                def _(pool):
                    cleared = sem("a_cleared", scope)
                    nc.gpsimd.memset(zero[:, :], 0.0).then_inc(cleared, 1)
                    pool.wait_ge(cleared, 1)
                    with pool.Fori(0, DEPTH * QUADS // 2) as n:
                        now = Steps(pool, n + 1, ((1, 0), (16, 0), (32, 0)))
                        for j in range(2):
                            pool.wait_ge(raw_in[j].sem, now.count(raw_in[j]))
                            pool.wait_ge(split_out[j].sem, now.count(split_out[j], -1))
                            nc.gpsimd.tensor_tensor(w_hi[:, j], w_raw[:, j], zero[:, :].broadcast_to([C, 6 * 128]), ALU.add).then_inc(hi_done[j].sem, 1)
                            pool.wait_ge(hi_done[j].sem, now.count(hi_done[j]))
                            nc.gpsimd.tensor_tensor(w_lo[:, j], w_raw[:, j], w_hi[:, j].bitcast(F32), ALU.subtract).then_inc(lo_done[j].sem, 1)

                @block.tensor
                def _(pe):
                    def step(s, prev, cur):
                        now = Steps(pe, s + 1, PE_USES)

                        def score(i):
                            if i == 0:
                                pe.wait_ge(S["lnv2"].sem, now.count(S["lnv2"], -2))
                                pe.wait_ge(S["qk_sb"].sem, now.count(S["qk_sb"], -1))
                                pe.wait_ge(S["qm"].sem, now.count(S["qm"], -1))
                            else:
                                pe.wait_ge(st_tile.sem, now.count(st_tile, i - 1 - TILES))
                            for half in range(2):
                                last = nc.tensor.matmul(ps[:, 5 + half, :], qk[:, 1, 128 * i:128 * i + 128], qm[:, i, 4 * half:4 * half + 4, :],
                                                        start=True, stop=True)
                            last.then_inc(s_tile.sem, 1)

                        def weigh(i):
                            if i == 0:
                                pe.wait_ge(S["vk_sb"].sem, now.count(S["vk_sb"], -1))
                                pe.wait_ge(S["state"].sem, now.count(S["state"], -1))
                            pe.wait_ge(st_tile.sem, now.count(st_tile, i - TILES))
                            nc.tensor.matmul(ps[:, 7, 128 * i:128 * i + 128], qk[:, 0, 128 * i:128 * i + 128], state[:, i, :],
                                             start=True, stop=False, skip_group_check=True)
                            for h in range(AH):
                                last = nc.tensor.matmul(ps[:, 7, 128 * i + AD * h:128 * i + AD * h + AD], st[:, i % 2, h, :], vk[:, i, AD * h:AD * h + AD],
                                                        start=False, stop=True, skip_group_check=True)
                            last.then_inc(o_tile.sem, 1)

                        if cur:
                            if prev:
                                pe.wait_ge(loaded_rest, 16)
                            pe.wait_ge(S["state"].sem, now.count(S["state"], -1))
                            pe.wait_ge(S["den1"].sem, now.count(S["den1"], -1))
                            cols = bass.ts(s, N) if prev else slice(0, N)
                            nc.tensor.matmul(ps[:, 0, :], mean_w[:, :], xT[:, cols], start=True, stop=True).then_inc(S["mean"].sem, 1)
                        if prev:
                            score(0)
                            score(1)
                        if cur:
                            pe.wait_ge(S["sq"].sem, now.count(S["sq"]))
                            nc.tensor.matmul(ps[:, 0, :], mean_w[:, :], sq[:, :], start=True, stop=True).then_inc(S["var"].sem, 1)
                        if prev:
                            weigh(0)
                            score(2)
                        if cur:
                            pe.wait_ge(S["xn"].sem, now.count(S["xn"]))
                            for i, w in enumerate((wq, wk)):
                                nc.tensor.matmul(ps[:, 1 + i, :], w[:, :], xn[:, :], start=True, stop=True)
                            for i in range(TILES):
                                last = nc.tensor.matmul(ps[:, 3 + i // 2, 256 * (i % 2):256 * (i % 2) + 256], xn[:, 128 * i:128 * i + 128], wv_wk[:, :],
                                                        start=True, stop=True)
                            last.then_inc(S["proj"].sem, 1)
                        if prev:
                            weigh(1)
                            score(3)
                            weigh(2)
                            weigh(3)
                        if cur:
                            pe.wait_ge(S["vk_sb"].sem, now.count(S["vk_sb"]))
                            for i in range(1, TILES):
                                for j in range(i):
                                    last = nc.tensor.matmul(ps[:, 0, 128 * i:128 * i + 128], vk[:, j, C:], vk[:, j, 0:C], start=j == 0, stop=j == i - 1)
                            last.then_inc(S["states"].sem, 1)
                            pe.wait_ge(S["qz"].sem, now.count(S["qz"]))
                            for i in range(TILES):
                                last = nc.tensor.matmul(ps[:, 1, AH * i:AH * i + AH], qz[:, 128 * i:128 * i + 128], headmask[:, :], start=True, stop=True)
                            last.then_inc(S["den"].sem, 1)
                        if prev:
                            pe.wait_ge(S["on2"].sem, now.count(S["on2"], -1))
                            for i in range(TILES):
                                last = nc.tensor.transpose(ps[:, 5, 128 * i:128 * i + 128], o[:, 128 * i:128 * i + 128], ident[:, :])
                            last.then_inc(S["oT"].sem, 1)
                            pe.wait_ge(S["oT_sb"].sem, now.count(S["oT_sb"], -1))
                            nc.tensor.matmul(ps[:, 6, :], wo[:, :], oT[:, :], start=True, stop=True).then_inc(S["y"].sem, 1)
                            pe.wait_ge(S["x1"].sem, now.count(S["x1"], -1))
                            nc.tensor.matmul(ps[:, 5, :], mean_w[:, :], xb[:, :], start=True, stop=True).then_inc(S["mean2"].sem, 1)
                            pe.wait_ge(S["sq2"].sem, now.count(S["sq2"], -1))
                            nc.tensor.matmul(ps[:, 6, :], mean_w[:, :], sq2[:, :], start=True, stop=True).then_inc(S["var2"].sem, 1)

                    pe.wait_ge(loaded, 16 * LOADS)
                    steps_of(pe, step)

                @block.scalar
                def _(act):
                    def step(s, prev, cur):
                        now = Steps(act, s + 1, ACT_USES)
                        if cur:
                            act.wait_ge(S["xc"].sem, now.count(S["xc"]))
                            nc.scalar.activation(sq[:, :], xc[:, :], ACT.Square).then_inc(S["sq"].sem, 1)
                            act.wait_ge(S["var"].sem, now.count(S["var"]))
                            nc.scalar.activation(sq[:, :], ps[:, 0, :], ACT.Ln, bias=EPS).then_inc(S["lnv"].sem, 1)
                            act.wait_ge(S["lnv"].sem, now.count(S["lnv"]))
                            nc.scalar.activation(sq[:, :], sq[:, :], ACT.Exp, scale=-0.5).then_inc(S["rstd"].sem, 1)
                            act.wait_ge(S["proj"].sem, now.count(S["proj"]))
                            if prev:
                                act.wait_ge(o_tile.sem, now.count(o_tile, -1))
                            for i in range(2):
                                nc.scalar.activation(qk[:, i, :], ps[:, 1 + i, :], ACT.Copy).then_inc(S["qk_sb"].sem, 1)
                            for i in range(2):
                                nc.scalar.activation(vk[:, 2 * i:2 * i + 2, :], ps[:, 3 + i, :].rearrange("p (t n) -> p t n", t=2), ACT.Copy).then_inc(S["vk_sb"].sem, 1)
                        if prev:
                            act.wait_ge(S["on"].sem, now.count(S["on"], -1))
                            nc.scalar.activation(osq[:, :], o[:, :], ACT.Square).then_inc(S["osq"].sem, 1)
                            act.wait_ge(S["ss"].sem, now.count(S["ss"], -1))
                            nc.scalar.activation(ss[:, :], ss[:, :], ACT.Ln, bias=EPS, scale=1.0 / AD).then_inc(S["lnr"].sem, 1)
                            act.wait_ge(S["lnr"].sem, now.count(S["lnr"], -1))
                            nc.scalar.activation(ss[:, :], ss[:, :], ACT.Exp, scale=-0.5).then_inc(S["rr"].sem, 1)
                        if cur:
                            act.wait_ge(S["den"].sem, now.count(S["den"]))
                            nc.scalar.activation(den[:, :], ps[:, 1, 0:TILES * AH], ACT.Abs).then_inc(S["den1"].sem, 1)
                        if prev:
                            act.wait_ge(S["oT"].sem, now.count(S["oT"], -1))
                            nc.scalar.activation(oT[:, :], ps[:, 5, :], ACT.Identity, scale=nw[:, 0:1]).then_inc(S["oT_sb"].sem, 1)
                            act.wait_ge(S["xc2"].sem, now.count(S["xc2"], -1))
                            nc.scalar.activation(sq2[:, :], xc2[:, :], ACT.Square).then_inc(S["sq2"].sem, 1)
                            act.wait_ge(S["var2"].sem, now.count(S["var2"], -1))
                            nc.scalar.activation(sq2[:, :], ps[:, 6, :], ACT.Ln, bias=EPS).then_inc(S["lnv2"].sem, 1)
                            act.wait_ge(S["lnv2"].sem, now.count(S["lnv2"], -1))
                            nc.scalar.activation(sq2[:, :], sq2[:, :], ACT.Exp, scale=-0.5).then_inc(S["rstd2"].sem, 1)

                    act.preload_act_table_set("natural_log_exp_and_others")
                    act.wait_ge(loaded, 16 * LOADS)
                    steps_of(act, step)

                @block.vector
                def _(dve):
                    heads = lambda a: a.rearrange("p (g d) -> p g d", d=AD)

                    def step(s, prev, cur):
                        now = Steps(dve, s + 1, DVE_USES)
                        col = (bass.ts(s, N), bass.ts(s - 1, N)) if prev and cur else (slice(0, N), slice(TOK - N, TOK))

                        def mask(i):
                            dve.wait_ge(s_tile.sem, now.count(s_tile, i - TILES))
                            if i >= 2:
                                dve.wait_ge(o_tile.sem, now.count(o_tile, i - 2 - TILES))
                            nc.vector.tensor_tensor(st[:, i % 2], ps[:, 5:7, :].rearrange("p a (h q) -> p (a h) q", q=128),
                                                    causal[:, :].unsqueeze(1).broadcast_to([128, AH, 128]), ALU.mult).then_inc(st_tile.sem, 1)

                        if cur:
                            dve.wait_ge(S["mean"].sem, now.count(S["mean"]))
                            nc.vector.tensor_tensor(xc[:, :], xT[:, col[0]], ps[:, 0, :], ALU.subtract).then_inc(S["xc"].sem, 1)
                        if prev:
                            mask(0)
                            mask(1)
                        if cur:
                            dve.wait_ge(S["rstd"].sem, now.count(S["rstd"]))
                            nc.vector.tensor_tensor(xn[:, :], xc[:, :], sq[:, :], ALU.mult).then_inc(S["xn"].sem, 1)
                        if prev:
                            mask(2)
                            mask(3)
                            dve.wait_ge(o_tile.sem, now.count(o_tile, -1))
                            dve.wait_ge(S["rden"].sem, now.count(S["rden"], -1))
                            nc.vector.tensor_tensor(heads(o[:, :]), heads(ps[:, 7, :]), den[:, :].unsqueeze(2).broadcast_to([128, TILES * AH, AD]),
                                                    ALU.mult).then_inc(S["on"].sem, 1)
                        if cur:
                            dve.wait_ge(S["qk_sb"].sem, now.count(S["qk_sb"]))
                            nc.vector.tensor_tensor_scan(ksum[:, :], qk[:, 1, :], qk[:, 1, :], 0.0, ALU.add, ALU.bypass).then_inc(S["ksum"].sem, 1)
                            dve.wait_ge(S["ksum"].sem, now.count(S["ksum"]))
                            nc.vector.tensor_tensor(qz[:, :], qk[:, 0, :], ksum[:, :], ALU.mult).then_inc(S["qz"].sem, 1)
                        if prev:
                            dve.wait_ge(S["osq"].sem, now.count(S["osq"], -1))
                            nc.vector.tensor_reduce(ss[:, :], heads(osq[:, :]), AX.X, ALU.add).then_inc(S["ss"].sem, 1)
                        if cur:
                            for i in range(TILES):
                                nc.vector.tensor_tensor(qm[:, i], qk[:, 0, 128 * i:128 * i + 128].unsqueeze(1).broadcast_to([C, AH, 128]),
                                                        headmask[:, :].unsqueeze(2).broadcast_to([C, AH, 128]), ALU.mult).then_inc(S["qm"].sem, 1)
                                if prev and i == 0:
                                    dve.wait_ge(S["rr"].sem, now.count(S["rr"], -1))
                                    nc.vector.tensor_tensor(heads(o[:, :]), heads(o[:, :]), ss[:, :].unsqueeze(2).broadcast_to([128, TILES * AH, AD]),
                                                            ALU.mult).then_inc(S["on2"].sem, 1)
                            dve.wait_ge(S["states"].sem, now.count(S["states"]))
                            nc.vector.tensor_tensor(state[:, 1:, :], ps[:, 0, C:].rearrange("p (t n) -> p t n", t=TILES - 1),
                                                    blockmask[:, :].unsqueeze(1).broadcast_to([C, TILES - 1, C]), ALU.mult).then_inc(S["state"].sem, 1)
                            dve.wait_ge(S["den1"].sem, now.count(S["den1"]))
                            nc.vector.tensor_scalar_max(den[:, :], den[:, :], 1.0).then_inc(S["denmax"].sem, 1)
                            dve.wait_ge(S["denmax"].sem, now.count(S["denmax"]))
                            nc.vector.reciprocal(den[:, :], den[:, :]).then_inc(S["rden"].sem, 1)
                        elif prev:
                            dve.wait_ge(S["rr"].sem, now.count(S["rr"], -1))
                            nc.vector.tensor_tensor(heads(o[:, :]), heads(o[:, :]), ss[:, :].unsqueeze(2).broadcast_to([128, TILES * AH, AD]),
                                                    ALU.mult).then_inc(S["on2"].sem, 1)
                        if prev:
                            dve.wait_ge(S["y"].sem, now.count(S["y"], -1))
                            nc.vector.tensor_tensor(xb[:, :], xT[:, col[1]], ps[:, 6, :], ALU.add).then_inc(S["x1"].sem, 1)
                            dve.wait_ge(S["mean2"].sem, now.count(S["mean2"], -1))
                            nc.vector.tensor_tensor(xc2[:, :], xb[:, :], ps[:, 5, :], ALU.subtract).then_inc(S["xc2"].sem, 1)
                            nc.vector.tensor_copy(xT[:, col[1]], xb[:, :])
                            dve.wait_ge(S["rstd2"].sem, now.count(S["rstd2"], -1))
                            nc.vector.tensor_tensor(zT[:, col[1]], xc2[:, :], sq2[:, :], ALU.mult).then_inc(S["z"].sem, 1)

                    nc.vector.memset(state[:, 0, :], 0.0)
                    dve.wait_ge(loaded, 16 * LOADS)
                    dve.wait_ge(loaded_rest, 16)
                    steps_of(dve, step)

        PAD = WIN
        NORM_FLOOR_INV = 1e12
        PRE = 24
        STEPS = DEPTH * B
        NJ = 3
        NO, SS, FB = (3, 4), (5, 6), 7

        def per_quad(name, per=1, ahead=0):
            return Signal(name, per, QUADS, ahead)

        ORDER = ([("qk", 0, i) for i in range(4)] + [("qk", 1, i) for i in range(4)] + [("v", 0, i) for i in range(TILES)]
                 + [("qk", 2, i) for i in range(4)] + [("v", 1, i) for i in range(TILES)] + [("qk", 3, i) for i in range(4)]
                 + [("gate", -1, i) for i in range(3)] + [("val", -1, i) for i in range(3)])
        assert len(ORDER) % NJ == 0
        qk_ready, qk_read = Signal("qk_ready", 1, 4 * QUADS), Signal("qk_read", 1, 4 * QUADS)
        v_ready, v_read = Signal("v_ready", 1, 2 * TILES), Signal("v_read", 1, 2 * TILES)
        xs_done = Signal("xs_done", 32, ahead=1)
        x_hi, x_lo = Signal("x_hi", ahead=1), Signal("x_lo", ahead=1)
        sq_done = Signal("sq_done", 1, 4 * QUADS)
        sq_sum, sq_hi, sq_lo = ([per_quad(f"{n}{i}") for i in range(2)] for n in ("sq_sum", "sq_hi", "sq_lo"))
        n_ready = per_quad("n_ready", ahead=1)
        q_sum, k_sum = per_quad("q_sum"), per_quad("k_sum")
        n_log, n_inv, u_done = Signal("n_log", 1, 2 * QUADS), per_quad("n_inv"), per_quad("u_done", 2)
        gain, rope_q, rope_k = per_quad("gain"), per_quad("rope_q", ahead=1), per_quad("rope_k", ahead=1)
        k_dma, s_ready = per_quad("k_dma", 16 * HQ), per_quad("s_ready", ahead=2)
        s_max, s_sub, p_exp = per_quad("s_max"), per_quad("s_sub", ahead=1), per_quad("p_exp")
        p_sum, p_inv, p_norm = per_quad("p_sum"), per_quad("p_inv"), per_quad("p_norm")
        p_tr, t_dma = per_quad("p_tr", ahead=2), per_quad("t_dma", 16 * HQ, ahead=2)
        o_ready = [per_quad(f"o_ready{i}", ahead=3) for i in range(2)]
        o_read = [per_quad(f"o_read{i}", ahead=3) for i in range(2)]
        vs_dma = Signal("vs_dma", 32, 2)
        wo_ready, fs_done = Signal("wo_ready"), Signal("fs_done", 2)
        F = {n: Signal("f_" + n) for n in ("x1", "mean", "xc", "sq", "var", "lnv", "rstd", "xn", "xa", "w2")}
        x2 = Signal("x2", 1, 1, 4)
        gate_ready, val_ready = Signal("gate_ready", 1, 3), Signal("val_ready", 1, 3)
        gate_done, val_done = Signal("gate_done", 1, 3), Signal("val_done", 1, 3, ahead=3)
        w_qkv = [Signal(f"w_qkv{g}", 48) for g in range(QUADS)]
        w_out, w_ff = Signal("w_out", 16), Signal("w_ff", 64)
        GRANTED = [xs_done, x_hi, x_lo, n_ready, rope_q, rope_k, s_ready, s_sub, p_tr, t_dma, *o_ready, *o_read, x2, val_done]

        SP_USES = [(1, -1), (1, 1), (1, 3), *((4, c) for c in range(-3, 2)), (8, -4), (8, 0), (16, -16), (16, 0)]
        PE_USES = [(1, -1), (1, 0), (1, 2), (2, -2), (3, -5), (3, -4), (3, -3), (3, 0), *((4, c) for c in range(-4, 2)),
                   *((8, c) for c in range(-7, 1)), *((16, c) for c in range(-15, 1)), (64, -64), (64, -32), *((256, 64 * c) for c in range(-4, 1))]
        ACT_USES = [(1, -1), (3, -5), (3, -4), (3, -3), (32, 32), *((4, c) for c in range(-3, 2)), *((8, c) for c in range(-7, 1)),
                    *((16, c) for c in range(-15, 1))]
        POOL_USES = [*((4, c) for c in range(-4, 1)), *((8, c) for c in range(-6, 1, 2)), *((16, c) for c in range(-14, 1, 2))]
        DVE_USES = [(1, -1), (1, 1), (3, -5), (3, -4), (3, -3), *((4, c) for c in range(-5, 2)), *((8, c) for c in range(-6, 1, 2)),
                    *((16, c) for c in range(-12, 1, 4)), *((256, 64 * c) for c in range(-4, 1))]

        def stage_ffn(phase):
            scope = ExitStack()
            with scope:
                def t(name, shape, dt=F32):
                    return sb(f"f{phase}_" + name, shape, dt, scope=scope)

                wh, wl = t("wh", [C, QUADS, 6, 128], F32R), t("wl", [C, QUADS, 6, 128], F32R)
                wout = t("wout", [128, 8, C])
                w1, w2 = t("w1", [C, 2 * FF]), t("w2", [128, 3, C])
                pa, pf = t("pa", [128, QUADS, 4]), t("pf", [128, 9])
                tan2, cos2 = t("tan2", [128, 2, N]), t("cos2", [128, 2, N])
                mask, ones = t("mask", [128, 768], BF16), t("ones", [128, 128], F32R)
                identb = t("identb", [128, 128], BF16)
                xs, xh, x1 = t("xs", [C, N]), t("xh", [C, N], F32R), t("x1", [C, N])
                xl = xs[:, :].bitcast(F32R)
                ab, rn, u = t("ab", [128, 2, 4, N]), t("rn", [128, 2, N]), t("u", [128, 4, N])
                sq = t("sq", [128, 4, N], F32R)
                kb = t("kb", [128, 2, HQ, PAD + N])
                p, pt = t("p", [128, 1024]), t("pt", [128, 1024])
                tb = t("tb", [128, HQ, 1024])
                v, vs = t("v", [128, TILES, 1024]), t("vs", [128, TILES, 1024])
                ot = t("ot", [128, 8, N])
                mx, rs = t("mx", [128, 16]), t("rs", [128, 16])
                fs, fc, fq, hid = t("fs", [C, N]), t("fc", [C, N]), t("fq", [C, N]), t("hid", [128, 3, N])
                consts, zeroed = sem(f"f{phase}_consts", scope), sem(f"f{phase}_zeroed", scope)
                masked, xs_first = sem(f"f{phase}_masked", scope), sem(f"f{phase}_xs_first", scope)
                edges = sem(f"f{phase}_edges", scope)
                split_first = sem(f"f{phase}_split_first", scope)
                N_CONST, N_MASKED = 6 * 16, 3
                block = scope.enter_context(nc.Block())

                L0, FIRST = phase * DEPTH, phase * STEPS

                def bank(*which):
                    return ps[:, ORDER.index(which) % NJ, :]

                def window(tile, i):
                    return 128 * tile + WIN * i

                def steps_of(eng, step):
                    step(FIRST, False, True)
                    with eng.Fori(FIRST + 1, FIRST + STEPS) as s:
                        step(s, True, True)
                    step(FIRST + STEPS, True, False)

                @block.sync
                def _(sp):
                    if phase == 0:
                        for s in GRANTED:
                            sp.sem_inc(s.sem, s.ahead * s.per)

                    def load_qkv(at, quads):
                        for g in quads:
                            for part, w in enumerate((wh, wl)):
                                sp.dma_start(w[:, g].bitcast(F32), split_w[bass.ds(at * QUADS + g, 1), part].rearrange("l c (q n) -> (l c) q n", q=6)).then_inc(w_qkv[g].sem, 16)
                            sp.dma_start(pa[:, g], wf["pa"][bass.ds(at, 1)].rearrange("l c n -> (l c) n")).then_inc(w_qkv[g].sem, 16)

                    def load_out(at):
                        sp.dma_start(wout[:, :, :], wf["wout"][bass.ds(at, 1)].rearrange("l (k p) n -> p (l k) n", p=128)).then_inc(w_out.sem, 16)

                    def load_ff(at):
                        sp.dma_start(w1[:, :], wf["w1"][bass.ds(at, 1)].rearrange("l c n -> (l c) n")).then_inc(w_ff.sem, 16)
                        sp.dma_start(w2[:, 0:2, :], wf["w2"][bass.ds(at, 1), 0:256].rearrange("l (k p) n -> p (l k) n", p=128)).then_inc(w_ff.sem, 16)
                        sp.dma_start(w2[0:FFC[2], 2, :], wf["w2"][bass.ds(at, 1), 256:FF].rearrange("l p n -> (l p) n")).then_inc(w_ff.sem, 16)
                        sp.dma_start(pf[:, :], wf["pf"][bass.ds(at, 1)].rearrange("l c n -> (l c) n")).then_inc(w_ff.sem, 16)

                    sp.dma_start(xs[0:64, :], zT[0:64, 0:N]).then_inc(xs_first, 16)
                    sp.dma_start(xs[64:128, 1:N], zT[64:128, 0:N - 1]).then_inc(xs_first, 16)
                    load_qkv(0, range(1))
                    for dst, src in ((fc[:, 128:256], tabs["headsum"]), (tan2[:, :, :], tabs["tan2"]), (cos2[:, :, :], tabs["cos2"]),
                                     (hid[:, 0:2, 0:384], tabs["mask"].rearrange("p (a n) -> p a n", a=2)), (fc[:, 0:128], tabs["ident"]),
                                     (mean_w[:, :], tabs["mean_w"])):
                        sp.dma_start(dst, src).then_inc(consts, 16)
                    load_qkv(0, range(1, QUADS))
                    load_out(0)
                    load_ff(0)

                    def step(s, prev, cur, new_layer=None, next_layer=None):
                        now = Steps(sp, s + 1, SP_USES)
                        if new_layer is not None:
                            sp.wait_ge(qk_read.sem, now.count(qk_read, -1))
                            load_qkv(new_layer, range(1, QUADS))
                        next_col = N if not prev else sp.snap((s + 1) % B * N)
                        for k in range(QUADS):
                            if cur if k >= 2 else prev:
                                g = k - 2
                                sp.wait_ge(o_ready[1].sem, now.count(o_ready[1], g - 1))
                                sp.wait_ge(p_tr.sem, now.count(p_tr, g))
                                for w in range(4):
                                    rows = slice(32 * w, 32 * w + 32)
                                    sp.dma_start(tb[rows, w, :], pt[rows, :]).then_inc(t_dma.sem, 16)
                            if k in (1, 2) and cur:
                                i = k - 1
                                sp.wait_ge(v_read.sem, now.count(v_read, TILES * i + TILES - 1))
                                half = slice(512 * i, 512 * i + 512)
                                sp.dma_start(vs[WIN:128, :, half], v[0:128 - WIN, :, half]).then_inc(vs_dma.sem, 16)
                                sp.dma_start(vs[0:WIN, 1:TILES, half], v[128 - WIN:128, 0:TILES - 1, half]).then_inc(vs_dma.sem, 16)
                            if k == 2 and cur:
                                sp.wait_ge(x2.sem, now.count(x2, -3))
                            if k == 3 and cur:
                                sp.wait_ge(qk_ready.sem, now.count(qk_ready, 4 * QUADS - 1))
                                sp.dma_start(xs[0:64, :], zT[0:64, bass.ds(next_col, N)]).then_inc(xs_done.sem, 16)
                                sp.dma_start(xs[64:128, 1:N], zT[64:128, bass.ds(next_col, N - 1)]).then_inc(xs_done.sem, 16)
                            if k == 3 and next_layer is not None:
                                load_qkv(next_layer, range(1))
                            if k == 3 and new_layer is not None:
                                sp.wait_ge(wo_ready.sem, now.count(wo_ready, -1))
                                load_out(new_layer)
                            if cur:
                                sp.wait_ge(s_ready.sem, now.count(s_ready, k - 1))
                                sp.wait_ge(rope_k.sem, now.count(rope_k, k))
                                for h in range(HQ):
                                    rows = slice(32 * h, 32 * h + 32)
                                    sp.dma_start(kb[rows, :, h, PAD:], ab[rows, k % 2, 2:4, :]).then_inc(k_dma.sem, 16)
                        if new_layer is not None:
                            sp.wait_ge(x2.sem, now.count(x2, -1))
                            load_ff(new_layer)

                    def later_sequences(first, end):
                        with sp.Fori(1, end) as b:
                            step(first + b, True, True)

                    sp.wait_ge(zeroed, 3)
                    step(FIRST, False, True)
                    with sp.Fori(1, DEPTH) as at:
                        later_sequences(FIRST - B + at * B, B - 1)
                        step(FIRST - 1 + at * B, True, True, next_layer=at)
                        step(FIRST + at * B, True, True, new_layer=at)
                    later_sequences(FIRST + STEPS - B, B)
                    step(FIRST + STEPS, True, False)

                @block.tensor
                def _(pe):
                    def step(s, prev, cur):
                        now = Steps(pe, s + 1, PE_USES)
                        layer = Steps(pe, (s >> 2) + 1, ((48, 0),))
                        before = Steps(pe, ((s - 1) >> 2) + 1, ((16, 0), (64, 0)))

                        def bank_free(*which):
                            n = ORDER.index(which) - NJ
                            while not (prev if ORDER[n][1] < 0 else cur) and n >= 0:
                                n -= NJ
                            if n < 0 and not prev:
                                return
                            kind, g, i = ORDER[n]
                            at = 0 if n >= 0 else -1
                            if kind == "qk":
                                pe.wait_ge(qk_read.sem, now.count(qk_read, 4 * (g + QUADS * at) + i))
                            elif kind == "v":
                                pe.wait_ge(v_read.sem, now.count(v_read, TILES * (g + 2 * at) + i))
                            elif kind == "gate":
                                pe.wait_ge(gate_done.sem, now.count(gate_done, i + 3 * (at - 1)))
                            else:
                                pe.wait_ge(val_done.sem, now.count(val_done, i + 3 * (at - 1)))

                        def project(g, masked_scores=None):
                            pe.wait_ge(w_qkv[g].sem, layer.count(w_qkv[g]))
                            for i in range(4):
                                if i == 3 and masked_scores is not None:
                                    mask_scores(masked_scores)
                                bank_free("qk", g, i)
                                nc.tensor.matmul(bank("qk", g, i), wh[:, g, i, :], xh[:, :], start=True, stop=False)
                                nc.tensor.matmul(bank("qk", g, i), wh[:, g, i, :], xl, start=False, stop=False)
                                nc.tensor.matmul(bank("qk", g, i), wl[:, g, i, :], xh[:, :], start=False, stop=True).then_inc(qk_ready.sem, 1)

                        def project_v(i):
                            pe.wait_ge(w_qkv[2 * i + 1].sem, layer.count(w_qkv[2 * i + 1]))
                            for tile in range(TILES):
                                bank_free("v", i, tile)
                                cols, pair = slice(128 * tile, 128 * tile + 128), slice(2 * i, 2 * i + 2)
                                nc.tensor.matmul(bank("v", i, tile), xh[:, cols], wh[:, pair, 4:6, :], start=True, stop=False)
                                nc.tensor.matmul(bank("v", i, tile), xh[:, cols], wl[:, pair, 4:6, :], start=False, stop=False)
                                nc.tensor.matmul(bank("v", i, tile), xl[:, cols], wh[:, pair, 4:6, :], start=False, stop=True).then_inc(v_ready.sem, 1)

                        def norms(g):
                            for i in range(2):
                                pe.wait_ge(o_read[i].sem, now.count(o_read[i], g - 3))
                                pe.wait_ge(sq_hi[i].sem, now.count(sq_hi[i], g))
                                nc.tensor.matmul(ps[:, NO[i], :], ones[:, :], sq[:, 2 * i + 1, :], start=True, stop=False)
                                pe.wait_ge(sq_lo[i].sem, now.count(sq_lo[i], g))
                                last = nc.tensor.matmul(ps[:, NO[i], :], ones[:, :], sq[:, 2 * i, :], start=False, stop=True)
                            last.then_inc(n_ready.sem, 1)

                        def mask_scores(g):
                            pe.wait_ge(s_sub.sem, now.count(s_sub, g - 1))
                            for j in range(2):
                                nc.tensor.matmul(ps[:, SS[j], :], identb[:, :], mask[:, 256 * j:256 * j + 512], start=True, stop=False, skip_group_check=True)

                        def scores(g):
                            pe.wait_ge(rope_q.sem, now.count(rope_q, g))
                            pe.wait_ge(k_dma.sem, now.count(k_dma, g))
                            for tile in range(TILES):
                                for a in range(2):
                                    for i in range(4):
                                        w0 = window(tile, i)
                                        rows = slice(32 * i, 32 * i + 32)
                                        last = nc.tensor.matmul(ps[rows, SS[tile // 2], 256 * (tile % 2):256 * (tile % 2) + 256],
                                                                ab[:, g % 2, a, w0:w0 + WIN], kb[:, a, :, w0:w0 + 2 * WIN],
                                                                start=False, stop=a == 1, skip_group_check=True, tile_position=(0, 32 * i))
                            last.then_inc(s_ready.sem, 1)

                        def values(g):
                            at = g + 2 if cur else -1
                            pe.wait_ge(n_log.sem, now.count(n_log, 2 * at))
                            if not cur and g == -1:
                                for i in range(2):
                                    pe.wait_ge(o_read[i].sem, now.count(o_read[i], g - 1))
                            pe.wait_ge(vs_dma.sem, now.count(vs_dma, g // 2))
                            pe.wait_ge(t_dma.sem, now.count(t_dma, g))
                            for pair in range(2):
                                if pair:
                                    pe.wait_ge(n_log.sem, now.count(n_log, 2 * at + 1))
                                for tile in range(TILES):
                                    for blk, val in ((0, vs), (1, v)):
                                        for h in (2 * pair, 2 * pair + 1):
                                            rows = slice(64 * (h % 2), 64 * (h % 2) + 64)
                                            c0 = ((tile * HQ + h) * 2 + blk) * WIN
                                            d0 = 256 * (g % QUADS) + 64 * h
                                            last = nc.tensor.matmul(ps[rows, NO[pair], 128 * tile:128 * tile + 128],
                                                                    val[:, tile, d0:d0 + 64], tb[:, :, c0:c0 + WIN],
                                                                    start=blk == 0, stop=blk == 1, tile_position=(0, 64 * (h % 2)))
                                last.then_inc(o_ready[pair].sem, 1)

                        f = ps[:, FB, :]

                        def project_out(g):
                            if g == 0:
                                pe.wait_ge(x2.sem, now.count(x2, -2))
                                pe.wait_ge(w_out.sem, before.count(w_out))
                            for i in range(2):
                                pe.wait_ge(o_read[i].sem, now.count(o_read[i], g - QUADS))
                                last = nc.tensor.matmul(f, wout[:, 2 * g + i, :], ot[:, 2 * g + i, :], start=g + i == 0, stop=g + i == QUADS)
                            if g == QUADS - 1:
                                last.then_inc(wo_ready.sem, 1)

                        def hidden(kind, first, ready):
                            for j in range(3):
                                m = FFC[j]
                                bank_free(kind, -1, j)
                                nc.tensor.matmul(bank(kind, -1, j)[0:m], w1[:, first + 128 * j:first + 128 * j + m], fq[:, :],
                                                 start=True, stop=True).then_inc(ready.sem, 1)

                        if cur:
                            if not prev:
                                pe.wait_ge(split_first, 2)
                            pe.wait_ge(x_hi.sem, now.count(x_hi, -1))
                            pe.wait_ge(x_lo.sem, now.count(x_lo, -1))
                            project(0, -1 if prev else None)
                        else:
                            mask_scores(-1)
                        if prev:
                            scores(-1)
                        if cur:
                            if not prev:
                                pe.wait_ge(consts, N_CONST)
                                pe.wait_ge(masked, N_MASKED)
                            norms(0)
                        if prev:
                            project_out(0)
                            project_out(1)
                            values(-2)
                        if cur:
                            project(1, 0)
                            scores(0)
                            project_v(0)
                            norms(1)
                        if prev:
                            project_out(2)
                            values(-1)
                        if cur:
                            project(2, 1)
                        if prev:
                            project_out(3)
                        if cur:
                            scores(1)
                        if prev:
                            pe.wait_ge(fs_done.sem, now.count(fs_done, -1))
                            nc.tensor.matmul(f, mean_w[:, :], fs[:, :], start=True, stop=True).then_inc(F["mean"].sem, 1)
                        if cur:
                            project_v(1)
                            norms(2)
                        if prev:
                            pe.wait_ge(F["sq"].sem, now.count(F["sq"], -1))
                            nc.tensor.matmul(f, mean_w[:, :], fq[:, :], start=True, stop=True).then_inc(F["var"].sem, 1)
                        if cur:
                            values(0)
                        if cur:
                            project(3, 2)
                        if prev:
                            pe.wait_ge(w_ff.sem, before.count(w_ff))
                            pe.wait_ge(F["xa"].sem, now.count(F["xa"], -1))
                            hidden("gate", FF, gate_ready)
                        if cur:
                            scores(2)
                            norms(3)
                        if prev:
                            hidden("val", 0, val_ready)
                        if cur:
                            values(1)
                        if prev:
                            pe.wait_ge(val_done.sem, now.count(val_done, 2 - 3))
                            for j in range(3):
                                m = FFC[j]
                                last = nc.tensor.matmul(f, w2[0:m, j, :], hid[0:m, j, :], start=j == 0, stop=j == 2)
                            last.then_inc(F["w2"].sem, 1)
                        else:
                            pe.wait_ge(qk_read.sem, now.count(qk_read, 4 * QUADS - 1))

                    steps_of(pe, step)

                @block.scalar
                def _(act):
                    def step(s, prev, cur):
                        now = Steps(act, s + 1, ACT_USES)

                        def evacuate(g):
                            act.wait_ge(rope_q.sem, now.count(rope_q, g - 1))
                            act.wait_ge(rope_k.sem, now.count(rope_k, g - 1))
                            act.wait_ge(s_ready.sem, now.count(s_ready, g - 2))
                            for i in range(4):
                                act.wait_ge(qk_ready.sem, now.count(qk_ready, 4 * g + i))
                                nc.scalar.activation(u[:, i, :], bank("qk", g, i), ACT.Square).then_inc(sq_done.sem, 1)
                                nc.scalar.activation(ab[:, g % 2, i, :], bank("qk", g, i), ACT.Identity, scale=pa[:, g, i:i + 1]).then_inc(qk_read.sem, 1)
                            act.wait_ge(n_ready.sem, now.count(n_ready, g - 1))
                            for i in range(2):
                                act.wait_ge(sq_sum[i].sem, now.count(sq_sum[i], g))
                                nc.scalar.activation(sq[:, 2 * i + 1, :], u[:, 2 * i + 1, :], ACT.Copy).then_inc(sq_hi[i].sem, 1)

                        def evacuate_v(i, tiles):
                            act.wait_ge(o_ready[1].sem, now.count(o_ready[1], 2 * i + 1 - QUADS))
                            for tile in tiles:
                                act.wait_ge(v_ready.sem, now.count(v_ready, TILES * i + tile))
                                nc.scalar.activation(v[:, tile, 512 * i:512 * i + 512], bank("v", i, tile), ACT.Copy).then_inc(v_read.sem, 1)

                        def inverse_norms(g):
                            act.wait_ge(rope_q.sem, now.count(rope_q, g - 1))
                            act.wait_ge(rope_k.sem, now.count(rope_k, g - 1))
                            act.wait_ge(n_ready.sem, now.count(n_ready, g))
                            for i in range(2):
                                nc.scalar.activation(rn[:, i, :], ps[:, NO[i], :], ACT.Ln, scale=2.0 ** PRE).then_inc(n_log.sem, 1)
                            act.wait_ge(n_log.sem, now.count(n_log, 2 * g + 1))
                            nc.scalar.activation(rn[:, :, :], rn[:, :, :], ACT.Exp, scale=-0.5).then_inc(n_inv.sem, 1)

                        def exponentials(g):
                            act.wait_ge(s_sub.sem, now.count(s_sub, g))
                            nc.scalar.activation(p[:, :], p[:, :], ACT.Exp).then_inc(p_exp.sem, 1)

                        def evacuate_out(g, pairs=(0, 1)):
                            for pair in pairs:
                                act.wait_ge(o_ready[pair].sem, now.count(o_ready[pair], g))
                                nc.scalar.activation(ot[:, 2 * (g % QUADS) + pair, :], ps[:, NO[pair], :], ACT.Copy).then_inc(o_read[pair].sem, 1)

                        if cur:
                            evacuate(0)
                            inverse_norms(0)
                        if prev:
                            evacuate_out(-2, (0,))
                            exponentials(-1)
                            evacuate_out(-2, (1,))
                        if cur:
                            evacuate(1)
                            evacuate_v(0, range(TILES))
                            inverse_norms(1)
                            exponentials(0)
                        if prev:
                            evacuate_out(-1)
                        if cur:
                            evacuate(2)
                        if prev:
                            act.wait_ge(F["x1"].sem, now.count(F["x1"], -1))
                            nc.scalar.activation(fs[0:64, :], x1[0:64, :], ACT.Copy).then_inc(fs_done.sem, 1)
                            nc.scalar.activation(fs[64:128, 1:N], x1[64:128, 0:N - 1], ACT.Copy).then_inc(fs_done.sem, 1)
                        if cur:
                            evacuate_v(1, range(2))
                        if prev:
                            act.wait_ge(F["xc"].sem, now.count(F["xc"], -1))
                            nc.scalar.activation(fq[:, :], fc[:, :], ACT.Square).then_inc(F["sq"].sem, 1)
                        if cur:
                            evacuate_v(1, range(2, TILES))
                            inverse_norms(2)
                            exponentials(1)
                        if prev:
                            act.wait_ge(F["var"].sem, now.count(F["var"], -1))
                            nc.scalar.activation(fq[:, :], ps[:, FB, :], ACT.Ln, bias=EPS).then_inc(F["lnv"].sem, 1)
                            act.wait_ge(F["lnv"].sem, now.count(F["lnv"], -1))
                            nc.scalar.activation(fq[:, :], fq[:, :], ACT.Exp, scale=-0.5).then_inc(F["rstd"].sem, 1)
                        if cur:
                            evacuate_out(0, (0,))
                        if prev:
                            act.wait_ge(F["xn"].sem, now.count(F["xn"], -1))
                            nc.scalar.activation(fq[:, :], fc[:, :], ACT.Identity, bias=pf[:, 1:2], scale=pf[:, 0:1]).then_inc(F["xa"].sem, 1)
                        if cur:
                            evacuate(3)
                        if prev:
                            for j in range(3):
                                m = FFC[j]
                                act.wait_ge(gate_ready.sem, now.count(gate_ready, j - 3))
                                nc.scalar.activation(hid[0:m, j, :], bank("gate", -1, j)[0:m], ACT.Gelu, bias=pf[0:m, 3 + j:4 + j]).then_inc(gate_done.sem, 1)
                            act.preload_act_table_set("natural_log_exp_and_others")
                        if cur:
                            inverse_norms(3)
                            exponentials(2)
                            act.wait_ge(xs_done.sem, now.count(xs_done))
                            nc.scalar.activation(xh[:, :], xs[:, :], ACT.Copy).then_inc(x_hi.sem, 1)
                            evacuate_out(1)

                    act.preload_act_table_set("natural_log_exp_and_others")
                    act.wait_ge(edges, 2)
                    act.wait_ge(xs_first, 32)
                    nc.scalar.activation(xh[:, :], xs[:, :], ACT.Copy).then_inc(split_first, 1)
                    steps_of(act, step)

                @block.gpsimd
                def _(pool):
                    def step(s, prev, cur):
                        now = Steps(pool, s + 1, POOL_USES)
                        for k in range(QUADS if cur else 0):
                            for i in range(2):
                                pool.wait_ge(sq_done.sem, now.count(sq_done, 4 * k + 2 * i + 1))
                                nc.gpsimd.tensor_tensor(u[:, 2 * i + 1, :], u[:, 2 * i, :], u[:, 2 * i + 1, :], ALU.add).then_inc(sq_sum[i].sem, 1)
                            pool.wait_ge(u_done.sem, now.count(u_done, k))
                            nc.gpsimd.tensor_tensor(u[:, 0:2, :], u[:, 0:2, :], ab[:, k % 2, 0:2, :], ALU.add).then_inc(q_sum.sem, 1)
                            pool.wait_ge(q_sum.sem, now.count(q_sum, k))
                            pool.wait_ge(gain.sem, now.count(gain, k))
                            nc.gpsimd.tensor_tensor(ab[:, k % 2, 0:2, :], u[:, 0:2, :], rn[:, 0:1, :].broadcast_to([128, 2, N]), ALU.mult).then_inc(rope_q.sem, 1)

                    nc.gpsimd.memset(kb[:, :, :, :], 0.0).then_inc(zeroed, 1)
                    nc.gpsimd.memset(vs[0:WIN, 0, :], 0.0).then_inc(zeroed, 1)
                    steps_of(pool, step)

                @block.vector
                def _(dve):
                    def step(s, prev, cur):
                        now = Steps(dve, s + 1, DVE_USES)
                        cols = slice(N * ((s - 1) % B), N * ((s - 1) % B) + N) if not (prev and cur) else bass.ds(((s - 1) & (B - 1)) * N, N)
                        f, prow = ps[:, FB, :], p[:, :].rearrange("p (n k) -> p n k", k=64)
                        def probabilities(g):
                            dve.wait_ge(p_exp.sem, now.count(p_exp, g))
                            nc.vector.tensor_reduce(rs[:, :], prow, AX.X, ALU.add).then_inc(p_sum.sem, 1)
                            dve.wait_ge(p_sum.sem, now.count(p_sum, g))
                            nc.vector.reciprocal(rs[:, :], rs[:, :]).then_inc(p_inv.sem, 1)
                            dve.wait_ge(p_inv.sem, now.count(p_inv, g))
                            nc.vector.tensor_tensor(prow, prow, rs[:, :].unsqueeze(2).broadcast_to([128, 16, 64]), ALU.mult).then_inc(p_norm.sem, 1)
                            dve.wait_ge(p_norm.sem, now.count(p_norm, g))
                            dve.wait_ge(t_dma.sem, now.count(t_dma, g - 1))
                            nc.vector.transpose(pt[:, :], p[:, :]).then_inc(p_tr.sem, 1)

                        def normalise_keys(k):
                            dve.wait_ge(n_inv.sem, now.count(n_inv, k))
                            nc.vector.scalar_tensor_tensor(out=rn[:, :, :], in0=rn[:, :, :], scalar=NORM_FLOOR_INV / 2 ** (PRE // 2), in1=cos2[:, :, :],
                                                           op0=ALU.min, op1=ALU.mult).then_inc(gain.sem, 1)
                            dve.wait_ge(gain.sem, now.count(gain, k))
                            dve.wait_ge(k_sum.sem, now.count(k_sum, k))
                            nc.vector.tensor_tensor(ab[:, k % 2, 2:4, :], u[:, 2:4, :], rn[:, 1:2, :].broadcast_to([128, 2, N]), ALU.mult).then_inc(rope_k.sem, 1)

                        def less_maximum(g):
                            srow = ps[:, 5:7, :].rearrange("p a (n k) -> p (a n) k", k=64)
                            dve.wait_ge(s_ready.sem, now.count(s_ready, g))
                            nc.vector.tensor_reduce(mx[:, :], srow, AX.X, ALU.max).then_inc(s_max.sem, 1)
                            dve.wait_ge(s_max.sem, now.count(s_max, g))
                            dve.wait_ge(p_tr.sem, now.count(p_tr, g - 1))
                            nc.vector.tensor_tensor(prow, srow, mx[:, :].unsqueeze(2).broadcast_to([128, 16, 64]), ALU.subtract).then_inc(s_sub.sem, 1)

                        for k in range(QUADS):
                            if k == 3 and cur:
                                dve.wait_ge(o_ready[1].sem, now.count(o_ready[1], 0))
                                nc.vector.tensor_copy(ot[:, 1, :], ps[:, NO[1], :]).then_inc(o_read[1].sem, 1)
                            if k and (cur if k >= 2 else prev):
                                probabilities(k - 2)
                            if k == 2 and prev:
                                dve.wait_ge(wo_ready.sem, now.count(wo_ready, -1))
                                nc.vector.tensor_tensor(x1[:, :], zT[:, cols], f, ALU.add).then_inc(F["x1"].sem, 1)
                            if cur:
                                dve.wait_ge(qk_read.sem, now.count(qk_read, 4 * k + 3))
                                dve.wait_ge(rope_q.sem, now.count(rope_q, k - 1))
                                dve.wait_ge(rope_k.sem, now.count(rope_k, k - 1))
                                for i in range(2):
                                    dve.wait_ge(sq_hi[i].sem, now.count(sq_hi[i], k))
                                    nc.vector.tensor_tensor(sq[:, 2 * i, :], u[:, 2 * i + 1, :], sq[:, 2 * i + 1, :].bitcast(F32), ALU.subtract).then_inc(sq_lo[i].sem, 1)
                                dve.wait_ge(sq_sum[1].sem, now.count(sq_sum[1], k))
                                for a in range(2):
                                    if a:
                                        for i in range(2):
                                            dve.wait_ge(sq_lo[i].sem, now.count(sq_lo[i], k))
                                    nc.vector.tensor_tensor(u[:, a:4:2, :], ab[:, k % 2, 1 - a:4:2, :], tan2[:, a:a + 1, :].broadcast_to([128, 2, N]),
                                                            ALU.mult).then_inc(u_done.sem, 1)
                                dve.wait_ge(u_done.sem, now.count(u_done, k))
                                nc.vector.tensor_tensor(u[:, 2:4, :], u[:, 2:4, :], ab[:, k % 2, 2:4, :], ALU.add).then_inc(k_sum.sem, 1)
                            if k == 2 and prev:
                                dve.wait_ge(F["mean"].sem, now.count(F["mean"], -1))
                                nc.vector.tensor_tensor(fc[:, :], fs[:, :], f, ALU.subtract).then_inc(F["xc"].sem, 1)
                            if cur and k == 0:
                                normalise_keys(k)
                            if cur if k else prev:
                                less_maximum(k - 1)
                            if cur and k:
                                normalise_keys(k)
                            if k == 3 and prev:
                                for j in range(3):
                                    m = FFC[j]
                                    dve.wait_ge(gate_done.sem, now.count(gate_done, j - 3))
                                    dve.wait_ge(val_ready.sem, now.count(val_ready, j - 3))
                                    nc.vector.scalar_tensor_tensor(out=hid[0:m, j, :], in0=bank("val", -1, j)[0:m], scalar=pf[0:m, 6 + j:7 + j],
                                                                   in1=hid[0:m, j, :], op0=ALU.add, op1=ALU.mult).then_inc(val_done.sem, 1)
                            if k == 2 and prev:
                                dve.wait_ge(F["rstd"].sem, now.count(F["rstd"], -1))
                                nc.vector.tensor_tensor(fc[:, :], fc[:, :], fq[:, :], ALU.mult).then_inc(F["xn"].sem, 1)
                            if k == 3 and cur:
                                dve.wait_ge(x_hi.sem, now.count(x_hi))
                                nc.vector.tensor_tensor(xl, xs[:, :], xh[:, :].bitcast(F32), ALU.subtract).then_inc(x_lo.sem, 1)
                        if cur:
                            probabilities(2)
                        if prev:
                            dve.wait_ge(F["w2"].sem, now.count(F["w2"], -1))
                            nc.vector.scalar_tensor_tensor(out=zT[:, cols], in0=f, scalar=pf[:, 2:3], in1=x1[:, :], op0=ALU.add, op1=ALU.add).then_inc(x2.sem, 1)

                    nc.vector.memset(xs[64:128, 0:1], 0.0).then_inc(edges, 1)
                    nc.vector.memset(fs[64:128, 0:1], 0.0).then_inc(edges, 1)
                    nc.vector.memset(tb[:, :, :], 0.0).then_inc(zeroed, 1)
                    dve.wait_ge(split_first, 1)
                    nc.vector.tensor_tensor(xl, xs[:, :], xh[:, :].bitcast(F32), ALU.subtract).then_inc(split_first, 1)
                    dve.wait_ge(consts, N_CONST)
                    nc.vector.tensor_copy(mask[:, :].rearrange("p (a n) -> p a n", a=2), hid[:, 0:2, 0:384]).then_inc(masked, 1)
                    nc.vector.tensor_copy(identb[:, :], fc[:, 0:128]).then_inc(masked, 1)
                    nc.vector.tensor_copy(ones[:, :], fc[:, 128:256]).then_inc(masked, 1)
                    steps_of(dve, step)

        def stage_b():
            scope = ExitStack()
            with scope:
                def t(name, shape):
                    return sb("b_" + name, shape, scope=scope)

                wq, wk, wv = (t(n, [C, C]) for n in ("wq", "wk", "wv"))
                wqr, wkr = t("wqr", [C, C]), t("wkr", [C, C])
                qcos, qsin, kcos, ksin, decay = (t(n, [128, N]) for n in ("qcos", "qsin", "kcos", "ksin", "decay"))
                xc, sq, xn = (t(n, [C, N]) for n in ("xc", "sq", "xn"))
                xb, xc2, sq2 = (t(n, [C, N]) for n in ("xb", "xc2", "sq2"))
                rope, qk = t("rope", [C, 4, N]), t("qk", [C, 2, N])
                v, st = t("v", [128, N]), t("st", [128, TILES, N])
                S = {n: Signal("b_" + n) for n in ("x", "mean", "xc", "sq", "var", "lnv", "rstd", "xn", "proj", "v_sb", "scores", "ret",
                                                   "x2", "mean2", "xc2", "sq2", "var2", "rstd2", "z")}
                S.update(rope4=Signal("b_rope4", 4), qk=Signal("b_qk", 2), st=Signal("b_st", TILES), lnv2=Signal("b_lnv2", ahead=2))
                consts, turned = sem("b_consts", scope), sem("b_turned", scope)
                PE_USES = DVE_USES = ACT_USES = [(1, -1), (1, 0), (1, 1), (2, -2), (2, 0), (4, -4), (4, 0)]
                SBANK = [(4, 0), (5, 0), (6, 0), (5, 384)]
                block = scope.enter_context(nc.Block())

                def steps_of(eng, step):
                    step(0, False, True)
                    with eng.Fori(1, B) as s:
                        step(s, True, True)
                    step(B, True, False)

                def scores_of(i):
                    bank, col = SBANK[i]
                    return ps[:, bank, col:col + N - 128 * i]

                @block.sync
                def _(sp):
                    sp.sem_inc(S["lnv2"].sem, S["lnv2"].ahead)
                    for dst, src in ((wq, wb["wq"]), (wk, wb["wk"]), (wv, wb["wv"]), (qcos, tabs["ret_qcos"]), (qsin, tabs["ret_qsin"]),
                                     (kcos, tabs["ret_kcos"]), (ksin, tabs["ret_ksin"]), (decay, tabs["ret_decay"])):
                        sp.dma_start(dst[:, :], src).then_inc(consts, 16)

                @block.tensor
                def _(pe):
                    def step(s, prev, cur):
                        now = Steps(pe, s + 1, PE_USES)
                        cols = bass.ts(s, N) if prev else slice(0, N)
                        if cur:
                            pe.wait_ge(S["x"].sem, now.count(S["x"]))
                            if prev:
                                pe.wait_ge(S["v_sb"].sem, now.count(S["v_sb"], -1))
                            nc.tensor.matmul(ps[:, 0, :], mean_w[:, :], xT[:, cols], start=True, stop=True).then_inc(S["mean"].sem, 1)
                        if prev:
                            pe.wait_ge(S["lnv2"].sem, now.count(S["lnv2"], -2))
                            pe.wait_ge(S["qk"].sem, now.count(S["qk"], -1))
                            for i in range(TILES):
                                last = nc.tensor.matmul(scores_of(i), qk[:, 1, 128 * i:128 * i + 128], qk[:, 0, 128 * i:N], start=True, stop=True)
                            last.then_inc(S["scores"].sem, 1)
                        if cur:
                            pe.wait_ge(S["sq"].sem, now.count(S["sq"]))
                            nc.tensor.matmul(ps[:, 0, :], mean_w[:, :], sq[:, :], start=True, stop=True).then_inc(S["var"].sem, 1)
                        if prev:
                            pe.wait_ge(S["v_sb"].sem, now.count(S["v_sb"], -1))
                            pe.wait_ge(S["st"].sem, now.count(S["st"], -1))
                            for i in range(TILES):
                                last = nc.tensor.matmul(ps[:, 7, 128 * i:N], v[:, 128 * i:128 * i + 128], st[:, i, 128 * i:N],
                                                        start=i == 0, stop=i == TILES - 1, skip_group_check=True)
                            last.then_inc(S["ret"].sem, 1)
                        if cur:
                            pe.wait_ge(S["xn"].sem, now.count(S["xn"]))
                            for i in range(TILES):
                                nc.tensor.matmul(ps[:, 0, 128 * i:128 * i + 128], xn[:, 128 * i:128 * i + 128], wv[:, :], start=True, stop=True)
                            for i, w in enumerate((wq, wqr, wk)):
                                nc.tensor.matmul(ps[:, 1 + i, :], w[:, :], xn[:, :], start=True, stop=True)
                            last = nc.tensor.matmul(ps[:, 4, :], wkr[:, :], xn[:, :], start=True, stop=True)
                            last.then_inc(S["proj"].sem, 1)
                        if prev:
                            pe.wait_ge(S["x2"].sem, now.count(S["x2"], -1))
                            nc.tensor.matmul(ps[:, 5, :], mean_w[:, :], xb[:, :], start=True, stop=True).then_inc(S["mean2"].sem, 1)
                            pe.wait_ge(S["sq2"].sem, now.count(S["sq2"], -1))
                            nc.tensor.matmul(ps[:, 6, :], mean_w[:, :], sq2[:, :], start=True, stop=True).then_inc(S["var2"].sem, 1)

                    pe.wait_ge(turned, 4)
                    steps_of(pe, step)

                @block.scalar
                def _(act):
                    def step(s, prev, cur):
                        now = Steps(act, s + 1, ACT_USES)
                        if cur:
                            act.wait_ge(S["xc"].sem, now.count(S["xc"]))
                            nc.scalar.activation(sq[:, :], xc[:, :], ACT.Square).then_inc(S["sq"].sem, 1)
                            act.wait_ge(S["var"].sem, now.count(S["var"]))
                            nc.scalar.activation(sq[:, :], ps[:, 0, :], ACT.Ln, bias=EPS).then_inc(S["lnv"].sem, 1)
                            act.wait_ge(S["lnv"].sem, now.count(S["lnv"]))
                            nc.scalar.activation(sq[:, :], sq[:, :], ACT.Exp, scale=-0.5).then_inc(S["rstd"].sem, 1)
                        if prev:
                            act.wait_ge(S["xc2"].sem, now.count(S["xc2"], -1))
                            nc.scalar.activation(sq2[:, :], xc2[:, :], ACT.Square).then_inc(S["sq2"].sem, 1)
                        if cur:
                            act.wait_ge(S["proj"].sem, now.count(S["proj"]))
                            if prev:
                                act.wait_ge(S["ret"].sem, now.count(S["ret"], -1))
                            nc.scalar.activation(v[:, :], ps[:, 0, :], ACT.Copy).then_inc(S["v_sb"].sem, 1)
                        if prev:
                            act.wait_ge(S["var2"].sem, now.count(S["var2"], -1))
                            nc.scalar.activation(sq2[:, :], ps[:, 6, :], ACT.Ln, bias=EPS).then_inc(S["lnv2"].sem, 1)
                            act.wait_ge(S["lnv2"].sem, now.count(S["lnv2"], -1))
                            nc.scalar.activation(sq2[:, :], sq2[:, :], ACT.Exp, scale=-0.5).then_inc(S["rstd2"].sem, 1)

                    steps_of(act, step)

                @block.vector
                def _(dve):
                    def step(s, prev, cur):
                        now = Steps(dve, s + 1, DVE_USES)
                        col, before = (bass.ts(s, N), bass.ts(s - 1, N)) if prev and cur else (slice(0, N), slice(TOK - N, TOK))
                        if cur:
                            nc.vector.tensor_tensor(xT[:, col], xT[:, col], zT[:, col], ALU.add).then_inc(S["x"].sem, 1)
                            dve.wait_ge(S["x"].sem, now.count(S["x"]))
                            dve.wait_ge(S["mean"].sem, now.count(S["mean"]))
                            nc.vector.tensor_tensor(xc[:, :], xT[:, col], ps[:, 0, :], ALU.subtract).then_inc(S["xc"].sem, 1)
                        if prev:
                            dve.wait_ge(S["scores"].sem, now.count(S["scores"], -1))
                            for i in range(TILES):
                                nc.vector.tensor_tensor(st[:, i, 128 * i:N], scores_of(i), decay[:, 0:N - 128 * i], ALU.mult).then_inc(S["st"].sem, 1)
                        if cur:
                            dve.wait_ge(S["rstd"].sem, now.count(S["rstd"]))
                            nc.vector.tensor_tensor(xn[:, :], xc[:, :], sq[:, :], ALU.mult).then_inc(S["xn"].sem, 1)
                        if prev:
                            dve.wait_ge(S["ret"].sem, now.count(S["ret"], -1))
                            nc.vector.tensor_tensor(xb[:, :], xT[:, before], ps[:, 7, :], ALU.add).then_inc(S["x2"].sem, 1)
                            dve.wait_ge(S["mean2"].sem, now.count(S["mean2"], -1))
                            nc.vector.tensor_tensor(xc2[:, :], xb[:, :], ps[:, 5, :], ALU.subtract).then_inc(S["xc2"].sem, 1)
                            nc.vector.tensor_copy(xT[:, before], xb[:, :])
                        if cur:
                            dve.wait_ge(S["proj"].sem, now.count(S["proj"]))
                            for i, tab in enumerate((qcos, qsin, kcos, ksin)):
                                nc.vector.tensor_tensor(rope[:, i, :], ps[:, 1 + i, :], tab[:, :], ALU.mult).then_inc(S["rope4"].sem, 1)
                            dve.wait_ge(S["rope4"].sem, now.count(S["rope4"]))
                            for i in range(2):
                                nc.vector.tensor_tensor(qk[:, i, :], rope[:, 2 * i, :], rope[:, 2 * i + 1, :], ALU.add).then_inc(S["qk"].sem, 1)
                        if prev:
                            dve.wait_ge(S["rstd2"].sem, now.count(S["rstd2"], -1))
                            nc.vector.tensor_tensor(zT[:, before], xc2[:, :], sq2[:, :], ALU.mult).then_inc(S["z"].sem, 1)

                    dve.wait_ge(consts, 16 * 8)
                    for dst, src in ((wqr, wq), (wkr, wk)):
                        nc.vector.tensor_scalar_mul(dst[:, 0:C:2], src[:, 1:C:2], -1.0).then_inc(turned, 1)
                        nc.vector.tensor_copy(dst[:, 1:C:2], src[:, 0:C:2]).then_inc(turned, 1)
                    steps_of(dve, step)

        def finish():
            summed, stored = sem("summed"), sem("stored")
            with nc.Block() as block:
                @block.vector
                def _(dve):
                    for b in range(B):
                        cols = slice(N * b, N * b + N)
                        nc.vector.tensor_tensor(xT[:, cols], xT[:, cols], zT[:, cols], ALU.add).then_inc(summed, 1)

                @block.sync
                def _(sp):
                    for b in range(B):
                        cols = slice(N * b, N * b + N)
                        sp.wait_ge(summed, b + 1)
                        sp.dma_start(out[:, cols], xT[:, cols]).then_inc(stored, 16)
                    sp.wait_ge(stored, 16 * B)

        stage_a()
        stage_ffn(0)
        stage_b()
        stage_ffn(1)
        finish()


def constants():
    f = np.float32
    C = 128
    p = np.arange(128)
    t = {}
    t["mean_w"] = np.full((C, C), 1.0 / C, f)
    t["ident"] = np.eye(128, dtype=f)
    t["headmask"] = (p[:, None] // 16 == np.arange(8)[None, :]).astype(f)
    t["blockmask"] = (p[:, None] // 16 == p[None, :] // 16).astype(f)
    t["headsum"] = (p[:, None] // 32 == p[None, :] // 32).astype(f)
    n, dh, win = 512, 64, 32
    half = np.arange(0, dh, 2, dtype=f)
    inv_freq = f(1.0) / (10000.0 ** (half.astype(np.float64) / dh)).astype(f)
    freqs = (np.arange(n, dtype=f)[:, None] * inv_freq[None, :]).astype(f).astype(np.float64)
    base = ((half + f(0.4 * dh)) / f(1.4 * dh)).astype(f)
    power = ((np.arange(n, dtype=f) - f(n // 2)) / f(win // 2)).astype(f)
    scale = base.astype(np.float64)[None, :] ** power.astype(np.float64)[:, None]
    tan, cos = np.tan(freqs), np.cos(freqs)
    four = lambda a: np.tile(a.T, (4, 1))
    t["tan2"] = np.stack([four(-tan), four(tan)], 1).astype(f)
    t["cos2"] = (np.stack([four(8.0 * cos * scale), four(cos / scale)], 1) * 2.0 ** 12).astype(f)
    q, key = p % 32, np.arange(64)
    off = (key[None, :] < q[:, None]) | (key[None, :] > q[:, None] + 32)
    later = np.where(off, f(-1e30), f(0.0)).astype(f)
    first = np.where(off | ((p[:, None] < 32) & (key[None, :] < 32)), f(-1e30), f(0.0)).astype(f)
    t["mask"] = np.concatenate([np.tile(first, (1, 4)), np.tile(later, (1, 8))], 1)
    vec = (np.arange(0, C, 2, dtype=f) + f(0.4 * C)) / f(1.4 * C)
    freq = f(1.0) / (10000.0 ** (np.arange(C // 2, dtype=np.float64) / (C // 2))).astype(f)
    pos = np.arange(n, dtype=f)
    scale = np.repeat(vec.astype(np.float64)[:, None] ** (pos / f(512.0)).astype(np.float64)[None, :], 2, axis=0)
    angle = np.repeat((pos[None, :] * freq[:, None]).astype(f).astype(np.float64), 2, axis=0)
    t["ret_qcos"], t["ret_qsin"] = (np.cos(angle) * scale).astype(f), (np.sin(angle) * scale).astype(f)
    t["ret_kcos"], t["ret_ksin"] = (np.cos(angle) / scale).astype(f), (np.sin(angle) / scale).astype(f)
    gap = np.arange(n)[None, :] - p[:, None]
    t["ret_decay"] = np.where(gap >= 0, 0.96875 ** np.maximum(gap, 0), 0.0).astype(f)
    t["causal"] = (p[:, None] <= p[None, :]).astype(f)
    return t


def kernel(**inputs):
    import concourse.bacc as _bacc
    from concourse import mybir as _mybir
    from concourse.bass_utils import run_bass_kernel_spmd as _run

    nc = _bacc.Bacc("TRN2", target_bir_lowering=False, num_devices=1)
    arrays = {}

    def give(name, a):
        a = np.ascontiguousarray(a)
        arrays[name] = a
        return nc.dram_tensor(name, a.shape, _mybir.dt.from_np(a.dtype), kind="ExternalInput").ap()

    i = {k: np.asarray(v) for k, v in inputs.items()}
    x = give("x", i["L0_attn_a_hidden_states"].reshape(-1, 128).T)
    tabs = {k: give("t_" + k, v) for k, v in constants().items()}
    wqT, wkT, wvT = (i["L0_attn_a_" + n].T for n in ("Wq", "Wk", "Wv"))
    wa = {"wq": give("wq", wqT), "wk": give("wk", wkT), "wv_wk": give("wv_wk", np.concatenate([wvT, wkT], 1)),
          "wo": give("wo", i["L0_attn_a_Wo"].T), "nw": give("nw", np.tile(i["L0_attn_a_norm_w"], 8)[:, None])}
    wb = {n: give("ret_" + n, i["L0_attn_b_W_" + n[1].upper()]) for n in ("wq", "wk", "wv")}
    wf = {}
    w = i["L0_ffn_Wqkv"].reshape(6, 128, 3, 4, 4, 2, 32)
    qk = w[:, :, 0:2].transpose(0, 1, 3, 2, 5, 4, 6).reshape(6, 128, 4, 4, 128)
    wf["wqkv"] = give("wqkv", np.concatenate([qk, w[:, :, 2].reshape(6, 128, 4, 2, 128)], 3).transpose(0, 2, 1, 3, 4).reshape(24, 128, 768))
    qs, ks = (np.tile(i["L0_ffn_" + n].reshape(6, 1, 2, 32), (1, 4, 1, 1)).transpose(0, 1, 3, 2).reshape(6, 128, 2) for n in ("q_scale", "k_scale"))
    wf["pa"] = give("pa", np.concatenate([qs, ks], 2))
    wf["wout"] = give("wout", i["L0_ffn_Wo"])
    wf["w1"], wf["w2"] = give("w1", i["L0_ffn_W1"]), give("w2", i["L0_ffn_W2"])
    b1 = np.zeros((6, 2, 384), np.float32)
    b1[:, :, :341] = i["L0_ffn_b1"].reshape(6, 2, 341)
    b1 = b1.reshape(6, 2, 3, 128).transpose(0, 3, 1, 2)
    wf["pf"] = give("pf", np.concatenate([np.stack([i["L0_ffn_" + n] for n in ("ln_g", "ln_b", "b2")], 2), b1[:, :, 1], b1[:, :, 0]], 2))
    out = nc.dram_tensor("y", (128, 2048), _mybir.dt.float32, kind="ExternalOutput").ap()
    build_hybrid(nc, x, tabs, wa, wb, wf, out)
    r = _run(nc, [arrays], core_ids=[0])
    return r.results[0]["y"].T.reshape(4, 512, 128)
```
